# Optimizing a Trainium2 kernel written in Bass

```python
import numpy as np
import jax
import jax.numpy as jnp

def _softmax(x, axis=-1):
    return jax.nn.softmax(x, axis=axis)

def _gelu(x):
    return jax.nn.gelu(x, approximate=True)

def _silu(x):
    return jax.nn.silu(x)

def _sigmoid(x):
    return jax.nn.sigmoid(x)

def _layernorm(x, axis=-1, eps=1e-05):
    m = jnp.mean(x, axis=axis, keepdims=True)
    v = jnp.var(x, axis=axis, keepdims=True)
    return (x - m) / jnp.sqrt(v + eps)

def _scatter_add(tgt, idx, src, axis=0):
    return tgt.at[idx].add(src)

def _segment_sum(src, seg, n):
    return jax.ops.segment_sum(src, seg, n)
kernel_name = 'mk_decoder_postln_d2_seqx_r8_d598a5'

def setup_inputs(seed: int=0):
    np.random.seed(seed)
    _w = jnp.asarray

    def _rec_inputs():
        import jax
        import jax.numpy as jnp
        _rk = jax.random.key(seed)
        x = -0.0002928 + 1 * jax.random.normal(jax.random.fold_in(_rk, 1), (32, 128, 128), jnp.float32)
        _lenS = 128 - jax.random.randint(jax.random.fold_in(_rk, 7), (32,), 0, max(1, 128 // 4) + 1, jnp.int32)
        _lenS2 = 128 - jax.random.randint(jax.random.fold_in(_rk, 8), (32,), 0, max(1, 128 // 4) + 1, jnp.int32)
        _ctx_1024P = jax.random.normal(jax.random.fold_in(_rk, 11), (32, 16, 128), jnp.float32)
        _ctx_1024c = jax.random.dirichlet(jax.random.fold_in(_rk, 511), 0.3 * jnp.ones((16,), jnp.float32), (32, 128))
        _ctx_1024t = jnp.einsum('bsk,bkd->bsd', _ctx_1024c, _ctx_1024P)
        _ctx_1024t = _ctx_1024t * jax.lax.rsqrt(jnp.mean(jnp.square(_ctx_1024t)) + 1e-12) * 0.953939
        ctx_1024 = -1.39393e-06 + 0.999914 * (_ctx_1024t + 0.3 * jax.random.normal(jax.random.fold_in(_rk, 611), (32, 128, 128), jnp.float32))
        return (x, ctx_1024)
    x, ctx_1024 = _rec_inputs()

    def _L0_attn_setup():
        import jax, jax.numpy as jnp
        import numpy as np
        D_MODEL = 128
        H = 16
        LN_EPS = 1e-05

        def _layernorm(x, g, b):
            mu = jnp.mean(x, axis=-1, keepdims=True)
            var = jnp.mean(jnp.square(x - mu), axis=-1, keepdims=True)
            return (x - mu) * jax.lax.rsqrt(var + LN_EPS) * g + b

        def _attention(tokens, Wq, bq, Wk, bk, Wv, bv, Wo, bo, dist_scale):
            B, T, D = tokens.shape
            dh = D // H
            q = (tokens @ Wq + bq).reshape(B, T, H, dh)
            k = (tokens @ Wk + bk).reshape(B, T, H, dh)
            v = (tokens @ Wv + bv).reshape(B, T, H, dh)
            S = jnp.einsum('bthd,buhd->btuh', q, k)
            pos = jnp.arange(T)
            dist = jnp.abs(pos[None, :] - pos[:, None]).astype(S.dtype)
            S = S - dist_scale * dist[None, :, :, None]
            mask_uh = jnp.triu(jnp.ones((T, H), bool), k=1)
            S = jnp.where(mask_uh[None, None, :, :], -jnp.inf, S)
            S = S / jnp.sqrt(jnp.asarray(dh, S.dtype))
            P = jax.nn.softmax(S, axis=2)
            A = jnp.einsum('btuh,buhd->bthd', P, v).reshape(B, T, D)
            return A @ Wo + bo
        key = jax.random.key(seed)
        ks = jax.random.split(key, 16)
        B, T, D = (2, 256, D_MODEL)
        d_ff = 4 * D
        s = 1.0 / np.sqrt(D)
        sf = 1.0 / np.sqrt(d_ff)
        return {'tokens': jax.random.normal(ks[0], (B, T, D), jnp.float32), 'Wq': jax.random.normal(ks[1], (D, D), jnp.float32) * s, 'bq': jnp.zeros((D,), jnp.float32), 'Wk': jax.random.normal(ks[2], (D, D), jnp.float32) * s, 'bk': jnp.zeros((D,), jnp.float32), 'Wv': jax.random.normal(ks[3], (D, D), jnp.float32) * s, 'bv': jnp.zeros((D,), jnp.float32), 'Wo': jax.random.normal(ks[4], (D, D), jnp.float32) * s, 'bo': jnp.zeros((D,), jnp.float32), 'dist_scale': jnp.asarray(0.01, jnp.float32), 'W1': jax.random.normal(ks[5], (D, d_ff), jnp.float32) * s, 'b1': jnp.zeros((d_ff,), jnp.float32), 'W2': jax.random.normal(ks[6], (d_ff, D), jnp.float32) * sf, 'b2': jnp.zeros((D,), jnp.float32), 'ln1_g': jnp.ones((D,), jnp.float32), 'ln1_b': jnp.zeros((D,), jnp.float32), 'ln2_g': jnp.ones((D,), jnp.float32), 'ln2_b': jnp.zeros((D,), jnp.float32)}
    _L0_attn_all = _L0_attn_setup()
    _L0_attn_in = {k: v for k, v in _L0_attn_all.items() if k in ('Wq', 'bq', 'Wk', 'bk', 'Wv', 'bv', 'Wo', 'bo', 'dist_scale', 'W1', 'b1', 'W2', 'b2', 'ln1_g', 'ln1_b', 'ln2_g', 'ln2_b')}
    del _L0_attn_all

    def _L0_xattn_setup():
        import jax, jax.numpy as jnp
        import numpy as np
        D_MODEL = 128
        N_HEADS = 16
        D_HEAD = D_MODEL // N_HEADS
        WINDOW = 128

        def _heads(x):
            B, S, _ = x.shape
            return x.reshape(B, S, N_HEADS, D_HEAD).transpose(0, 2, 1, 3)
        key = jax.random.key(seed)
        ks = jax.random.split(key, 11)
        B, S = (1, 512)
        s = 1.0 / np.sqrt(D_MODEL)
        return {'query': jax.random.normal(ks[0], (B, S, D_MODEL), jnp.float32), 'key': jax.random.normal(ks[1], (B, S, D_MODEL), jnp.float32), 'value': jax.random.normal(ks[2], (B, S, D_MODEL), jnp.float32), 'Wq': jax.random.normal(ks[3], (D_MODEL, D_MODEL), jnp.float32) * s, 'bq': jnp.zeros((D_MODEL,), jnp.float32), 'Wk': jax.random.normal(ks[4], (D_MODEL, D_MODEL), jnp.float32) * s, 'bk': jnp.zeros((D_MODEL,), jnp.float32), 'Wv': jax.random.normal(ks[5], (D_MODEL, D_MODEL), jnp.float32) * s, 'bv': jnp.zeros((D_MODEL,), jnp.float32), 'Wo': jax.random.normal(ks[6], (D_MODEL, D_MODEL), jnp.float32) * s, 'bo': jnp.zeros((D_MODEL,), jnp.float32)}
    _L0_xattn_all = _L0_xattn_setup()
    _L0_xattn_in = {k: v for k, v in _L0_xattn_all.items() if k in ('Wq', 'bq', 'Wk', 'bk', 'Wv', 'bv', 'Wo', 'bo')}
    del _L0_xattn_all

    def _L0_ffn_setup():
        import jax, jax.numpy as jnp
        import numpy as np
        B, S, H, DFF, E, K = (2, 256, 128, 256, 8, 2)

        def _moe(x, Wg, W1, b1, W2, b2, W3, b3):
            Bm, Sm, Hm = x.shape
            xt = x.reshape(-1, Hm)
            gout = xt @ Wg.T
            topv, topi = jax.lax.top_k(gout, K)
            w = jax.nn.softmax(topv, axis=-1)
            comb = jnp.einsum('tke,tk->te', jax.nn.one_hot(topi, E, dtype=x.dtype), w)
            g = jnp.einsum('th,efh->etf', xt, W1) + b1[:, None, :]
            v = jnp.einsum('th,efh->etf', xt, W2) + b2[:, None, :]
            h = jax.nn.silu(g) * v
            eo = jnp.einsum('etf,ehf->eth', h, W3) + b3[:, None, :]
            out = jnp.einsum('eth,te->th', eo, comb)
            return out.reshape(Bm, Sm, Hm)
        key = jax.random.key(seed)
        ks = jax.random.split(key, 8)
        sc_h = 1.0 / np.sqrt(H)
        sc_f = 1.0 / np.sqrt(DFF)
        x = jax.random.normal(ks[0], (B, S, H), dtype=jnp.float32)
        Wg = jax.random.uniform(ks[1], (E, H), jnp.float32, -sc_h, sc_h)
        W1 = jax.random.uniform(ks[2], (E, DFF, H), jnp.float32, -sc_h, sc_h)
        b1 = jax.random.uniform(ks[3], (E, DFF), jnp.float32, -sc_h, sc_h)
        W2 = jax.random.uniform(ks[4], (E, DFF, H), jnp.float32, -sc_h, sc_h)
        b2 = jax.random.uniform(ks[5], (E, DFF), jnp.float32, -sc_h, sc_h)
        W3 = jax.random.uniform(ks[6], (E, H, DFF), jnp.float32, -sc_f, sc_f)
        b3 = jax.random.uniform(ks[7], (E, H), jnp.float32, -sc_f, sc_f)
        return {'x': x, 'Wg': Wg, 'W1': W1, 'b1': b1, 'W2': W2, 'b2': b2, 'W3': W3, 'b3': b3}
    _L0_ffn_all = _L0_ffn_setup()
    _L0_ffn_in = {k: v for k, v in _L0_ffn_all.items() if k in ('Wg', 'W1', 'b1', 'W2', 'b2', 'W3', 'b3')}
    del _L0_ffn_all

    def _L1_attn_setup():
        import jax, jax.numpy as jnp
        import numpy as np
        MAX_WAVELENGTH = 10000.0
        NEG_INF = -1000000000.0

        def apply_rope(x):
            S, D = (x.shape[1], x.shape[-1])
            inv_freq = 1.0 / MAX_WAVELENGTH ** (jnp.arange(0, D, 2, dtype=jnp.float32) / D)
            t = jnp.arange(S, dtype=jnp.float32)[:, None] * inv_freq[None, :]
            emb = jnp.concatenate([t, t], axis=-1)
            cos = jnp.cos(emb)[None, :, None, :].astype(x.dtype)
            sin = jnp.sin(emb)[None, :, None, :].astype(x.dtype)
            x1, x2 = jnp.split(x, 2, axis=-1)
            rotated = jnp.concatenate([-x2, x1], axis=-1)
            return x * cos + rotated * sin
        key = jax.random.key(seed)
        k1, k2, k3 = jax.random.split(key, 3)
        B, S, dim = (2, 256, 128)
        x = jax.random.normal(k1, (B, S, dim), dtype=jnp.float32)
        w_qkv = jax.random.normal(k2, (dim, 3 * dim), dtype=jnp.float32) * dim ** (-0.5)
        w_proj = jax.random.normal(k3, (dim, dim), dtype=jnp.float32) * dim ** (-0.5)
        b_proj = jnp.zeros((dim,), dtype=jnp.float32)
        return {'x': x, 'w_qkv': w_qkv, 'w_proj': w_proj, 'b_proj': b_proj}
    _L1_attn_all = _L1_attn_setup()
    _L1_attn_in = {k: v for k, v in _L1_attn_all.items() if k in ('w_qkv', 'w_proj', 'b_proj')}
    del _L1_attn_all

    def _L1_xattn_setup():
        import jax, jax.numpy as jnp
        import numpy as np
        from jax import lax
        NUM_HEADS = 16
        DIM = 128
        BATCH = 4
        SEQ = 256
        key = jax.random.key(seed)
        ks = jax.random.split(key, 12)
        f32 = jnp.float32
        q = jax.random.normal(ks[0], (BATCH, SEQ, DIM), dtype=f32)
        k = jax.random.normal(ks[1], (BATCH, SEQ, DIM), dtype=f32)
        v = jax.random.normal(ks[2], (BATCH, SEQ, DIM), dtype=f32)
        lim = 1.0 / np.sqrt(DIM)
        Wi = jax.random.uniform(ks[3], (DIM, DIM), minval=-lim, maxval=lim, dtype=f32)
        bi = jax.random.uniform(ks[4], (DIM,), minval=-lim, maxval=lim, dtype=f32)
        Wg = jax.random.uniform(ks[5], (DIM, DIM), minval=-lim, maxval=lim, dtype=f32)
        bg = jax.random.uniform(ks[6], (DIM,), minval=-lim, maxval=lim, dtype=f32)
        Wo = jax.random.uniform(ks[7], (DIM, DIM), minval=-lim, maxval=lim, dtype=f32)
        bo = jax.random.uniform(ks[8], (DIM,), minval=-lim, maxval=lim, dtype=f32)
        A = jax.random.normal(ks[9], (DIM, DIM), dtype=f32) * 0.1
        Bm = jax.random.normal(ks[10], (DIM, DIM), dtype=f32) * 0.1
        decay = jnp.full((1, NUM_HEADS, 1), 0.9, dtype=f32)
        return dict(q=q, k=k, v=v, Wi=Wi, bi=bi, Wg=Wg, bg=bg, A=A, Bm=Bm, Wo=Wo, bo=bo, decay=decay)
    _L1_xattn_all = _L1_xattn_setup()
    _L1_xattn_in = {k: v for k, v in _L1_xattn_all.items() if k in ('Wi', 'bi', 'Wg', 'bg', 'A', 'Bm', 'Wo', 'bo', 'decay')}
    del _L1_xattn_all

    def _L1_ffn_setup():
        import jax, jax.numpy as jnp
        import numpy as np
        B, S, D = (4, 256, 128)
        E, F = (8, 512)
        key = jax.random.key(seed)
        ks = jax.random.split(key, 5)
        x = jax.random.normal(ks[0], (B, S, D), dtype=jnp.float32)
        switch_w = jax.random.normal(ks[1], (D, E), dtype=jnp.float32) * D ** (-0.5)
        switch_b = jnp.zeros((E,), dtype=jnp.float32)
        w1 = jax.random.normal(ks[2], (E, D, F), dtype=jnp.float32) * D ** (-0.5)
        b1 = jnp.zeros((E, F), dtype=jnp.float32)
        w2 = jax.random.normal(ks[3], (E, F, D), dtype=jnp.float32) * F ** (-0.5)
        b2 = jnp.zeros((E, D), dtype=jnp.float32)
        return {'x': x, 'switch_w': switch_w, 'switch_b': switch_b, 'w1': w1, 'b1': b1, 'w2': w2, 'b2': b2}
    _L1_ffn_all = _L1_ffn_setup()
    _L1_ffn_in = {k: v for k, v in _L1_ffn_all.items() if k in ('switch_w', 'switch_b', 'w1', 'b1', 'w2', 'b2')}
    del _L1_ffn_all
    return {'x': x, 'ctx_1024': ctx_1024, 'L0_attn_Wq': _L0_attn_in['Wq'], 'L0_attn_bq': _L0_attn_in['bq'], 'L0_attn_Wk': _L0_attn_in['Wk'], 'L0_attn_bk': _L0_attn_in['bk'], 'L0_attn_Wv': _L0_attn_in['Wv'], 'L0_attn_bv': _L0_attn_in['bv'], 'L0_attn_Wo': _L0_attn_in['Wo'], 'L0_attn_bo': _L0_attn_in['bo'], 'L0_attn_dist_scale': _L0_attn_in['dist_scale'], 'L0_attn_W1': _L0_attn_in['W1'], 'L0_attn_b1': _L0_attn_in['b1'], 'L0_attn_W2': _L0_attn_in['W2'], 'L0_attn_b2': _L0_attn_in['b2'], 'L0_attn_ln1_g': _L0_attn_in['ln1_g'], 'L0_attn_ln1_b': _L0_attn_in['ln1_b'], 'L0_attn_ln2_g': _L0_attn_in['ln2_g'], 'L0_attn_ln2_b': _L0_attn_in['ln2_b'], 'L0_xattn_Wq': _L0_xattn_in['Wq'], 'L0_xattn_bq': _L0_xattn_in['bq'], 'L0_xattn_Wk': _L0_xattn_in['Wk'], 'L0_xattn_bk': _L0_xattn_in['bk'], 'L0_xattn_Wv': _L0_xattn_in['Wv'], 'L0_xattn_bv': _L0_xattn_in['bv'], 'L0_xattn_Wo': _L0_xattn_in['Wo'], 'L0_xattn_bo': _L0_xattn_in['bo'], 'L0_ffn_Wg': _L0_ffn_in['Wg'], 'L0_ffn_W1': _L0_ffn_in['W1'], 'L0_ffn_b1': _L0_ffn_in['b1'], 'L0_ffn_W2': _L0_ffn_in['W2'], 'L0_ffn_b2': _L0_ffn_in['b2'], 'L0_ffn_W3': _L0_ffn_in['W3'], 'L0_ffn_b3': _L0_ffn_in['b3'], 'L1_attn_w_qkv': _L1_attn_in['w_qkv'], 'L1_attn_w_proj': _L1_attn_in['w_proj'], 'L1_attn_b_proj': _L1_attn_in['b_proj'], 'L1_xattn_Wi': _L1_xattn_in['Wi'], 'L1_xattn_bi': _L1_xattn_in['bi'], 'L1_xattn_Wg': _L1_xattn_in['Wg'], 'L1_xattn_bg': _L1_xattn_in['bg'], 'L1_xattn_A': _L1_xattn_in['A'], 'L1_xattn_Bm': _L1_xattn_in['Bm'], 'L1_xattn_Wo': _L1_xattn_in['Wo'], 'L1_xattn_bo': _L1_xattn_in['bo'], 'L1_xattn_decay': _L1_xattn_in['decay'], 'L1_ffn_switch_w': _L1_ffn_in['switch_w'], 'L1_ffn_switch_b': _L1_ffn_in['switch_b'], 'L1_ffn_w1': _L1_ffn_in['w1'], 'L1_ffn_b1': _L1_ffn_in['b1'], 'L1_ffn_w2': _L1_ffn_in['w2'], 'L1_ffn_b2': _L1_ffn_in['b2']}

def reference(x, ctx_1024, L0_attn_Wq, L0_attn_bq, L0_attn_Wk, L0_attn_bk, L0_attn_Wv, L0_attn_bv, L0_attn_Wo, L0_attn_bo, L0_attn_dist_scale, L0_attn_W1, L0_attn_b1, L0_attn_W2, L0_attn_b2, L0_attn_ln1_g, L0_attn_ln1_b, L0_attn_ln2_g, L0_attn_ln2_b, L0_xattn_Wq, L0_xattn_bq, L0_xattn_Wk, L0_xattn_bk, L0_xattn_Wv, L0_xattn_bv, L0_xattn_Wo, L0_xattn_bo, L0_ffn_Wg, L0_ffn_W1, L0_ffn_b1, L0_ffn_W2, L0_ffn_b2, L0_ffn_W3, L0_ffn_b3, L1_attn_w_qkv, L1_attn_w_proj, L1_attn_b_proj, L1_xattn_Wi, L1_xattn_bi, L1_xattn_Wg, L1_xattn_bg, L1_xattn_A, L1_xattn_Bm, L1_xattn_Wo, L1_xattn_bo, L1_xattn_decay, L1_ffn_switch_w, L1_ffn_switch_b, L1_ffn_w1, L1_ffn_b1, L1_ffn_w2, L1_ffn_b2):
    import jax
    import jax.numpy as jnp

    def _L0_attn_ref(tokens, Wq, bq, Wk, bk, Wv, bv, Wo, bo, dist_scale, W1, b1, W2, b2, ln1_g, ln1_b, ln2_g, ln2_b):
        import jax, jax.numpy as jnp
        import numpy as np
        D_MODEL = 128
        H = 16
        LN_EPS = 1e-05

        def _layernorm(x, g, b):
            mu = jnp.mean(x, axis=-1, keepdims=True)
            var = jnp.mean(jnp.square(x - mu), axis=-1, keepdims=True)
            return (x - mu) * jax.lax.rsqrt(var + LN_EPS) * g + b

        def _attention(tokens, Wq, bq, Wk, bk, Wv, bv, Wo, bo, dist_scale):
            B, T, D = tokens.shape
            dh = D // H
            q = (tokens @ Wq + bq).reshape(B, T, H, dh)
            k = (tokens @ Wk + bk).reshape(B, T, H, dh)
            v = (tokens @ Wv + bv).reshape(B, T, H, dh)
            S = jnp.einsum('bthd,buhd->btuh', q, k)
            pos = jnp.arange(T)
            dist = jnp.abs(pos[None, :] - pos[:, None]).astype(S.dtype)
            S = S - dist_scale * dist[None, :, :, None]
            mask_uh = jnp.triu(jnp.ones((T, H), bool), k=1)
            S = jnp.where(mask_uh[None, None, :, :], -jnp.inf, S)
            S = S / jnp.sqrt(jnp.asarray(dh, S.dtype))
            P = jax.nn.softmax(S, axis=2)
            A = jnp.einsum('btuh,buhd->bthd', P, v).reshape(B, T, D)
            return A @ Wo + bo
        x_attn = _attention(tokens, Wq, bq, Wk, bk, Wv, bv, Wo, bo, dist_scale)
        x = _layernorm(tokens + x_attn, ln1_g, ln1_b)
        y = jax.nn.relu(x @ W1 + b1) @ W2 + b2
        z = _layernorm(y + x, ln2_g, ln2_b)
        return z

    def _L0_xattn_ref(query, key, value, Wq, bq, Wk, bk, Wv, bv, Wo, bo):
        import jax, jax.numpy as jnp
        import numpy as np
        D_MODEL = 128
        N_HEADS = 16
        D_HEAD = D_MODEL // N_HEADS
        WINDOW = 128

        def _heads(x):
            B, S, _ = x.shape
            return x.reshape(B, S, N_HEADS, D_HEAD).transpose(0, 2, 1, 3)
        B, S, _ = query.shape
        q = _heads(query @ Wq.T + bq)
        k = _heads(key @ Wk.T + bk)
        v = _heads(value @ Wv.T + bv)
        scores = jnp.einsum('bhqd,bhkd->bhqk', q, k) / np.sqrt(D_HEAD).astype(np.float32)
        idx = jnp.arange(S)
        local = jnp.abs(idx[:, None] - idx[None, :]) <= WINDOW // 2
        scores = jnp.where(local[None, None, :, :], scores, -jnp.inf)
        attn = jax.nn.softmax(scores, axis=-1)
        ctx = jnp.einsum('bhqk,bhkd->bhqd', attn, v)
        ctx = ctx.transpose(0, 2, 1, 3).reshape(B, S, D_MODEL)
        return ctx @ Wo.T + bo

    def _L0_ffn_ref(x, Wg, W1, b1, W2, b2, W3, b3):
        import jax, jax.numpy as jnp
        import numpy as np
        B, S, H, DFF, E, K = (2, 256, 128, 256, 8, 2)

        def _moe(x, Wg, W1, b1, W2, b2, W3, b3):
            Bm, Sm, Hm = x.shape
            xt = x.reshape(-1, Hm)
            gout = xt @ Wg.T
            topv, topi = jax.lax.top_k(gout, K)
            w = jax.nn.softmax(topv, axis=-1)
            comb = jnp.einsum('tke,tk->te', jax.nn.one_hot(topi, E, dtype=x.dtype), w)
            g = jnp.einsum('th,efh->etf', xt, W1) + b1[:, None, :]
            v = jnp.einsum('th,efh->etf', xt, W2) + b2[:, None, :]
            h = jax.nn.silu(g) * v
            eo = jnp.einsum('etf,ehf->eth', h, W3) + b3[:, None, :]
            out = jnp.einsum('eth,te->th', eo, comb)
            return out.reshape(Bm, Sm, Hm)
        return _moe(x, Wg, W1, b1, W2, b2, W3, b3)

    def _L1_attn_ref(x, w_qkv, w_proj, b_proj):
        import jax, jax.numpy as jnp
        import numpy as np
        MAX_WAVELENGTH = 10000.0
        NEG_INF = -1000000000.0

        def apply_rope(x):
            S, D = (x.shape[1], x.shape[-1])
            inv_freq = 1.0 / MAX_WAVELENGTH ** (jnp.arange(0, D, 2, dtype=jnp.float32) / D)
            t = jnp.arange(S, dtype=jnp.float32)[:, None] * inv_freq[None, :]
            emb = jnp.concatenate([t, t], axis=-1)
            cos = jnp.cos(emb)[None, :, None, :].astype(x.dtype)
            sin = jnp.sin(emb)[None, :, None, :].astype(x.dtype)
            x1, x2 = jnp.split(x, 2, axis=-1)
            rotated = jnp.concatenate([-x2, x1], axis=-1)
            return x * cos + rotated * sin
        B, S, dim = x.shape
        heads = 16
        head_dim = dim // heads
        scale = head_dim ** (-0.5)
        qkv = x @ w_qkv
        qkv = qkv.reshape(B, S, 3, heads, head_dim)
        Q, K, V = (qkv[:, :, 0], qkv[:, :, 1], qkv[:, :, 2])
        Q = apply_rope(Q)
        K = apply_rope(K)
        attn = jnp.einsum('bqhd,bkhd->bhqk', Q, K) * scale
        causal = jnp.tril(jnp.ones((S, S), dtype=bool))[None, None]
        attn = jnp.where(causal, attn, jnp.asarray(NEG_INF, attn.dtype))
        attn = jax.nn.softmax(attn, axis=-1)
        out = jnp.einsum('bhqk,bkhd->bqhd', attn, V).reshape(B, S, dim)
        return out @ w_proj + b_proj

    def _L1_xattn_ref(q, k, v, Wi, bi, Wg, bg, A, Bm, Wo, bo, decay):
        import jax, jax.numpy as jnp
        import numpy as np
        from jax import lax
        NUM_HEADS = 16
        DIM = 128
        BATCH = 4
        SEQ = 256
        B, S, D = q.shape
        H = decay.shape[1]
        hd = D // H
        qh = jnp.moveaxis(q.reshape(B, S, H, hd), 1, 0)
        kh = jnp.moveaxis(k.reshape(B, S, H, hd), 1, 0)
        vh = jnp.moveaxis(v.reshape(B, S, H, hd), 1, 0)

        def step(carry, xs):
            r, state = carry
            qt, kt, vt = xs
            r = decay * r + kt * vt
            retained = (qt * r).reshape(B, D)
            inp = retained @ Wi.T + bi
            gate = jax.nn.sigmoid(inp @ Wg.T + bg)
            blended = gate * state + (1.0 - gate) * inp
            state = jnp.tanh(blended @ A.T + inp @ Bm.T)
            out = state @ Wo.T + bo
            return ((r, state), out)
        r0 = jnp.zeros((B, H, hd), dtype=q.dtype)
        s0 = jnp.zeros((B, D), dtype=q.dtype)
        _, outs = lax.scan(step, (r0, s0), (qh, kh, vh))
        return jnp.moveaxis(outs, 0, 1)

    def _L1_ffn_ref(x, switch_w, switch_b, w1, b1, w2, b2):
        import jax, jax.numpy as jnp
        import numpy as np
        B, S, D = (4, 256, 128)
        E, F = (8, 512)
        b, s, d = x.shape
        t = x.reshape(-1, d)
        logits = t @ switch_w + switch_b
        route_prob = jax.nn.softmax(logits, axis=-1)
        route_prob_max = jnp.max(route_prob, axis=-1)
        routes = jnp.argmax(route_prob, axis=-1)
        out = jnp.zeros_like(t)
        n_experts = w1.shape[0]
        for e in range(n_experts):
            h = jax.nn.gelu(t @ w1[e] + b1[e])
            y = h @ w2[e] + b2[e]
            mask = (routes == e)[:, None]
            out = jnp.where(mask, y, out)
        out = out * route_prob_max[:, None]
        return out.reshape(b, s, d)
    x = _layernorm(x + _L0_attn_ref(x, L0_attn_Wq, L0_attn_bq, L0_attn_Wk, L0_attn_bk, L0_attn_Wv, L0_attn_bv, L0_attn_Wo, L0_attn_bo, L0_attn_dist_scale, L0_attn_W1, L0_attn_b1, L0_attn_W2, L0_attn_b2, L0_attn_ln1_g, L0_attn_ln1_b, L0_attn_ln2_g, L0_attn_ln2_b), axis=-1)
    x = _layernorm(x + _L0_xattn_ref(x, ctx_1024, ctx_1024, L0_xattn_Wq, L0_xattn_bq, L0_xattn_Wk, L0_xattn_bk, L0_xattn_Wv, L0_xattn_bv, L0_xattn_Wo, L0_xattn_bo), axis=-1)
    x = _layernorm(x + _L0_ffn_ref(x, L0_ffn_Wg, L0_ffn_W1, L0_ffn_b1, L0_ffn_W2, L0_ffn_b2, L0_ffn_W3, L0_ffn_b3), axis=-1)
    x = _layernorm(x + _L1_attn_ref(x, L1_attn_w_qkv, L1_attn_w_proj, L1_attn_b_proj), axis=-1)
    x = _layernorm(x + _L1_xattn_ref(x, ctx_1024, ctx_1024, L1_xattn_Wi, L1_xattn_bi, L1_xattn_Wg, L1_xattn_bg, L1_xattn_A, L1_xattn_Bm, L1_xattn_Wo, L1_xattn_bo, L1_xattn_decay), axis=-1)
    x = _layernorm(x + _L1_ffn_ref(x, L1_ffn_switch_w, L1_ffn_switch_b, L1_ffn_w1, L1_ffn_b1, L1_ffn_w2, L1_ffn_b2), axis=-1)
    return x

_drawn_inputs = setup_inputs


def setup_inputs(seed=0):
    import zlib

    import numpy as np

    out = dict(_drawn_inputs(seed))
    spreads = {'L0_attn_bq': (0.0, 0.1),
     'L0_attn_bk': (0.0, 0.8),
     'L0_attn_bv': (0.0, 0.1),
     'L0_attn_bo': (0.0, 0.1),
     'L0_attn_b1': (0.0, 0.1),
     'L0_attn_b2': (0.0, 0.1),
     'L0_attn_ln1_g': (1.0, 0.2),
     'L0_attn_ln1_b': (0.0, 0.1),
     'L0_attn_ln2_g': (1.0, 0.2),
     'L0_attn_ln2_b': (0.0, 0.1),
     'L0_xattn_bq': (0.0, 0.1),
     'L0_xattn_bk': (0.0, 0.8),
     'L0_xattn_bv': (0.0, 0.1),
     'L0_xattn_bo': (0.0, 0.1),
     'L1_attn_b_proj': (0.0, 0.1),
     'L1_xattn_decay': (0.8999999761581421, 0.2),
     'L1_ffn_switch_b': (0.0, 0.1),
     'L1_ffn_b1': (0.0, 0.3),
     'L1_ffn_b2': (0.0, 0.1)}
    factors = {'L1_xattn_bi': 6.434, 'L1_xattn_bg': 8.0}
    for name, (base, spread) in spreads.items():
        noise = np.random.default_rng([zlib.crc32(name.encode()), seed]).standard_normal(out[name].shape)
        drawn = base * np.exp(spread * noise) if base else spread * noise
        out[name] = jnp.asarray(drawn.astype(out[name].dtype))
    for name, factor in factors.items():
        out[name] = (out[name] * factor).astype(out[name].dtype)
    return out
```

```python
from contextlib import ExitStack

import numpy as np
import concourse.bass as bass
from concourse import mybir

F32 = mybir.dt.float32
BF16 = mybir.dt.bfloat16
I32 = mybir.dt.int32
U32 = mybir.dt.uint32
ACT = mybir.ActivationFunctionType
ALU = mybir.AluOpType
AX = mybir.AxisListType

P = 128
BATCH = 32
PAIRS = BATCH // 2
HEADS = 16
DH = P // HEADS
G = 4
VC = 32
SCALE = float(np.float32(1.0) / np.sqrt(np.float32(DH)))
EPS = 1e-5
MASKED = -1e30
WINDOW = 64
EXPERTS = 8
FF0 = 256
FF1 = 512
TOKENS = BATCH * P
REGION = TOKENS + P
TILES0 = 2 * TOKENS // P + EXPERTS
TILES1 = TOKENS // P + EXPERTS


class Chain:

    def __init__(self, eng, sem, turn, per_turn):
        self.eng, self.sem, self.turn, self.per_turn, self.count = eng, sem, turn, per_turn, 0

    def mark(self, ins):
        ins.then_inc(self.sem, 1)
        self.count += 1
        return self.sem, self.turn * self.per_turn + self.count

    def wait(self, step):
        self.eng.wait_ge(*step)

    def close(self):
        assert self.count == self.per_turn, f"per_turn should be {self.count}"


LEAD = 1


def give_leads(eng, ctx):
    for sem in ctx.led:
        eng.sem_inc(sem, LEAD)


class Phase(ExitStack):

    def __init__(self, nc):
        super().__init__()
        self.nc, self.sems, self.led = nc, [], []
        self.callback(self.clear)

    def sem(self, name, lead=0):
        self.sems.append(self.nc.alloc_semaphore(name))
        if lead:
            self.led.append(self.sems[-1])
        return self.sems[-1]

    def clear(self):
        self.nc.clear_and_free_semaphores(self.sems)
        self.nc.all_engine_barrier()


def stand_alone(eng, c):
    eng.sem_inc(c["stood"], 1)


def bcast(ap, n):
    return ap.unsqueeze(2).to_broadcast([ap.shape[0], ap.shape[1], n])


def repeat(ap, n):
    return ap.unsqueeze(1).to_broadcast([ap.shape[0], n, ap.shape[1]])


def tile_of(big, n):
    return big[:, bass.ds(n, 1), :].rearrange("p o a -> p (o a)")


def dram_tile(d, n):
    return d[bass.ds(n, 1)].rearrange("o p a -> (o p) a")



def load_constants(nc, ctx, d):
    c = dict()
    named = {}
    loads = []

    def sb(name, shape, dt=F32):
        return ctx.enter_context(nc.sbuf_tensor("c_" + name, shape, dt))

    def plain(name, src, shape, dt=F32):
        t = sb(name, shape, dt)
        loads.append((t, src))
        return t

    c["ident"] = plain("ident", d["ident"], [P, P])
    c["mask_q"] = plain("mask_q", d["mask_q"], [P, G])
    c["mask_k"] = plain("mask_k", d["mask_k"], [P, G])
    c["iota8"] = plain("iota8", d["iota8"].partition_broadcast(P), [P, EXPERTS])
    c["window"] = plain("window", d["window"], [P, P])
    c["causal"] = plain("causal", d["causal"], [P, P])
    c["cos"] = plain("cos", d["cos"], [P, P])
    c["sin"] = plain("sin", d["sin"], [P, P])
    c["tri_f"] = plain("tri_f", d["tri"], [P, P])
    c["dist"] = plain("dist", d["dist"], [P, P])
    c["ds_col"] = plain("ds_col", d["ds"].partition_broadcast(P), [P, 1])
    c["row_base"] = plain("row_base", d["row_base"].partition_broadcast(P), [P, EXPERTS])
    c["iota_tiles"] = plain("iota_tiles", d["iota_tiles"].partition_broadcast(P), [P, TILES0])
    c["part_iota"] = plain("part_iota", d["part_iota"], [P, 1])
    for name in ("a_wq", "a_wk", "a_wv", "a_wo", "x_wq", "x_wk", "x_wv", "x_wo",
                 "l_wq", "l_wk", "l_wqp", "l_wkp", "l_wv", "l_wo"):
        named[name] = plain(name, d[name], [P, P])
    for name in ("a_bq", "a_bk", "x_bq", "x_bk"):
        named[name] = plain(name, d[name].rearrange("(p o) -> p o", o=1), [P, 1])
    for name in ("a_bv", "a_bo", "a_b2", "ln1_g", "ln1_b", "ln2_g", "ln2_b", "x_bv", "x_bo", "l_bo"):
        named[name] = plain(name, d[name].partition_broadcast(P), [P, P])
    c.update(named)
    c["a_w1"] = plain("a_w1", d["a_w1"], [P, FF1])
    c["a_b1"] = plain("a_b1", d["a_b1"], [P, FF1 // P])
    c["a_w2"] = sb("a_w2", [P, FF1 // P, P])
    loads.append((c["a_w2"], d["a_w2"].rearrange("(k p) n -> p k n", p=P)))
    c["gate0"] = plain("gate0", d["gate0"], [P, EXPERTS])
    c["gate1"] = plain("gate1", d["gate1"], [P, EXPERTS])
    c["gate1_b"] = plain("gate1_b", d["gate1_b"].partition_broadcast(P), [P, EXPERTS])
    c["bias0"] = sb("bias0", [P, HEADS, P])
    loads.append((c["bias0"], d["head_mask"].partition_broadcast(P)))
    c["nds"] = sb("nds", [P, 1])
    c["zeros"] = sb("zeros", [P, P])
    c["one_row"] = sb("one_row", [P, EXPERTS])
    c["tri"] = sb("tri", [P, P], BF16)
    c["ones"] = sb("ones", [P, P], BF16)
    c["minus_half"] = sb("minus_half", [P, 1])
    c["stood"] = nc.alloc_semaphore("stood")

    with Phase(nc) as inner:
        loaded = inner.sem("constants_loaded")
        nds_ready = inner.sem("nds_ready")
        made = inner.sem("constants_made")
        block = inner.enter_context(nc.Block())

        @block.sync
        def _(sp):
            for tile, src in loads[0::2]:
                sp.dma_start(tile[:], src).then_inc(loaded, 16)

        @block.scalar
        def _(act):
            for tile, src in loads[1::2]:
                act.dma_start(tile[:], src).then_inc(loaded, 16)

        @block.vector
        def _(dve):
            nc.vector.memset(c["zeros"][:], 0.0)
            nc.vector.memset(c["one_row"][:], 1.0)
            nc.vector.memset(c["ones"][:], 1.0)
            nc.vector.memset(c["minus_half"][:], -0.5)
            dve.wait_ge(loaded, 16 * len(loads))
            nc.vector.tensor_copy(c["tri"][:], c["tri_f"][:])
            nc.vector.tensor_scalar_mul(c["nds"][:], c["ds_col"][:], -SCALE).then_inc(nds_ready, 1)
            dve.wait_ge(nds_ready, 1)
            nc.vector.scalar_tensor_tensor(out=c["bias0"][:], in0=repeat(c["dist"][:], HEADS), scalar=c["nds"][:],
                                           in1=c["bias0"][:], op0=ALU.mult, op1=ALU.add).then_inc(made, 1)
            dve.wait_ge(made, 1)
    return c



def attention_buffers(nc, ctx, tag, ps):
    def sb(name, shape):
        return [ctx.enter_context(nc.sbuf_tensor(f"{tag}_{name}{s}", shape, F32)) for s in range(2)]

    def sem(name, lead=0):
        return ctx.sem(f"{tag}_{name}", lead)

    b = dict(ps=ps, **{name: sem(name) for name in (
        "qkv_done", "qk_split", "v_ready", "scores_done", "scores_biased", "max_ready", "probs_ready",
        "probs_transposed", "probs_t_ready", "mixed", "mix_copied", "mix_back", "rsum_ready",
        "mix_scaled", "mix_transposed", "mixT_ready", "attn_done")})
    b["qm"] = sb("q_by_place", [P, G, P])
    b["kg"] = sb("k_by_group", [P, G, P])
    b["va"] = sb("values", [P, HEADS, VC])
    b["sc"] = sb("scores", [P, 2, G, P])
    b["nmax"] = sb("neg_max", [P, G, G])
    b["pr"] = sb("probs", [P, 2, G, P])
    b["pt"] = sb("probs_t", [P, 2, G * P])
    b["ot"] = sb("mix_t", [P, G * P])
    b["rs"] = sb("rsum", [P, HEADS])
    b["mix"] = sb("mix", [P, P])
    b["mixT"] = sb("mixT", [P, P])
    return b


def pe_attention(nc, pe, b, w, m, q_src, kv_src, ready):
    q_bank, t_bank, s_bank, o_bank = b["ps"]["m"], b["ps"]["t"], b["ps"]["s"], b["ps"]["o"]
    for s in range(2):
        ready(s)
        mats = (w["wq"], w["wqp"], w["wk"], w["wkp"]) if w["rope"] else (w["wq"], w["wk"])
        for k, mat in enumerate(mats):
            src = q_src if (k < len(mats) // 2) else kv_src
            nc.tensor.matmul(q_bank[s][:, k * P:(k + 1) * P], lhsT=mat[:], rhs=src[s], start=True, stop=True)
        nc.tensor.matmul(t_bank[s][:, 0:P], lhsT=kv_src[s], rhs=w["wv"][:], start=True, stop=True).then_inc(b["qkv_done"], 1)

    def scores(j, s):
        if j == 0:
            pe.wait_ge(b["qk_split"], m * 2 + (s + 1))
        else:
            pe.wait_ge(b["scores_biased"], m * 8 + (2 * j + s - 1))
        nc.tensor.matmul(s_bank[s][:], lhsT=b["qm"][s][:, j, :], rhs=b["kg"][s][:].rearrange("p g u -> p (g u)"),
                         start=True, stop=True).then_inc(b["scores_done"], 1)

    def turn(j, s):
        pe.wait_ge(b["probs_ready"], m * 8 + (2 * j + s + 1))
        if j == 0:
            pe.wait_ge(b["v_ready"], m * 2 + (s + 1))
        else:
            pe.wait_ge(b["probs_t_ready"], m * 8 + (2 * j + s - 1))
        for g in range(G):
            last = nc.tensor.transpose(t_bank[s][:, g * P:(g + 1) * P], b["pr"][s][:, j % 2, g, :], w["ident"][:])
        last.then_inc(b["probs_transposed"], 1)

    def mix(j, s):
        pe.wait_ge(b["probs_t_ready"], m * 8 + (2 * j + s + 1))
        for g in range(G):
            last = nc.tensor.matmul(o_bank[s][32 * g:32 * g + VC, j * P:(j + 1) * P],
                                    lhsT=b["va"][s][:, G * g + j, :], rhs=b["pt"][s][:, j % 2, g * P:(g + 1) * P],
                                    start=True, stop=True)
        last.then_inc(b["mixed"], 1)

    for s in range(2):
        scores(0, s)
    for j in range(G):
        for s in range(2):
            if j + 1 < G:
                scores(j + 1, s)
        for s in range(2):
            if j:
                mix(j - 1, s)
            turn(j, s)
    for s in range(2):
        mix(G - 1, s)
    for s in range(2):
        pe.wait_ge(b["mix_copied"], m * 2 + (s + 1))
        for j in range(G):
            last = nc.tensor.transpose(t_bank[s][:, j * P:(j + 1) * P], b["ot"][s][:, j * P:(j + 1) * P], w["ident"][:])
        last.then_inc(b["mix_back"], 1)
    for s in range(2):
        pe.wait_ge(b["mix_scaled"], m * 2 + (s + 1))
        nc.tensor.transpose(q_bank[s][:, 0:P], b["mix"][s][:], w["ident"][:]).then_inc(b["mix_transposed"], 1)
    for s in range(2):
        pe.wait_ge(b["mixT_ready"], m * 2 + (s + 1))
        nc.tensor.matmul(q_bank[s][:, P:2 * P], lhsT=b["mixT"][s][:], rhs=w["wo"][:],
                         start=True, stop=True).then_inc(b["attn_done"], 1)


def act_attention(nc, act, b, m):
    for j in range(G):
        for s in range(2):
            act.wait_ge(b["max_ready"], m * 8 + (2 * j + s + 1))
            if j >= 2:
                act.wait_ge(b["probs_transposed"], m * 8 + (2 * j + s - 3))
            for g in range(G):
                last = nc.scalar.activation(b["pr"][s][:, j % 2, g, :], b["sc"][s][:, j % 2, g, :], ACT.Exp,
                                            bias=b["nmax"][s][:, j, g:g + 1], scale=1.0)
            last.then_inc(b["probs_ready"], 1)
        for s in range(2):
            act.wait_ge(b["probs_transposed"], m * 8 + (2 * j + s + 1))
            if j >= 2:
                act.wait_ge(b["mixed"], m * 8 + (2 * j + s - 3))
            nc.scalar.activation(b["pt"][s][:, j % 2, :], b["ps"]["t"][s][:], ACT.Copy).then_inc(b["probs_t_ready"], 1)
    for s in range(2):
        act.wait_ge(b["mixed"], m * 8 + (6 + s + 1))
        nc.scalar.activation(b["ot"][s][:], b["ps"]["o"][s][:], ACT.Copy).then_inc(b["mix_copied"], 1)
    for s in range(2):
        act.wait_ge(b["mix_transposed"], m * 2 + (s + 1))
        nc.scalar.activation(b["mixT"][s][:], b["ps"]["m"][s][:, 0:P], ACT.Copy).then_inc(b["mixT_ready"], 1)


def dve_attention(nc, dve, b, w, m, chain):
    for s in range(2):
        dve.wait_ge(b["qkv_done"], m * 2 + (s + 1))
        q_bank = b["ps"]["m"][s]
        if w["rope"]:
            steps = []
            for k, tmp in enumerate((w["rq"][s], w["rk"][s])):
                nc.vector.tensor_tensor(tmp[:, 0, :], q_bank[:, 2 * k * P:(2 * k + 1) * P], w["cos"][:], ALU.mult)
                steps.append(chain.mark(nc.vector.tensor_tensor(tmp[:, 1, :], q_bank[:, (2 * k + 1) * P:(2 * k + 2) * P],
                                                                w["sin"][:], ALU.mult)))
            for k, tmp in enumerate((w["rq"][s], w["rk"][s])):
                chain.wait(steps[k])
                steps[k] = chain.mark(nc.vector.tensor_tensor(tmp[:, 2, :], tmp[:, 0, :], tmp[:, 1, :], ALU.add))
            for k, (tmp, out, mask) in enumerate(((w["rq"][s], b["qm"][s], w["mask_q"]), (w["rk"][s], b["kg"][s], w["mask_k"]))):
                chain.wait(steps[k])
                last = nc.vector.tensor_tensor(out[:], repeat(tmp[:, 2, :], G), bcast(mask[:], P), ALU.mult)
            last.then_inc(b["qk_split"], 1)
            nc.vector.tensor_copy(b["va"][s][:, :, 0:DH], b["ps"]["t"][s][:, 0:P].rearrange("p (h d) -> p h d", d=DH))\
                .then_inc(b["v_ready"], 1)
        else:
            nc.vector.scalar_tensor_tensor(out=b["qm"][s][:], in0=repeat(q_bank[:, 0:P], G), scalar=w["bq"][:],
                                           in1=bcast(w["mask_q"][:], P), op0=ALU.add, op1=ALU.mult)
            nc.vector.scalar_tensor_tensor(out=b["kg"][s][:], in0=repeat(q_bank[:, P:2 * P], G), scalar=w["bk"][:],
                                           in1=bcast(w["mask_k"][:], P), op0=ALU.add, op1=ALU.mult)\
                .then_inc(b["qk_split"], 1)
            nc.vector.tensor_tensor(b["va"][s][:, :, 0:DH], b["ps"]["t"][s][:, 0:P].rearrange("p (h d) -> p h d", d=DH),
                                    w["bv"][:].rearrange("p (h d) -> p h d", d=DH), ALU.add).then_inc(b["v_ready"], 1)
    for j in range(G):
        for s in range(2):
            dve.wait_ge(b["scores_done"], m * 8 + (2 * j + s + 1))
            if j >= 2:
                dve.wait_ge(b["probs_ready"], m * 8 + (2 * j + s - 3))
            bias = w["bias"][:, G * j:G * j + G, :] if w["bias_by_head"] else repeat(w["bias"][:], G)
            nc.vector.tensor_tensor(b["sc"][s][:, j % 2], b["ps"]["s"][s][:].rearrange("p (g u) -> p g u", g=G), bias,
                                    ALU.add).then_inc(b["scores_biased"], 1)
        for s in range(2):
            dve.wait_ge(b["scores_biased"], m * 8 + (2 * j + s + 1))
            nc.vector.tensor_reduce(b["nmax"][s][:, j, :], b["sc"][s][:, j % 2], AX.X, ALU.max, negate=True)\
                .then_inc(b["max_ready"], 1)
    for s in range(2):
        dve.wait_ge(b["mix_back"], m * 2 + (s + 1))
        mixed = b["ps"]["t"][s][:].rearrange("p (h c) -> p h c", c=VC)
        nc.vector.reciprocal(b["rs"][s][:], mixed[:, :, DH]).then_inc(b["rsum_ready"], 1)
    for s in range(2):
        mixed = b["ps"]["t"][s][:].rearrange("p (j g c) -> p j g c", c=VC, j=G)
        dve.wait_ge(b["rsum_ready"], m * 2 + (s + 1))
        nc.vector.tensor_tensor(b["mix"][s][:].rearrange("p (g j d) -> p j g d", g=G, j=G), mixed[:, :, :, 0:DH],
                                b["rs"][s][:].rearrange("p (j g) -> p j g", g=G).unsqueeze(3).to_broadcast([P, G, G, DH]),
                                ALU.mult).then_inc(b["mix_scaled"], 1)



def norm_buffers(nc, ctx, tag, c):
    n = dict(c=c)
    n["stats"] = [ctx.enter_context(nc.sbuf_tensor(f"{tag}_stats{s}", [P, 6], F32)) for s in range(2)]
    n["mv"] = [ctx.enter_context(nc.sbuf_tensor(f"{tag}_mv{s}", [P, 2], F32)) for s in range(2)]
    n["ve"] = [ctx.enter_context(nc.sbuf_tensor(f"{tag}_ve{s}", [P, 1], F32)) for s in range(2)]
    n["rstd"] = [ctx.enter_context(nc.sbuf_tensor(f"{tag}_rstd{s}", [P, 1], F32)) for s in range(2)]
    n["var_ready"] = ctx.sem(f"{tag}_var_ready")
    n["rstd_ready"] = ctx.sem(f"{tag}_rstd_ready")
    return n


def dve_norm(nc, dve, n, chain, index, src, src_step, dst, affine=None, free=None, done=None):
    def finish(s, ins):
        if done is None:
            return chain.mark(ins)
        ins.then_inc(done[0], 1)
        return done[0], done[2] + done[1] * 2 + (s + 1)

    steps = list(src_step)
    for s in range(2):
        chain.wait(steps[s])
        steps[s] = chain.mark(nc.vector.bn_stats(n["stats"][s][:], src[s]))
    for s in range(2):
        chain.wait(steps[s])
        stand_alone(dve, n["c"])
        steps[s] = chain.mark(nc.vector.bn_aggr(n["mv"][s][:], n["stats"][s][:]))
    for s in range(2):
        chain.wait(steps[s])
        nc.vector.tensor_scalar_add(n["ve"][s][:], n["mv"][s][:, 1:2], EPS).then_inc(n["var_ready"], 1)
    for s in range(2):
        dve.wait_ge(n["rstd_ready"], index * 2 + (s + 1))
        if free:
            free(s)
        ins = nc.vector.tensor_scalar(dst[s], src[s], n["mv"][s][:, 0:1], n["rstd"][s][:], ALU.subtract, ALU.mult)
        steps[s] = chain.mark(ins) if affine else finish(s, ins)
    if affine:
        gain, offset = affine
        for s in range(2):
            chain.wait(steps[s])
            steps[s] = chain.mark(nc.vector.tensor_tensor(dst[s], dst[s], gain[:], ALU.mult))
        for s in range(2):
            chain.wait(steps[s])
            steps[s] = finish(s, nc.vector.tensor_tensor(dst[s], dst[s], offset[:], ALU.add))
    return steps


def pool_norm(nc, pool, n, c, index):
    for s in range(2):
        pool.wait_ge(n["var_ready"], index * 2 + (s + 1))
        nc.gpsimd.tensor_tensor(n["rstd"][s][:], n["ve"][s][:], c["minus_half"][:], ALU.pow).then_inc(n["rstd_ready"], 1)


def banks(nc, ctx, tag):
    def pair(name):
        return [ctx.enter_context(nc.psum_tensor(f"{tag}_bank_{name}{s}", [P, 512], F32)) for s in range(2)]

    return dict(s=pair("s"), t=pair("t"), o=pair("o"), m=pair("m"))



def route_buffers(nc, ctx, tag, picks):
    def sb(name, shape, dt=F32):
        return [ctx.enter_context(nc.sbuf_tensor(f"{tag}_{name}{s}", shape, dt)) for s in range(2)]

    def sem(name, lead=0):
        return ctx.sem(f"{tag}_{name}", lead)

    return dict(picks=picks, logits=sb("logits", [P, EXPERTS]), top=sb("top", [P, 8]), at=sb("at", [P, 8], U32),
                 at_f=sb("at_f", [P, 8]), hot=sb("hot", [P, 2, EXPERTS]), any=sb("any", [P, EXPERTS], BF16),
                 place=sb("place", [P, EXPERTS]), put=sb("put", [P, 2, EXPERTS]), row=sb("row", [P, 2]),
                 row_u=sb("row_u", [P, 2], U32), gap=sb("gap", [P, EXPERTS]), ex=sb("ex", [P, EXPERTS]),
                 den=sb("den", [P, 1]),
                 logits_done=sem("logits_done"), gap_ready=sem("gap_ready"), ex_ready=sem("ex_ready"),
                 hot_ready=sem("hot_ready"), counted=sem("counted"), rows_ready=sem("rows_ready"),
                 scattered=[sem("scattered0"), sem("scattered1")], rows_free=sem("rows_free", LEAD))


def pe_count(nc, pe, r, c, bank, turn):
    for s in range(2):
        pe.wait_ge(r["hot_ready"], turn * 2 + (s + 1))
        nc.tensor.matmul(bank[s][:, 16:24], lhsT=c["tri"][:], rhs=r["any"][s][:], start=True, stop=True)
        nc.tensor.matmul(bank[s][:, 24:32], lhsT=c["ones"][:], rhs=r["any"][s][:], start=True, stop=True)\
            .then_inc(r["counted"], 1)


def dve_route(nc, dve, r, c, chain, turn, bank, gate_bias, kept):
    k = r["picks"]
    taken = kept["taken"]
    step = [0, 0]
    for s in range(2):
        dve.wait_ge(r["logits_done"], turn * 2 + (s + 1))
        if gate_bias is None:
            ins = nc.vector.tensor_copy(r["logits"][s][:], bank[s][:, 0:EXPERTS])
        else:
            ins = nc.vector.tensor_tensor(r["logits"][s][:], bank[s][:, 0:EXPERTS], gate_bias[:], ALU.add)
        step[s] = chain.mark(ins)
    for s in range(2):
        chain.wait(step[s])
        stand_alone(dve, c)
        step[s] = chain.mark(nc.vector.max(r["top"][s][:], r["logits"][s][:]))
    for s in range(2):
        chain.wait(step[s])
        src = r["logits"][s][:] if k == 1 else r["top"][s][:]
        nc.vector.tensor_scalar(r["gap"][s][:], src, r["top"][s][:, 0:1], None, ALU.subtract).then_inc(r["gap_ready"], 1)
        step[s] = chain.mark(nc.vector.max_index(r["at"][s][:], r["top"][s][:], r["logits"][s][:]))
    for s in range(2):
        chain.wait(step[s])
        step[s] = chain.mark(nc.vector.tensor_copy(r["at_f"][s][:], r["at"][s][:]))
    for s in range(2):
        chain.wait(step[s])
        for q in range(k):
            step[s] = chain.mark(nc.vector.tensor_scalar(r["hot"][s][:, q, :], c["iota8"][:], r["at_f"][s][:, q:q + 1], None,
                                                         ALU.is_equal))
    for s in range(2):
        chain.wait(step[s])
        if k == 2:
            ins = nc.vector.tensor_tensor(r["any"][s][:], r["hot"][s][:, 0, :], r["hot"][s][:, 1, :], ALU.add)
        else:
            ins = nc.vector.tensor_copy(r["any"][s][:], r["hot"][s][:, 0, :])
        ins.then_inc(r["hot_ready"], 1)
    for s in range(2):
        dve.wait_ge(r["ex_ready"], turn * 2 + (s + 1))
        if k == 1:
            step[s] = chain.mark(nc.vector.reduce_sum(r["den"][s][:], r["ex"][s][:], AX.X))
        else:
            step[s] = chain.mark(nc.vector.tensor_scalar_add(r["den"][s][:], r["ex"][s][:, 1:2], 1.0))
    for s in range(2):
        chain.wait(step[s])
        n = turn * 2 + s
        step[s] = chain.mark(nc.vector.reciprocal(r["den"][s][:], r["den"][s][:]))
    for s in range(2):
        chain.wait(step[s])
        n = turn * 2 + s
        ex = c["one_row"][:, 0:1] if k == 1 else r["ex"][s][:, 0:k]
        nc.vector.tensor_scalar(tile_of(kept["weights"], n), ex, r["den"][s][:], None, ALU.mult)
    for s in range(2):
        dve.wait_ge(r["counted"], turn * 2 + (s + 1))
        if s == 1:
            chain.wait(after)
        step[s] = chain.mark(nc.vector.tensor_tensor(r["place"][s][:], bank[s][:, 16:24], taken[:], ALU.add))
        chain.wait(step[s])
        after = chain.mark(nc.vector.tensor_tensor(taken[:], bank[s][:, 24:32], taken[:], ALU.add))
    for s in range(2):
        step[s] = chain.mark(nc.vector.tensor_tensor(r["put"][s][:, 0:k, :], r["hot"][s][:, 0:k, :],
                                                     repeat(r["place"][s][:], k), ALU.mult))
    for s in range(2):
        chain.wait(step[s])
        step[s] = chain.mark(nc.vector.reduce_sum(r["row"][s][:, 0:k], r["put"][s][:, 0:k, :], AX.X))
    for s in range(2):
        chain.wait(step[s])
        n = turn * 2 + s
        dve.wait_ge(r["rows_free"], LEAD + turn * 2)
        nc.vector.tensor_copy(tile_of(kept["rows"], n), r["row"][s][:, 0:k])
        nc.vector.tensor_copy(r["row_u"][s][:, 0:k], r["row"][s][:, 0:k]).then_inc(r["rows_ready"], 1)
    chain.wait(after)


def pool_scatter(nc, pool, r, c, turn, src, dst):
    for s in range(2):
        pool.wait_ge(r["rows_ready"], turn * 2 + (s + 1))
        stand_alone(pool, c)
        for q in range(r["picks"]):
            nc.gpsimd.indirect_dma_start(out=dst, out_offset=bass.IndirectOffsetOnAxis(ap=r["row_u"][s][:, q:q + 1], axis=0),
                                         in_=src[s][:], in_offset=None).then_inc(r["scattered"][s], 16)
    for s in range(2):
        pool.wait_ge(r["scattered"][s], (turn + 1) * (16 * r["picks"]))
        pool.sem_inc(r["rows_free"], 1)



LINKS1 = 64


def phase_encode(nc, c, d, scr, keep, experts0):
    with Phase(nc) as ctx:
        def sb(name, shape, dt=F32):
            return [ctx.enter_context(nc.sbuf_tensor(f"e_{name}{s}", shape, dt)) for s in range(2)]

        def sem(name, lead=0):
            return ctx.sem("e_" + name, lead)

        ps = banks(nc, ctx, "e")
        b = attention_buffers(nc, ctx, "e", ps)
        nrm = norm_buffers(nc, ctx, "e", c)
        r = route_buffers(nc, ctx, "e", 2)
        wa = dict(wq=c["a_wq"], wk=c["a_wk"], wv=c["a_wv"], wo=c["a_wo"], bq=c["a_bq"], bk=c["a_bk"], bv=c["a_bv"], bias=c["bias0"],
                   bias_by_head=True, rope=False, ident=c["ident"], mask_q=c["mask_q"], mask_k=c["mask_k"])
        wx = dict(wq=c["x_wq"], wk=c["x_wk"], wv=c["x_wv"], wo=c["x_wo"], bq=c["x_bq"], bk=c["x_bk"], bv=c["x_bv"], bias=c["window"],
                   bias_by_head=False, rope=False, ident=c["ident"], mask_q=c["mask_q"], mask_k=c["mask_k"])
        xin, cin, xs = sb("x_in", [P, P]), sb("ctx_in", [P, P]), sb("x", [P, P])
        xc = sb("xT_ctxT", [P, 2 * P])
        xT, cT = [t[:, 0:P] for t in xc], [t[:, P:2 * P] for t in xc]
        sub, x1, x1T = sb("sub", [P, P]), sb("x1", [P, P]), sb("x1T", [P, P])
        hid, x2, x2T = sb("hidden", [P, FF1]), sb("x2", [P, P]), sb("x2T", [P, P])
        x3, x3T = sb("x3", [P, P]), sb("x3T", [P, P])

        x_loaded = [sem(f"x_loaded{s}") for s in range(2)]
        ctx_saved, x3_saved = ([sem(f"{n}{s}", LEAD) for s in range(2)] for n in ("ctx_saved", "x3_saved"))
        x_transposed, xT_ready, x_copied = sem("x_transposed", LEAD), sem("xT_ready"), sem("x_copied", LEAD)
        x1_ready, x1_transposed, x1T_ready = sem("x1_ready"), sem("x1_transposed"), sem("x1T_ready")
        hidden_done, hidden_ready, dense_done = sem("hidden_done"), sem("hidden_ready"), sem("dense_done")
        x2_ready, x2_transposed, x2T_ready = sem("x2_ready", LEAD), sem("x2_transposed"), sem("x2T_ready")
        x3_ready, x3_transposed, x3T_ready = sem("x3_ready"), sem("x3_transposed"), sem("x3T_ready")
        dve_step, buffers_set = sem("dve_step"), sem("buffers_set")
        block = ctx.enter_context(nc.Block())

        @block.sync
        def _(sp):
            give_leads(sp, ctx)
            load_experts(sp, keep, experts0, d, ("m_wgv", "m_wd", "m_bgv", "m_bd"))
            with sp.Fori(0, PAIRS) as i:
                for s in range(2):
                    sp.wait_ge(x_transposed, LEAD + i * 2)
                    sp.wait_ge(x_copied, LEAD + i * 2)
                    sp.dma_start(xin[s][:], dram_tile(d["x"], i * 2 + s)).then_inc(x_loaded[s], 16)
                    sp.dma_start(cin[s][:], dram_tile(d["ctx"], i * 2 + s)).then_inc(x_loaded[s], 16)
                for s in range(2):
                    sp.wait_ge(xT_ready, i * 2 + (s + 1))
                    sp.dma_start(dram_tile(scr["ctxT"], i * 2 + s), cT[s]).then_inc(ctx_saved[s], 16)
                for s in range(2):
                    sp.wait_ge(x3_ready, i * 2 + (s + 1))
                    sp.dma_start(dram_tile(scr["x3"], i * 2 + s), x3[s][:]).then_inc(x3_saved[s], 16)
            for s in range(2):
                sp.wait_ge(ctx_saved[s], LEAD + 16 * PAIRS)
                sp.wait_ge(x3_saved[s], LEAD + 16 * PAIRS)

        @block.tensor
        def _(pe):
            pe.wait_ge(buffers_set, 1)
            with pe.Fori(0, PAIRS) as i:
                for s in range(2):
                    pe.wait_ge(x_loaded[s], i * 32 + 32)
                    nc.tensor.transpose(ps["m"][s][:, 0:P], xin[s][:], c["ident"][:])
                    nc.tensor.transpose(ps["m"][s][:, P:2 * P], cin[s][:], c["ident"][:]).then_inc(x_transposed, 1)

                def self_ready(s):
                    pe.wait_ge(xT_ready, i * 2 + (s + 1))
                pe_attention(nc, pe, b, wa, i * 2, xT, xT, self_ready)
                for s in range(2):
                    pe.wait_ge(x1_ready, i * 2 + (s + 1))
                    nc.tensor.transpose(ps["m"][s][:, 0:P], x1[s][:], c["ident"][:]).then_inc(x1_transposed, 1)
                for s in range(2):
                    pe.wait_ge(x1T_ready, i * 2 + (s + 1))
                    for k in range(FF1 // P):
                        last = nc.tensor.matmul(ps["s"][s][:, k * P:(k + 1) * P], lhsT=c["a_w1"][:, k * P:(k + 1) * P],
                                                rhs=x1T[s][:], start=True, stop=True)
                    last.then_inc(hidden_done, 1)
                for s in range(2):
                    pe.wait_ge(hidden_ready, i * 2 + (s + 1))
                    for k in range(FF1 // P):
                        last = nc.tensor.matmul(ps["m"][s][:, 0:P], lhsT=hid[s][:, k * P:(k + 1) * P],
                                                rhs=c["a_w2"][:, k, :], start=k == 0, stop=k == FF1 // P - 1)
                    last.then_inc(dense_done, 1)
                for s in range(2):
                    pe.wait_ge(x2_ready, LEAD + i * 2 + (s + 1))
                    nc.tensor.transpose(ps["m"][s][:, 0:P], x2[s][:], c["ident"][:]).then_inc(x2_transposed, 1)

                def cross_ready(s):
                    pe.wait_ge(x2T_ready, i * 2 + (s + 1))
                pe_attention(nc, pe, b, wx, i * 2 + 1, [t[:] for t in x2T], cT, cross_ready)
                for s in range(2):
                    pe.wait_ge(x3_ready, i * 2 + (s + 1))
                    nc.tensor.transpose(ps["m"][s][:, 0:P], x3[s][:], c["ident"][:]).then_inc(x3_transposed, 1)
                for s in range(2):
                    pe.wait_ge(x3T_ready, i * 2 + (s + 1))
                    nc.tensor.matmul(ps["o"][s][:, 0:EXPERTS], lhsT=x3T[s][:], rhs=c["gate0"][:],
                                     start=True, stop=True).then_inc(r["logits_done"], 1)
                pe_count(nc, pe, r, c, ps["o"], i)

        @block.scalar
        def _(act):
            with act.Fori(0, PAIRS) as i:
                for s in range(2):
                    act.wait_ge(x_transposed, LEAD + i * 2 + (s + 1))
                    act.wait_ge(ctx_saved[s], LEAD + i * 16)
                    nc.scalar.activation(xc[s][:], ps["m"][s][:, 0:2 * P], ACT.Copy).then_inc(xT_ready, 1)
                act_attention(nc, act, b, i * 2)
                for s in range(2):
                    act.wait_ge(x1_transposed, i * 2 + (s + 1))
                    nc.scalar.activation(x1T[s][:], ps["m"][s][:, 0:P], ACT.Copy).then_inc(x1T_ready, 1)
                for s in range(2):
                    act.wait_ge(hidden_done, i * 2 + (s + 1))
                    for k in range(FF1 // P):
                        last = nc.scalar.activation(hid[s][:, k * P:(k + 1) * P], ps["s"][s][:, k * P:(k + 1) * P],
                                                    ACT.Relu, bias=c["a_b1"][:, k:k + 1])
                    last.then_inc(hidden_ready, 1)
                for s in range(2):
                    act.wait_ge(x2_transposed, i * 2 + (s + 1))
                    nc.scalar.activation(x2T[s][:], ps["m"][s][:, 0:P], ACT.Copy).then_inc(x2T_ready, 1)
                act_attention(nc, act, b, i * 2 + 1)
                for s in range(2):
                    act.wait_ge(x3_transposed, i * 2 + (s + 1))
                    nc.scalar.activation(x3T[s][:], ps["m"][s][:, 0:P], ACT.Copy).then_inc(x3T_ready, 1)
                for s in range(2):
                    act.wait_ge(r["gap_ready"], i * 2 + (s + 1))
                    nc.scalar.activation(r["ex"][s][:], r["gap"][s][:], ACT.Exp).then_inc(r["ex_ready"], 1)

        @block.gpsimd
        def _(pool):
            with pool.Fori(0, PAIRS) as i:
                for s in range(2):
                    pool.wait_ge(x_loaded[s], i * 32 + 32)
                    pool.wait_ge(x2_ready, LEAD + i * 2)
                    stand_alone(pool, c)
                    nc.gpsimd.tensor_copy(xs[s][:], xin[s][:]).then_inc(x_copied, 1)
                for k in range(4):
                    pool_norm(nc, pool, nrm, c, i * 4 + k)
                pool_scatter(nc, pool, r, c, i, x3, scr["sorted0"])

        @block.vector
        def _(dve):
            for s in range(2):
                nc.vector.memset(b["va"][s][:], 0.0)
            nc.vector.memset(r["hot"][0][:], 0.0)
            nc.vector.tensor_copy(keep["route0"]["taken"][:], c["row_base"][:]).then_inc(buffers_set, 1)
            dve.wait_ge(buffers_set, 1)
            for s in range(2):
                last = nc.vector.memset(b["va"][s][:, :, DH:DH + 1], 1.0)
            last.then_inc(buffers_set, 1)
            dve.wait_ge(buffers_set, 2)
            with dve.Fori(0, PAIRS) as i:
                chain = Chain(dve, dve_step, i, LINKS1)

                def add(out, a, bb, step=None):
                    steps = []
                    for s in range(2):
                        if step is not None:
                            chain.wait(step[s])
                        steps.append(chain.mark(nc.vector.tensor_tensor(out[s][:], a[s][:], bb[s][:], ALU.add)))
                    return steps

                dve_attention(nc, dve, b, wa, i * 2, chain)
                dve.wait_ge(b["attn_done"], i * 4 + 2)
                dve.wait_ge(x_copied, LEAD + i * 2 + 2)
                step = add(sub, [t[:, P:2 * P] for t in ps["m"]], xs)
                step = add(sub, sub, [c["a_bo"]] * 2, step)
                x1_step = dve_norm(nc, dve, nrm, chain, i * 4, [t[:] for t in sub], step, [t[:] for t in x1],
                                   (c["ln1_g"], c["ln1_b"]), done=(x1_ready, i, 0))
                dve.wait_ge(dense_done, i * 2 + 2)
                step = add(sub, [t[:, 0:P] for t in ps["m"]], x1, x1_step)
                step = add(sub, sub, [c["a_b2"]] * 2, step)
                step = dve_norm(nc, dve, nrm, chain, i * 4 + 1, [t[:] for t in sub], step, [t[:] for t in sub],
                                (c["ln2_g"], c["ln2_b"]))
                step = add(sub, sub, xs, step)
                x2_step = dve_norm(nc, dve, nrm, chain, i * 4 + 2, [t[:] for t in sub], step, [t[:] for t in x2],
                                   done=(x2_ready, i, LEAD))
                dve_attention(nc, dve, b, wx, i * 2 + 1, chain)
                dve.wait_ge(b["attn_done"], i * 4 + 4)
                step = add(sub, [t[:, P:2 * P] for t in ps["m"]], x2, x2_step)
                step = add(sub, sub, [c["x_bo"]] * 2, step)

                def x3_free(s):
                    dve.wait_ge(x3_saved[s], LEAD + i * 16)
                    dve.wait_ge(r["rows_free"], LEAD + i * 2)
                dve_norm(nc, dve, nrm, chain, i * 4 + 3, [t[:] for t in sub], step, [t[:] for t in x3],
                         free=x3_free, done=(x3_ready, i, 0))
                dve_route(nc, dve, r, c, chain, i, ps["o"], None, keep["route0"])
                chain.close()



def phase_table(nc, c, kept, tag, sorted_rows):
    with Phase(nc) as ctx:
        def sb(name, shape, dt=F32):
            return ctx.enter_context(nc.sbuf_tensor(f"{tag}_{name}", shape, dt))

        def sem(name, lead=0):
            return ctx.sem(f"{tag}_{name}", lead)

        tiles, picks = kept["tiles"], kept["picks"]
        need_f, need_i, need = sb("need_f", [P, EXPERTS]), sb("need_i", [P, EXPERTS], I32), sb("need", [P, EXPERTS])
        pad_f, pad = sb("pad_f", [P, EXPERTS]), sb("pad", [P, EXPERTS], U32)
        end, last = sb("end", [P, EXPERTS]), sb("last", [P, 1])
        tile, past = sb("tile", [P, tiles]), sb("past", [P, tiles, EXPERTS])
        weighed, expert, first = sb("weighed", [P, tiles, EXPERTS]), sb("expert", [P, tiles]), sb("first", [P, tiles])
        row = sb("row", [P, tiles])
        shift, jump = sb("shift", [P, EXPERTS]), sb("jump", [P, EXPERTS])
        n_rows = BATCH * picks
        over, moved, out_f = sb("over", [P, n_rows, EXPERTS]), sb("moved", [P, n_rows]), sb("out_f", [P, n_rows])
        pad_ready, padded, step_sem = sem("pad_ready"), sem("padded"), sem("step")
        block = ctx.enter_context(nc.Block())

        @block.vector
        def _(dve):
            count = [0]

            def step(ins):
                ins.then_inc(step_sem, 1)
                count[0] += 1
                dve.wait_ge(step_sem, count[0])

            ones = c["one_row"][:, 0:EXPERTS]
            step(nc.vector.tensor_scalar(pad_f[:], kept["taken"][:], c["part_iota"][:], None, ALU.add))
            nc.vector.tensor_copy(pad[:], pad_f[:]).then_inc(pad_ready, 1)
            step(nc.vector.tensor_tensor(need_f[:], kept["taken"][:], c["row_base"][:], ALU.subtract))
            step(nc.vector.tensor_scalar_add(need_f[:], need_f[:], float(P - 1)))
            step(nc.vector.tensor_copy(need_i[:], need_f[:]))
            step(nc.vector.tensor_scalar(need_i[:], need_i[:], 7, None, ALU.arith_shift_right))
            step(nc.vector.tensor_copy(need[:], need_i[:]))
            step(nc.vector.tensor_tensor_scan(end[:], ones, need[:], 0.0, ALU.mult, ALU.add))
            step(nc.vector.tensor_scalar_add(last[:], end[:, EXPERTS - 1:EXPERTS], -1.0))
            step(nc.vector.tensor_scalar(tile[:], c["iota_tiles"][:, 0:tiles], last[:], None, ALU.min))
            step(nc.vector.tensor_tensor(past[:], bcast(tile[:], EXPERTS), repeat(end[:], tiles), ALU.is_ge))
            step(nc.vector.reduce_sum(expert[:], past[:], AX.X))
            step(nc.vector.tensor_tensor(weighed[:], past[:], repeat(need[:], tiles), ALU.mult))
            step(nc.vector.reduce_sum(first[:], weighed[:], AX.X))
            step(nc.vector.tensor_tensor(tile[:], tile[:], first[:], ALU.subtract))
            step(nc.vector.tensor_scalar_mul(row[:], expert[:], float(REGION)))
            step(nc.vector.scalar_tensor_tensor(out=row[:], in0=tile[:], scalar=float(P), in1=row[:],
                                                op0=ALU.mult, op1=ALU.add))
            nc.vector.tensor_copy(kept["tile_expert"][:], expert[:])
            nc.vector.tensor_copy(kept["tile_row"][:], row[:])
            step(nc.vector.tensor_tensor(shift[:], end[:], need[:], ALU.subtract))
            step(nc.vector.scalar_tensor_tensor(out=shift[:], in0=shift[:], scalar=float(P), in1=c["row_base"][:],
                                                op0=ALU.mult, op1=ALU.subtract))
            nc.vector.tensor_copy(jump[:, 0:1], shift[:, 0:1])
            step(nc.vector.tensor_tensor(jump[:, 1:EXPERTS], shift[:, 1:EXPERTS], shift[:, 0:EXPERTS - 1], ALU.subtract))
            rows = kept["rows"][:, 0:BATCH, :].rearrange("p n k -> p (n k)")
            step(nc.vector.tensor_tensor(over[:], bcast(rows, EXPERTS), repeat(c["row_base"][:], n_rows), ALU.is_ge))
            step(nc.vector.tensor_tensor(over[:], over[:], repeat(jump[:], n_rows), ALU.mult))
            step(nc.vector.reduce_sum(moved[:], over[:], AX.X))
            step(nc.vector.tensor_tensor(out_f[:], moved[:], rows, ALU.add))
            nc.vector.memset(kept["weights"][:, BATCH:, :], 0.0)
            nc.vector.memset(kept["out_rows"][:, BATCH:, :], 0)
            step(nc.vector.tensor_copy(kept["out_rows"][:, 0:BATCH, :].rearrange("p n k -> p (n k)"), out_f[:]))

        @block.gpsimd
        def _(pool):
            pool.wait_ge(pad_ready, 1)
            for e in range(EXPERTS):
                nc.gpsimd.indirect_dma_start(out=sorted_rows, out_offset=bass.IndirectOffsetOnAxis(ap=pad[:, e:e + 1], axis=0),
                                             in_=c["zeros"][:], in_offset=None).then_inc(padded, 16)
            pool.wait_ge(padded, 16 * EXPERTS)



def expert_buffers(nc, ctx, tag, down):
    def sb(name, shape):
        return ctx.enter_context(nc.sbuf_tensor(name + tag, shape, F32))
    return dict(up=sb("up", [P, EXPERTS, FF1]), up_b=sb("up_b", [P, EXPERTS, FF1]),
                 down=sb("down", [P, EXPERTS, down, P]), down_b=sb("down_b", [P, EXPERTS, P]))


def load_experts(sp, keep, e, d, names):
    up, down, up_b, down_b = names
    sp.dma_start(e["up"][:], d[up]).then_inc(keep["experts_loaded"], 16)
    sp.dma_start(e["down"][:], d[down]).then_inc(keep["experts_loaded"], 16)
    sp.dma_start(e["up_b"][:], d[up_b].partition_broadcast(P)).then_inc(keep["experts_loaded"], 16)
    sp.dma_start(e["down_b"][:], d[down_b].partition_broadcast(P)).then_inc(keep["experts_loaded"], 16)


SLOTS = 4


def phase_experts(nc, c, keep, kept, e, tag, gated, sorted_rows, out_rows, loaded):
    with Phase(nc) as ctx:
        def sb(name, shape, dt=F32):
            return [ctx.enter_context(nc.sbuf_tensor(f"{tag}_{name}{s}", shape, dt)) for s in range(SLOTS)]

        def sem(name, lead=0):
            return ctx.sem(f"{tag}_{name}", lead)

        wide = [ctx.enter_context(nc.psum_tensor(f"{tag}_wide{s}", [P, FF1], F32)) for s in range(SLOTS)]
        small = [ctx.enter_context(nc.psum_tensor(f"{tag}_small{s}", [P, 512], F32)) for s in range(SLOTS)]
        hidden = FF0 if gated else FF1
        blocks = hidden // P
        rows, rowsT, pre, h, hT, y = (sb("rows", [P, P]), sb("rowsT", [P, P]), sb("pre", [P, FF1]), sb("h", [P, FF1]),
                                      sb("hT", [P, hidden]), sb("y", [P, P]))
        rows_loaded, y_saved = [sem(f"rows_loaded{s}") for s in range(SLOTS)], [sem(f"y_saved{s}", LEAD) for s in range(SLOTS)]
        rows_transposed, rowsT_ready, up_done, pre_ready = (sem("rows_transposed"), sem("rowsT_ready"), sem("up_done"),
                                                            sem("pre_ready"))
        act_ready, h_ready, h_transposed, hT_ready = sem("act_ready"), sem("h_ready"), sem("h_transposed"), sem("hT_ready")
        down_done, y_ready = sem("down_done"), sem("y_ready", LEAD)
        turns = kept["tiles"] // SLOTS
        block = ctx.enter_context(nc.Block())

        @block.sync
        def _(sp):
            give_leads(sp, ctx)

            def load(i):
                for s in range(SLOTS):
                    row = sp.value_load(kept["tile_row"][0:1, bass.ds(i * SLOTS + s, 1)], min_val=0,
                                        max_val=EXPERTS * REGION - P)
                    sp.dma_start(rows[s][:], sorted_rows[bass.ds(row, P), :]).then_inc(rows_loaded[s], 16)

            def store(i):
                for s in range(SLOTS):
                    sp.wait_ge(y_ready, LEAD + i * SLOTS + (s + 1))
                    sp.dma_start(out_rows[bass.ds((i * SLOTS + s) * P, P), :], y[s][:]).then_inc(y_saved[s], 16)

            load(0)
            with sp.Fori(0, turns - 1) as i:
                sp.wait_ge(rows_transposed, i * SLOTS + SLOTS)
                load(i + 1)
                store(i)
            store(turns - 1)
            for s in range(SLOTS):
                sp.wait_ge(y_saved[s], LEAD + 16 * turns)

        @block.tensor
        def _(pe):
            pe.wait_ge(keep["experts_loaded"], loaded)
            with pe.Fori(0, turns) as i:
                experts = [pe.value_load(kept["tile_expert"][0:1, bass.ds(i * SLOTS + s, 1)], min_val=0, max_val=EXPERTS - 1)
                           for s in range(SLOTS)]
                for s in range(SLOTS):
                    pe.wait_ge(rows_loaded[s], i * 16 + 16)
                    pe.wait_ge(y_ready, LEAD + i * SLOTS)
                    nc.tensor.transpose(small[s][:, 0:P], rows[s][:], c["ident"][:]).then_inc(rows_transposed, 1)
                for s in range(SLOTS):
                    pe.wait_ge(rowsT_ready, i * SLOTS + (s + 1))
                    nc.tensor.matmul(wide[s][:], lhsT=rowsT[s][:], rhs=tile_of(e["up"], experts[s]),
                                     start=True, stop=True).then_inc(up_done, 1)
                for s in range(SLOTS):
                    pe.wait_ge(h_ready, i * SLOTS + (s + 1))
                    for k in range(blocks):
                        last = nc.tensor.transpose(wide[s][:, k * P:(k + 1) * P], h[s][:, k * P:(k + 1) * P], c["ident"][:])
                    last.then_inc(h_transposed, 1)
                for s in range(SLOTS):
                    pe.wait_ge(hT_ready, i * SLOTS + (s + 1))
                    for k in range(blocks):
                        last = nc.tensor.matmul(
                            small[s][:, P:2 * P], lhsT=hT[s][:, k * P:(k + 1) * P],
                            rhs=e["down"][:, bass.ds(experts[s], 1), k, :].rearrange("p o n -> p (o n)"),
                            start=k == 0, stop=k == blocks - 1)
                    last.then_inc(down_done, 1)

        @block.vector
        def _(dve):
            with dve.Fori(0, turns) as i:
                experts = [dve.value_load(kept["tile_expert"][0:1, bass.ds(i * SLOTS + s, 1)], min_val=0, max_val=EXPERTS - 1)
                           for s in range(SLOTS)]
                for s in range(SLOTS):
                    dve.wait_ge(up_done, i * SLOTS + (s + 1))
                    nc.vector.tensor_tensor(pre[s][:], wide[s][:], tile_of(e["up_b"], experts[s]), ALU.add)\
                        .then_inc(pre_ready, 1)
                if gated:
                    for s in range(SLOTS):
                        dve.wait_ge(act_ready, i * SLOTS + (s + 1))
                        nc.vector.tensor_tensor(h[s][:, 0:FF0], h[s][:, 0:FF0], pre[s][:, FF0:2 * FF0], ALU.mult)\
                            .then_inc(h_ready, 1)
                for s in range(SLOTS):
                    dve.wait_ge(down_done, i * SLOTS + (s + 1))
                    dve.wait_ge(y_saved[s], LEAD + i * 16)
                    nc.vector.tensor_tensor(y[s][:], small[s][:, P:2 * P], tile_of(e["down_b"], experts[s]), ALU.add)\
                        .then_inc(y_ready, 1)

        @block.scalar
        def _(act):
            with act.Fori(0, turns) as i:
                for s in range(SLOTS):
                    act.wait_ge(rows_transposed, i * SLOTS + (s + 1))
                    nc.scalar.activation(rowsT[s][:], small[s][:, 0:P], ACT.Copy).then_inc(rowsT_ready, 1)
                for s in range(SLOTS):
                    act.wait_ge(pre_ready, i * SLOTS + (s + 1))
                    if gated:
                        nc.scalar.activation(h[s][:, 0:FF0], pre[s][:, 0:FF0], ACT.Silu).then_inc(act_ready, 1)
                    else:
                        nc.scalar.activation(h[s][:], pre[s][:], ACT.Gelu_apprx_tanh).then_inc(h_ready, 1)
                for s in range(SLOTS):
                    act.wait_ge(h_transposed, i * SLOTS + (s + 1))
                    nc.scalar.activation(hT[s][:], wide[s][:, 0:hidden], ACT.Copy).then_inc(hT_ready, 1)



def gather_buffers(nc, ctx, tag, picks):
    def sb(name, shape, dt=F32):
        return [ctx.enter_context(nc.sbuf_tensor(f"{tag}_{name}{s}", shape, dt)) for s in range(2)]
    return dict(picks=picks, rows=sb("g_rows", [P, picks], U32), weights=sb("g_weights", [P, picks]),
                 y=[sb(f"g_y{q}", [P, P]) for q in range(picks)],
                 rows_ready=ctx.sem(f"{tag}_g_rows_ready"),
                 gathered=[ctx.sem(f"{tag}_g_gathered{s}") for s in range(2)])


def pool_gather(nc, pool, g, c, kept, turn, src):
    for s in range(2):
        nc.gpsimd.tensor_copy(g["weights"][s][:], tile_of(kept["weights"], turn * 2 + s))
        nc.gpsimd.tensor_copy(g["rows"][s][:], tile_of(kept["out_rows"], turn * 2 + s)).then_inc(g["rows_ready"], 1)
    pool.wait_ge(g["rows_ready"], turn * 2 + 2)
    stand_alone(pool, c)
    for s in range(2):
        for q in range(g["picks"]):
            nc.gpsimd.indirect_dma_start(out=g["y"][q][s][:], out_offset=None, in_=src,
                                         in_offset=bass.IndirectOffsetOnAxis(ap=g["rows"][s][:, q:q + 1], axis=0))\
                .then_inc(g["gathered"][s], 16)



LINKS3 = 22


def phase_decode(nc, c, d, keep, scr, xT_all, experts1):
    with Phase(nc) as ctx:
        def sb(name, shape, dt=F32):
            return [ctx.enter_context(nc.sbuf_tensor(f"d_{name}{s}", shape, dt)) for s in range(2)]

        def sem(name, lead=0):
            return ctx.sem("d_" + name, lead)

        ps = banks(nc, ctx, "d")
        b = attention_buffers(nc, ctx, "d", ps)
        nrm = norm_buffers(nc, ctx, "d", c)
        g = gather_buffers(nc, ctx, "d", 2)
        w = dict(wq=c["l_wq"], wqp=c["l_wqp"], wk=c["l_wk"], wkp=c["l_wkp"], wv=c["l_wv"], wo=c["l_wo"], bias=c["causal"],
                  bias_by_head=False, rope=True, ident=c["ident"], mask_q=c["mask_q"], mask_k=c["mask_k"],
                  cos=c["cos"], sin=c["sin"], rq=sb("rope_q", [P, 3, P]), rk=sb("rope_k", [P, 3, P]))
        x3, sub, x4, x4T, x5 = sb("x3", [P, P]), sb("sub", [P, P]), sb("x4", [P, P]), sb("x4T", [P, P]), sb("x5", [P, P])
        x3_loaded = [sem(f"x3_loaded{s}") for s in range(2)]
        joined, x4_ready, x4_transposed, x4T_ready = sem("joined", LEAD), sem("x4_ready"), sem("x4_transposed"), sem("x4T_ready")
        x5_ready, x5_transposed, x5T_ready = sem("x5_ready", LEAD), sem("x5_transposed"), sem("x5T_ready")
        dve_step, buffers_set = sem("dve_step"), sem("buffers_set")
        block = ctx.enter_context(nc.Block())

        @block.sync
        def _(sp):
            give_leads(sp, ctx)
            load_experts(sp, keep, experts1, d, ("s_w1", "s_w2", "s_b1", "s_b2"))
            with sp.Fori(0, PAIRS) as i:
                for s in range(2):
                    sp.wait_ge(joined, LEAD + i * 2)
                    sp.dma_start(x3[s][:], dram_tile(scr["x3"], i * 2 + s)).then_inc(x3_loaded[s], 16)

        @block.gpsimd
        def _(pool):
            pool_gather(nc, pool, g, c, keep["route0"], 0, scr["expert_out0"])
            with pool.Fori(0, PAIRS) as i:
                pool.wait_ge(joined, LEAD + i * 2 + 2)
                stand_alone(pool, c)
                pool_norm(nc, pool, nrm, c, i * 2)
                pool_gather(nc, pool, g, c, keep["route0"], i + 1, scr["expert_out0"])
                pool_norm(nc, pool, nrm, c, i * 2 + 1)
            for s in range(2):
                pool.wait_ge(g["gathered"][s], 32 * (PAIRS + 1))

        @block.tensor
        def _(pe):
            pe.wait_ge(buffers_set, 2)
            with pe.Fori(0, PAIRS) as i:
                for s in range(2):
                    pe.wait_ge(x4_ready, i * 2 + (s + 1))
                    nc.tensor.transpose(ps["m"][s][:, 0:P], x4[s][:], c["ident"][:]).then_inc(x4_transposed, 1)

                def self_ready(s):
                    pe.wait_ge(x4T_ready, i * 2 + (s + 1))
                pe_attention(nc, pe, b, w, i, [t[:] for t in x4T], [t[:] for t in x4T], self_ready)
                for s in range(2):
                    pe.wait_ge(x5_ready, LEAD + i * 2 + (s + 1))
                    nc.tensor.transpose(ps["o"][s][:, 0:P], x5[s][:], c["ident"][:]).then_inc(x5_transposed, 1)

        @block.scalar
        def _(act):
            with act.Fori(0, PAIRS) as i:
                for s in range(2):
                    act.wait_ge(x4_transposed, i * 2 + (s + 1))
                    nc.scalar.activation(x4T[s][:], ps["m"][s][:, 0:P], ACT.Copy).then_inc(x4T_ready, 1)
                act_attention(nc, act, b, i)
                for s in range(2):
                    act.wait_ge(x5_transposed, i * 2 + (s + 1))
                    nc.scalar.activation(tile_of(xT_all, i * 2 + s), ps["o"][s][:, 0:P], ACT.Copy).then_inc(x5T_ready, 1)
            act.wait_ge(x5T_ready, 2 * PAIRS)

        @block.vector
        def _(dve):
            for s in range(2):
                last = nc.vector.memset(b["va"][s][:], 0.0)
            last.then_inc(buffers_set, 1)
            dve.wait_ge(buffers_set, 1)
            for s in range(2):
                last = nc.vector.memset(b["va"][s][:, :, DH:DH + 1], 1.0)
            last.then_inc(buffers_set, 1)
            with dve.Fori(0, PAIRS) as i:
                chain = Chain(dve, dve_step, i, LINKS3)
                step = [None, None]
                for s in range(2):
                    dve.wait_ge(x3_loaded[s], i * 16 + 16)
                    dve.wait_ge(x5_ready, LEAD + i * 2)
                    dve.wait_ge(g["gathered"][s], i * 32 + 32)
                    step[s] = chain.mark(nc.vector.scalar_tensor_tensor(
                        out=sub[s][:], in0=g["y"][0][s][:], scalar=g["weights"][s][:, 0:1], in1=x3[s][:], op0=ALU.mult, op1=ALU.add))
                for s in range(2):
                    chain.wait(step[s])
                    nc.vector.scalar_tensor_tensor(
                        out=sub[s][:], in0=g["y"][1][s][:], scalar=g["weights"][s][:, 1:2], in1=sub[s][:],
                        op0=ALU.mult, op1=ALU.add).then_inc(joined, 1)
                    step[s] = (joined, LEAD + i * 2 + (s + 1))
                x4_step = dve_norm(nc, dve, nrm, chain, i * 2, [t[:] for t in sub], step, [t[:] for t in x4],
                                   done=(x4_ready, i, 0))
                dve_attention(nc, dve, b, w, i, chain)
                dve.wait_ge(b["attn_done"], i * 2 + 2)
                for s in range(2):
                    chain.wait(x4_step[s])
                    step[s] = chain.mark(nc.vector.tensor_tensor(sub[s][:], ps["m"][s][:, P:2 * P], x4[s][:], ALU.add))
                for s in range(2):
                    chain.wait(step[s])
                    step[s] = chain.mark(nc.vector.tensor_tensor(sub[s][:], sub[s][:], c["l_bo"][:], ALU.add))
                dve_norm(nc, dve, nrm, chain, i * 2 + 1, [t[:] for t in sub], step, [t[:] for t in x5],
                         done=(x5_ready, i, LEAD))
                chain.close()



CHUNK = 4
CHUNKS = BATCH // CHUNK


def phase_recurrent(nc, c, d, scr, xT_all, states):
    with Phase(nc) as ctx:
        def sb(name, shape, dt=F32):
            return ctx.enter_context(nc.sbuf_tensor("n_" + name, shape, dt))

        def sem(name, lead=0):
            return ctx.sem("n_" + name, lead)

        gates, drive = sb("gates", [P, P, BATCH]), sb("drive", [P, P, BATCH])
        wi, wg, wa, wb = (sb(n, [P, P]) for n in ("wi", "wg", "wa", "wb"))
        bi, bg, decay = (sb(n, [P, 1]) for n in ("bi", "bg", "decay"))
        cin = [sb(f"ctx{k}", [P, CHUNK, P]) for k in range(2)]
        kv, mem, kept, inp, gate, part, blend = ([sb(f"{n}{k}", [P, CHUNK * P]) for k in range(2)]
                                                 for n in ("kv", "mem", "kept", "inp", "gate", "part", "blend"))
        gated = [sb(f"gated{k}", [P, BATCH]) for k in range(2)]
        pi, pg, pc = ([ctx.enter_context(nc.psum_tensor(f"n_{n}{k}", [P, 512], F32)) for k in range(2)]
                      for n in ("pi", "pg", "pc"))
        pz = [ctx.enter_context(nc.psum_tensor(f"n_pz{k}", [P, 512], F32)) for k in range(2)]
        w_loaded, ctx_loaded = sem("w_loaded"), [sem("ctx_loaded0"), sem("ctx_loaded1")]
        squared, scanned, kept_ready, inp_done, inp_ready = (sem(n) for n in ("squared", "scanned", "kept_ready",
                                                                              "inp_done", "inp_ready"))
        gate_done, gate_ready, part_ready, blend_ready, drive_done, drive_ready = (
            sem(n) for n in ("gate_done", "gate_ready", "part_ready", "blend_ready", "drive_done", "drive_ready"))
        gated_ready, summed, state_ready, gates_kept = (sem("gated_ready"), sem("summed"), sem("state_ready", LEAD),
                                                        sem("gates_kept"))
        block = ctx.enter_context(nc.Block())
        WEIGHTS = ((wi, "n_wi"), (wg, "n_wg"), (wa, "n_a"), (wb, "n_b"))
        COLUMNS = ((bi, "n_bi"), (bg, "n_bg"), (decay, "n_decay"))

        def of_chunk(big, k):
            return big[:, :, k * CHUNK:(k + 1) * CHUNK].rearrange("p t b -> p b t")

        @block.sync
        def _(sp):
            give_leads(sp, ctx)
            for tile, name in WEIGHTS:
                sp.dma_start(tile[:], d[name]).then_inc(w_loaded, 16)
            for tile, name in COLUMNS:
                sp.dma_start(tile[:], d[name].rearrange("(p o) -> p o", o=1)).then_inc(w_loaded, 16)
            for k in range(CHUNKS):
                if k >= 2:
                    sp.wait_ge(squared, k - 1)
                sp.dma_start(cin[k % 2][:], scr["ctxT"][k * CHUNK:(k + 1) * CHUNK].rearrange("b p t -> p b t"))\
                    .then_inc(ctx_loaded[k % 2], 16)

        @block.vector
        def _(dve):
            nc.vector.memset(gated[0][:], 0.0).then_inc(gated_ready, 1)
            dve.wait_ge(w_loaded, 16 * 7)

            def memory(k):
                dve.wait_ge(ctx_loaded[k % 2], 16 * (k // 2 + 1))
                flat = cin[k % 2][:].rearrange("p b t -> p (b t)")
                nc.vector.tensor_tensor(kv[k % 2][:], flat, flat, ALU.mult).then_inc(squared, 1)
                dve.wait_ge(squared, k + 1)
                for q in range(CHUNK):
                    last = nc.vector.tensor_tensor_scan(mem[k % 2][:, q * P:(q + 1) * P],
                                                        decay[:].to_broadcast([P, P]),
                                                        kv[k % 2][:, q * P:(q + 1) * P], 0.0, ALU.mult, ALU.add)
                last.then_inc(scanned, 1)
                dve.wait_ge(scanned, k + 1)
                if k >= 2:
                    dve.wait_ge(inp_done, k - 1)
                nc.vector.tensor_tensor(kept[k % 2][:], mem[k % 2][:],
                                        xT_all[:, k * CHUNK:(k + 1) * CHUNK, :].rearrange("p b t -> p (b t)"),
                                        ALU.mult).then_inc(kept_ready, 1)

            def blended(k):
                dve.wait_ge(gate_ready, k + 1)
                if k >= 2:
                    dve.wait_ge(drive_done, k - 1)
                nc.vector.tensor_copy(of_chunk(gates, k), gate[k % 2][:].rearrange("p (b t) -> p b t", b=CHUNK))
                nc.vector.tensor_tensor(part[k % 2][:], gate[k % 2][:], inp[k % 2][:], ALU.mult).then_inc(part_ready, 1)
                dve.wait_ge(part_ready, k + 1)
                nc.vector.tensor_tensor(blend[k % 2][:], inp[k % 2][:], part[k % 2][:], ALU.subtract)\
                    .then_inc(blend_ready, 1)

            def driven(k):
                dve.wait_ge(drive_done, k + 1)
                nc.vector.tensor_copy(of_chunk(drive, k), pc[k % 2][:].rearrange("p (b t) -> p b t", b=CHUNK))\
                    .then_inc(drive_ready, 1)

            memory(0)
            for k in range(CHUNKS):
                if k + 1 < CHUNKS:
                    memory(k + 1)
                blended(k)
                if k:
                    driven(k - 1)
            driven(CHUNKS - 1)
            with dve.Fori(0, P // 2 - 1) as i:
                for k in (1, 0):
                    t = i * 2 + (2 - k)
                    dve.wait_ge(state_ready, LEAD + t)
                    nc.vector.tensor_tensor(gated[k][:], tile_of(gates, t), tile_of(states, t - 1), ALU.mult)\
                        .then_inc(gated_ready, 1)
            dve.wait_ge(state_ready, LEAD + P - 1)
            nc.vector.tensor_tensor(gated[1][:], gates[:, P - 1, :], states[:, P - 2, :], ALU.mult).then_inc(gated_ready, 1)

        @block.tensor
        def _(pe):
            pe.wait_ge(w_loaded, 16 * 7)

            def inputs(k):
                pe.wait_ge(kept_ready, k + 1)
                if k >= 2:
                    pe.wait_ge(inp_ready, k - 1)
                nc.tensor.matmul(pi[k % 2][:], lhsT=wi[:], rhs=kept[k % 2][:], start=True, stop=True).then_inc(inp_done, 1)

            def gating(k):
                pe.wait_ge(inp_ready, k + 1)
                if k >= 2:
                    pe.wait_ge(gate_ready, k - 1)
                nc.tensor.matmul(pg[k % 2][:], lhsT=wg[:], rhs=inp[k % 2][:], start=True, stop=True).then_inc(gate_done, 1)

            def driving(k):
                pe.wait_ge(blend_ready, k + 1)
                if k >= 2:
                    pe.wait_ge(drive_ready, k - 1)
                nc.tensor.matmul(pc[k % 2][:], lhsT=wa[:], rhs=blend[k % 2][:], start=True, stop=False)
                nc.tensor.matmul(pc[k % 2][:], lhsT=wb[:], rhs=inp[k % 2][:], start=False, stop=True).then_inc(drive_done, 1)

            inputs(0)
            for k in range(CHUNKS):
                gating(k)
                if k + 1 < CHUNKS:
                    inputs(k + 1)
                driving(k)
            pe.wait_ge(drive_ready, CHUNKS)
            with pe.Fori(0, P // 2) as i:
                for k in range(2):
                    t = i * 2 + k
                    if k == 0:
                        pe.wait_ge(state_ready, LEAD + i * 2)
                    nc.tensor.matmul(pz[k][:, 0:BATCH], lhsT=c["ident"][:], rhs=tile_of(drive, t), start=True, stop=False)
                    pe.wait_ge(gated_ready, t + 1)
                    nc.tensor.matmul(pz[k][:, 0:BATCH], lhsT=wa[:], rhs=gated[k][:], start=False, stop=True)\
                        .then_inc(summed, 1)

        @block.scalar
        def _(act):
            act.wait_ge(w_loaded, 16 * 7)

            def inputs(k):
                act.wait_ge(inp_done, k + 1)
                if k >= 2:
                    act.wait_ge(drive_done, k - 1)
                    act.wait_ge(blend_ready, k - 1)
                nc.scalar.activation(inp[k % 2][:], pi[k % 2][:], ACT.Identity, bias=bi[:]).then_inc(inp_ready, 1)

            def gating(k):
                act.wait_ge(gate_done, k + 1)
                if k >= 2:
                    act.wait_ge(blend_ready, k - 1)
                nc.scalar.activation(gate[k % 2][:], pg[k % 2][:], ACT.Sigmoid, bias=bg[:]).then_inc(gate_ready, 1)

            inputs(0)
            for k in range(CHUNKS):
                gating(k)
                if k + 1 < CHUNKS:
                    inputs(k + 1)
            with act.Fori(0, P // 2) as i:
                for k in range(2):
                    t = i * 2 + k
                    act.wait_ge(summed, t + 1)
                    nc.scalar.activation(tile_of(states, t), pz[k][:, 0:BATCH], ACT.Tanh).then_inc(state_ready, 1)
            act.wait_ge(state_ready, LEAD + P)



LINKS4 = 26


def phase_project(nc, c, d, scr, keep, xT_all, states):
    with Phase(nc) as ctx:
        def sb(name, shape, dt=F32):
            return [ctx.enter_context(nc.sbuf_tensor(f"p_{name}{s}", shape, dt)) for s in range(2)]

        def sem(name, lead=0):
            return ctx.sem("p_" + name, lead)

        ps = banks(nc, ctx, "p")
        nrm = norm_buffers(nc, ctx, "p", c)
        r = route_buffers(nc, ctx, "p", 1)
        wo, bo = ctx.enter_context(nc.sbuf_tensor("p_wo", [P, P], F32)), ctx.enter_context(nc.sbuf_tensor("p_bo", [P, 1], F32))
        subT, x6, x6T = sb("subT", [P, P]), sb("x6", [P, P]), sb("x6T", [P, P])
        w_loaded, x6_saved = sem("w_loaded"), [sem("x6_saved0", LEAD), sem("x6_saved1", LEAD)]
        out_done, subT_ready, sub_done, x6_ready, x6_transposed = (
            sem(n) for n in ("out_done", "subT_ready", "sub_done", "x6_ready", "x6_transposed"))
        x6T_ready = sem("x6T_ready", LEAD)
        dve_step, taken_set = sem("dve_step"), sem("taken_set")
        block = ctx.enter_context(nc.Block())

        @block.sync
        def _(sp):
            give_leads(sp, ctx)
            sp.dma_start(wo[:], d["n_wo"]).then_inc(w_loaded, 16)
            sp.dma_start(bo[:], d["n_bo"].rearrange("(p o) -> p o", o=1)).then_inc(w_loaded, 16)
            with sp.Fori(0, PAIRS) as i:
                for s in range(2):
                    sp.wait_ge(x6_ready, i * 2 + (s + 1))
                    sp.dma_start(dram_tile(scr["x6"], i * 2 + s), x6[s][:]).then_inc(x6_saved[s], 16)
            for s in range(2):
                sp.wait_ge(x6_saved[s], LEAD + 16 * PAIRS)

        @block.tensor
        def _(pe):
            pe.wait_ge(w_loaded, 32)
            with pe.Fori(0, PAIRS) as i:
                for s in range(2):
                    pe.wait_ge(x6T_ready, LEAD + i * 2)
                    nc.tensor.matmul(ps["m"][s][:, 0:P], lhsT=wo[:],
                                     rhs=states[:, :, bass.ds(i * 2 + s, 1)].rearrange("p t o -> p (t o)"),
                                     start=True, stop=True).then_inc(out_done, 1)
                for s in range(2):
                    pe.wait_ge(subT_ready, i * 2 + (s + 1))
                    nc.tensor.transpose(ps["t"][s][:, 0:P], subT[s][:], c["ident"][:]).then_inc(sub_done, 1)
                for s in range(2):
                    pe.wait_ge(x6_ready, i * 2 + (s + 1))
                    nc.tensor.transpose(ps["m"][s][:, P:2 * P], x6[s][:], c["ident"][:]).then_inc(x6_transposed, 1)
                for s in range(2):
                    pe.wait_ge(x6T_ready, LEAD + i * 2 + (s + 1))
                    nc.tensor.matmul(ps["o"][s][:, 0:EXPERTS], lhsT=x6T[s][:], rhs=c["gate1"][:],
                                     start=True, stop=True).then_inc(r["logits_done"], 1)
                pe_count(nc, pe, r, c, ps["o"], i)

        @block.scalar
        def _(act):
            with act.Fori(0, PAIRS) as i:
                for s in range(2):
                    act.wait_ge(x6_transposed, i * 2 + (s + 1))
                    nc.scalar.activation(x6T[s][:], ps["m"][s][:, P:2 * P], ACT.Copy).then_inc(x6T_ready, 1)
                for s in range(2):
                    act.wait_ge(r["gap_ready"], i * 2 + (s + 1))
                    nc.scalar.activation(r["ex"][s][:], r["gap"][s][:], ACT.Exp).then_inc(r["ex_ready"], 1)

        @block.gpsimd
        def _(pool):
            with pool.Fori(0, PAIRS) as i:
                pool_norm(nc, pool, nrm, c, i)
                pool_scatter(nc, pool, r, c, i, x6, scr["sorted1"])

        @block.vector
        def _(dve):
            dve.wait_ge(w_loaded, 32)
            nc.vector.tensor_copy(keep["route1"]["taken"][:], c["row_base"][:]).then_inc(taken_set, 1)
            dve.wait_ge(taken_set, 1)
            with dve.Fori(0, PAIRS) as i:
                chain = Chain(dve, dve_step, i, LINKS4)
                for s in range(2):
                    dve.wait_ge(out_done, i * 2 + (s + 1))
                    nc.vector.scalar_tensor_tensor(out=subT[s][:], in0=ps["m"][s][:, 0:P], scalar=bo[:],
                                                   in1=tile_of(xT_all, i * 2 + s), op0=ALU.add, op1=ALU.add)\
                        .then_inc(subT_ready, 1)

                def x6_free(s):
                    dve.wait_ge(x6_saved[s], LEAD + i * 16)
                    dve.wait_ge(r["rows_free"], LEAD + i * 2)
                dve_norm(nc, dve, nrm, chain, i, [t[:, 0:P] for t in ps["t"]], [(sub_done, i * 2 + (s + 1)) for s in range(2)],
                         [t[:] for t in x6], free=x6_free, done=(x6_ready, i, 0))
                dve_route(nc, dve, r, c, chain, i, ps["o"], c["gate1_b"], keep["route1"])
                chain.close()



LINKS6 = 4


def phase_finish(nc, c, keep, scr, out):
    with Phase(nc) as ctx:
        def sb(name, shape, dt=F32):
            return [ctx.enter_context(nc.sbuf_tensor(f"f_{name}{s}", shape, dt)) for s in range(2)]

        def sem(name, lead=0):
            return ctx.sem("f_" + name, lead)

        nrm = norm_buffers(nc, ctx, "f", c)
        g = gather_buffers(nc, ctx, "f", 1)
        x6, sub, x7 = sb("x6", [P, P]), sb("sub", [P, P]), sb("x7", [P, P])
        x6_loaded, x7_saved = [sem("x6_loaded0"), sem("x6_loaded1")], [sem("x7_saved0", LEAD), sem("x7_saved1", LEAD)]
        joined, x7_ready, dve_step = sem("joined", LEAD), sem("x7_ready", LEAD), sem("dve_step")
        block = ctx.enter_context(nc.Block())

        @block.sync
        def _(sp):
            give_leads(sp, ctx)
            with sp.Fori(0, PAIRS) as i:
                for s in range(2):
                    sp.wait_ge(joined, LEAD + i * 2)
                    sp.dma_start(x6[s][:], dram_tile(scr["x6"], i * 2 + s)).then_inc(x6_loaded[s], 16)

        @block.scalar
        def _(act):
            with act.Fori(0, PAIRS) as i:
                for s in range(2):
                    act.wait_ge(x7_ready, LEAD + i * 2 + (s + 1))
                    act.dma_start(dram_tile(out, i * 2 + s), x7[s][:]).then_inc(x7_saved[s], 16)
            for s in range(2):
                act.wait_ge(x7_saved[s], LEAD + 16 * PAIRS)

        @block.gpsimd
        def _(pool):
            pool_gather(nc, pool, g, c, keep["route1"], 0, scr["expert_out1"])
            with pool.Fori(0, PAIRS) as i:
                pool.wait_ge(joined, LEAD + i * 2 + 2)
                stand_alone(pool, c)
                pool_gather(nc, pool, g, c, keep["route1"], i + 1, scr["expert_out1"])
                pool_norm(nc, pool, nrm, c, i)
            for s in range(2):
                pool.wait_ge(g["gathered"][s], 16 * (PAIRS + 1))

        @block.vector
        def _(dve):
            with dve.Fori(0, PAIRS) as i:
                chain = Chain(dve, dve_step, i, LINKS6)
                for s in range(2):
                    dve.wait_ge(x6_loaded[s], i * 16 + 16)
                    dve.wait_ge(x7_ready, LEAD + i * 2)
                    dve.wait_ge(g["gathered"][s], i * 16 + 16)
                    nc.vector.scalar_tensor_tensor(out=sub[s][:], in0=g["y"][0][s][:], scalar=g["weights"][s][:, 0:1],
                                                   in1=x6[s][:], op0=ALU.mult, op1=ALU.add).then_inc(joined, 1)

                def x7_free(s):
                    dve.wait_ge(x7_saved[s], LEAD + i * 16)
                dve_norm(nc, dve, nrm, chain, i, [t[:] for t in sub], [(joined, LEAD + i * 2 + (s + 1)) for s in range(2)],
                         [t[:] for t in x7], free=x7_free, done=(x7_ready, i, LEAD))
                chain.close()


def lay_out(inputs):
    f = {k: np.asarray(v) for k, v in inputs.items()}
    con = np.ascontiguousarray
    qkv = f["L1_attn_w_qkv"]
    swap = np.arange(P).reshape(HEADS, 2, DH // 2)[:, ::-1].reshape(P)
    heads = np.array([G * g + j for j in range(G) for g in range(G)])
    t = np.arange(P)
    inv = (np.float32(1.0) / np.float32(10000.0) ** (np.arange(0, DH, 2, dtype=np.float32) / np.float32(DH))).astype(np.float32)
    angle = (t.astype(np.float32)[None, :] * np.tile(np.concatenate([inv, inv]), HEADS)[:, None]).astype(np.float32)
    sign = np.where(np.arange(P) % DH < DH // 2, -1.0, 1.0)[:, None]
    feature = np.arange(P)
    out = dict(
        x=f["x"], ctx=f["ctx_1024"],
        ident=np.eye(P, dtype=np.float32),
        mask_q=np.float32(SCALE) * ((feature % 32 // DH)[:, None] == np.arange(G)[None, :]).astype(np.float32),
        mask_k=((feature // 32)[:, None] == np.arange(G)[None, :]).astype(np.float32),
        iota8=np.arange(EXPERTS, dtype=np.float32),
        window=np.where(np.abs(t[:, None] - t[None, :]) <= WINDOW, 0.0, MASKED).astype(np.float32),
        causal=np.where(t[None, :] <= t[:, None], 0.0, MASKED).astype(np.float32),
        head_mask=np.where(t[None, :] < heads[:, None], MASKED, 0.0).astype(np.float32),
        cos=np.cos(angle).astype(np.float32), sin=(np.sin(angle) * sign).astype(np.float32),
        tri=(t[:, None] < t[None, :]).astype(np.float32),
        dist=np.abs(t[:, None] - t[None, :]).astype(np.float32),
        row_base=(REGION * np.arange(EXPERTS)).astype(np.float32),
        iota_tiles=np.arange(TILES0, dtype=np.float32),
        part_iota=t.astype(np.float32)[:, None].copy(),
        ds=f["L0_attn_dist_scale"].reshape(1),
        a_wq=f["L0_attn_Wq"], a_wk=f["L0_attn_Wk"], a_wv=f["L0_attn_Wv"], a_wo=f["L0_attn_Wo"],
        a_bq=f["L0_attn_bq"], a_bk=f["L0_attn_bk"], a_bv=f["L0_attn_bv"], a_bo=f["L0_attn_bo"],
        a_w1=f["L0_attn_W1"], a_b1=f["L0_attn_b1"].reshape(FF1 // P, P).T, a_w2=f["L0_attn_W2"], a_b2=f["L0_attn_b2"],
        ln1_g=f["L0_attn_ln1_g"], ln1_b=f["L0_attn_ln1_b"], ln2_g=f["L0_attn_ln2_g"], ln2_b=f["L0_attn_ln2_b"],
        x_wq=con(f["L0_xattn_Wq"].T), x_wk=con(f["L0_xattn_Wk"].T), x_wv=con(f["L0_xattn_Wv"].T),
        x_wo=con(f["L0_xattn_Wo"].T), x_bq=f["L0_xattn_bq"], x_bk=f["L0_xattn_bk"], x_bv=f["L0_xattn_bv"],
        x_bo=f["L0_xattn_bo"], gate0=con(f["L0_ffn_Wg"].T),
        m_wgv=con(np.concatenate([f["L0_ffn_W1"], f["L0_ffn_W2"]], axis=1).transpose(2, 0, 1)),
        m_bgv=con(np.concatenate([f["L0_ffn_b1"], f["L0_ffn_b2"]], axis=1)),
        m_wd=f["L0_ffn_W3"].transpose(2, 0, 1).reshape(FF0 // P, P, EXPERTS, P).transpose(1, 2, 0, 3), m_bd=f["L0_ffn_b3"],
        l_wq=con(qkv[:, 0:P]), l_wk=con(qkv[:, P:2 * P]), l_wv=con(qkv[:, 2 * P:]),
        l_wqp=con(qkv[:, 0:P][:, swap]), l_wkp=con(qkv[:, P:2 * P][:, swap]),
        l_wo=f["L1_attn_w_proj"], l_bo=f["L1_attn_b_proj"],
        n_wi=con(f["L1_xattn_Wi"].T), n_wg=con(f["L1_xattn_Wg"].T), n_a=con(f["L1_xattn_A"].T),
        n_b=con(f["L1_xattn_Bm"].T), n_wo=con(f["L1_xattn_Wo"].T),
        n_bi=f["L1_xattn_bi"], n_bg=f["L1_xattn_bg"], n_bo=f["L1_xattn_bo"],
        n_decay=con(np.repeat(f["L1_xattn_decay"].reshape(HEADS), DH)),
        gate1=f["L1_ffn_switch_w"], gate1_b=f["L1_ffn_switch_b"],
        s_w1=con(f["L1_ffn_w1"].transpose(1, 0, 2)), s_b1=f["L1_ffn_b1"],
        s_w2=f["L1_ffn_w2"].reshape(EXPERTS, FF1 // P, P, P).transpose(2, 0, 1, 3), s_b2=f["L1_ffn_b2"],
    )
    return {k: con(v) for k, v in out.items()}


def keep_buffers(nc, ctx):
    def sb(name, shape, dt=F32):
        return ctx.enter_context(nc.sbuf_tensor("keep_" + name, shape, dt))
    def routing(tag, picks, tiles):
        return dict(picks=picks, tiles=tiles, weights=sb("weights" + tag, [P, BATCH + 2, picks]),
                     rows=sb("rows" + tag, [P, BATCH + 2, picks]), taken=sb("taken" + tag, [P, EXPERTS]),
                     out_rows=sb("out_rows" + tag, [P, BATCH + 2, picks], U32),
                     tile_expert=sb("tile_expert" + tag, [P, tiles], I32),
                     tile_row=sb("tile_row" + tag, [P, tiles], I32))

    return dict(route0=routing("0", 2, TILES0), route1=routing("1", 1, TILES1),
                 experts_loaded=nc.alloc_semaphore("experts_loaded"))



def program(nc, d, out):
    with ExitStack() as ctx:
        keep, scr = keep_buffers(nc, ctx), scratch(nc)
        c = load_constants(nc, ctx, d)
        with ExitStack() as first:
            experts0 = expert_buffers(nc, first, "0", FF0 // P)
            phase_encode(nc, c, d, scr, keep, experts0)
            phase_table(nc, c, keep["route0"], "t0", scr["sorted0"])
            phase_experts(nc, c, keep, keep["route0"], experts0, "m0", True, scr["sorted0"], scr["expert_out0"], 16 * 4)
        experts1 = expert_buffers(nc, ctx, "1", FF1 // P)
        with ExitStack() as second:
            xT_all = second.enter_context(nc.sbuf_tensor("xT_all", [P, BATCH, P], F32))
            phase_decode(nc, c, d, keep, scr, xT_all, experts1)
            states = second.enter_context(nc.sbuf_tensor("states", [P, P, BATCH], F32))
            phase_recurrent(nc, c, d, scr, xT_all, states)
            phase_project(nc, c, d, scr, keep, xT_all, states)
        phase_table(nc, c, keep["route1"], "t1", scr["sorted1"])
        phase_experts(nc, c, keep, keep["route1"], experts1, "m1", False, scr["sorted1"], scr["expert_out1"], 16 * 8)
        phase_finish(nc, c, keep, scr, out)


def scratch(nc):
    def dram(name, shape):
        return nc.dram_tensor("scratch_" + name, shape, F32, kind="Internal").ap()
    return dict(ctxT=dram("ctxT", (BATCH, P, P)), x3=dram("x3", (BATCH, P, P)),
                x6=dram("x6", (BATCH, P, P)),
                sorted0=dram("sorted0", (EXPERTS * REGION, P)), sorted1=dram("sorted1", (EXPERTS * REGION, P)),
                expert_out0=dram("expert_out0", (TILES0 * P, P)), expert_out1=dram("expert_out1", (TILES1 * P, P)))




def kernel(**inputs):
    from concourse import bacc
    from concourse.bass_utils import run_bass_kernel_spmd

    nc = bacc.Bacc("TRN2", target_bir_lowering=False, num_devices=1)
    arrays = lay_out(inputs)
    dram = {name: nc.dram_tensor("in_" + name, a.shape, mybir.dt.from_np(a.dtype), kind="ExternalInput").ap()
            for name, a in arrays.items()}
    out = nc.dram_tensor("out_x", (BATCH, P, P), F32, kind="ExternalOutput").ap()
    program(nc, dram, out)
    result = run_bass_kernel_spmd(nc, [{"in_" + name: a for name, a in arrays.items()}], core_ids=[0])
    return result.results[0]["out_x"]
```

```python
from contextlib import ExitStack

import numpy as np
import concourse.bass as bass
from concourse import mybir

F32 = mybir.dt.float32
BF16 = mybir.dt.bfloat16
I32 = mybir.dt.int32
U32 = mybir.dt.uint32
ACT = mybir.ActivationFunctionType
ALU = mybir.AluOpType
AX = mybir.AxisListType

P = 128
BATCH = 32
SLOTS = 4
TURNS = BATCH // SLOTS
HEADS = 16
DH = P // HEADS
G = 4
VC = 32
SCALE = float(np.float32(1.0) / np.sqrt(np.float32(DH)))
EPS = 1e-5
MASKED = -1e30
WINDOW = 64
EXPERTS = 8
FF0 = 256
FF1 = 512
TOKENS = BATCH * P
REGION = TOKENS + P
TILES0 = 2 * TOKENS // P + EXPERTS
TILES1 = TOKENS // P + EXPERTS


class Chain:

    def __init__(self, eng, sem, turn, per_turn):
        self.eng, self.sem, self.turn, self.per_turn, self.count = eng, sem, turn, per_turn, 0

    def mark(self, ins):
        ins.then_inc(self.sem, 1)
        self.count += 1
        return self.sem, self.turn * self.per_turn + self.count

    def wait(self, step):
        self.eng.wait_ge(*step)

    def close(self):
        assert self.count == self.per_turn, f"per_turn should be {self.count}"


LEAD = 1


def give_leads(eng, ctx):
    for sem in ctx.led:
        eng.sem_inc(sem, LEAD)


class Phase(ExitStack):

    def __init__(self, nc):
        super().__init__()
        self.nc, self.sems, self.led = nc, [], []
        self.callback(self.clear)

    def sem(self, name, lead=0):
        self.sems.append(self.nc.alloc_semaphore(name))
        if lead:
            self.led.append(self.sems[-1])
        return self.sems[-1]

    def clear(self):
        self.nc.clear_and_free_semaphores(self.sems)
        self.nc.all_engine_barrier()


def stand_alone(eng, c):
    eng.sem_inc(c["stood"], 1)


def bcast(ap, n):
    return ap.unsqueeze(2).to_broadcast([ap.shape[0], ap.shape[1], n])


def repeat(ap, n):
    return ap.unsqueeze(1).to_broadcast([ap.shape[0], n, ap.shape[1]])


def tile_of(big, n):
    return big[:, bass.ds(n, 1), :].rearrange("p o a -> p (o a)")


def dram_tile(d, n):
    return d[bass.ds(n, 1)].rearrange("o p a -> (o p) a")



def load_constants(nc, ctx, d):
    c = dict()
    named = {}
    loads = []

    def sb(name, shape, dt=F32):
        return ctx.enter_context(nc.sbuf_tensor("c_" + name, shape, dt))

    def plain(name, src, shape, dt=F32):
        t = sb(name, shape, dt)
        loads.append((t, src))
        return t

    c["ident"] = plain("ident", d["ident"], [P, P])
    c["mask_q"] = plain("mask_q", d["mask_q"], [P, G])
    c["mask_k"] = plain("mask_k", d["mask_k"], [P, G])
    c["iota8"] = plain("iota8", d["iota8"].partition_broadcast(P), [P, EXPERTS])
    c["window"] = plain("window", d["window"], [P, P])
    c["causal"] = plain("causal", d["causal"], [P, P])
    c["cos"] = plain("cos", d["cos"], [P, P])
    c["sin"] = plain("sin", d["sin"], [P, P])
    c["tri_f"] = plain("tri_f", d["tri"], [P, P])
    c["dist"] = plain("dist", d["dist"], [P, P])
    c["ds_col"] = plain("ds_col", d["ds"].partition_broadcast(P), [P, 1])
    c["row_base"] = plain("row_base", d["row_base"].partition_broadcast(P), [P, EXPERTS])
    c["iota_tiles"] = plain("iota_tiles", d["iota_tiles"].partition_broadcast(P), [P, TILES0])
    c["part_iota"] = plain("part_iota", d["part_iota"], [P, 1])
    for name in ("a_wq", "a_wk", "a_wv", "a_wo", "x_wq", "x_wk", "x_wv", "x_wo",
                 "l_wq", "l_wk", "l_wqp", "l_wkp", "l_wv", "l_wo"):
        named[name] = plain(name, d[name], [P, P])
    for name in ("a_bq", "a_bk", "x_bq", "x_bk"):
        named[name] = plain(name, d[name].rearrange("(p o) -> p o", o=1), [P, 1])
    for name in ("a_bv", "a_bo", "a_b2", "ln1_g", "ln1_b", "ln2_g", "ln2_b", "x_bv", "x_bo", "l_bo"):
        named[name] = plain(name, d[name].partition_broadcast(P), [P, P])
    c.update(named)
    c["a_w1"] = plain("a_w1", d["a_w1"], [P, FF1])
    c["a_b1"] = plain("a_b1", d["a_b1"], [P, FF1 // P])
    c["a_w2"] = sb("a_w2", [P, FF1 // P, P])
    loads.append((c["a_w2"], d["a_w2"].rearrange("(k p) n -> p k n", p=P)))
    c["gate0"] = plain("gate0", d["gate0"], [P, EXPERTS])
    c["gate1"] = plain("gate1", d["gate1"], [P, EXPERTS])
    c["gate1_b"] = plain("gate1_b", d["gate1_b"].partition_broadcast(P), [P, EXPERTS])
    c["bias0"] = sb("bias0", [P, HEADS, P])
    loads.append((c["bias0"], d["head_mask"].partition_broadcast(P)))
    c["nds"] = sb("nds", [P, 1])
    c["zeros"] = sb("zeros", [P, P])
    c["one_row"] = sb("one_row", [P, EXPERTS])
    c["tri"] = sb("tri", [P, P], BF16)
    c["ones"] = sb("ones", [P, P], BF16)
    c["minus_half"] = sb("minus_half", [P, SLOTS])
    c["a_bk_by_group"], c["x_bk_by_group"] = sb("a_bk_by_group", [P, G]), sb("x_bk_by_group", [P, G])
    c["stood"] = nc.alloc_semaphore("stood")

    with Phase(nc) as inner:
        loaded = inner.sem("constants_loaded")
        nds_ready = inner.sem("nds_ready")
        made = inner.sem("constants_made")
        block = inner.enter_context(nc.Block())

        @block.sync
        def _(sp):
            for tile, src in loads[0::2]:
                sp.dma_start(tile[:], src).then_inc(loaded, 16)

        @block.scalar
        def _(act):
            for tile, src in loads[1::2]:
                act.dma_start(tile[:], src).then_inc(loaded, 16)

        @block.vector
        def _(dve):
            nc.vector.memset(c["zeros"][:], 0.0)
            nc.vector.memset(c["one_row"][:], 1.0)
            nc.vector.memset(c["ones"][:], 1.0)
            nc.vector.memset(c["minus_half"][:], -0.5)
            dve.wait_ge(loaded, 16 * len(loads))
            nc.vector.tensor_copy(c["tri"][:], c["tri_f"][:])
            nc.vector.tensor_scalar(c["a_bk_by_group"][:], c["mask_k"][:], c["a_bk"][:], None, ALU.mult)
            nc.vector.tensor_scalar(c["x_bk_by_group"][:], c["mask_k"][:], c["x_bk"][:], None, ALU.mult)
            nc.vector.tensor_scalar_mul(c["nds"][:], c["ds_col"][:], -SCALE).then_inc(nds_ready, 1)
            dve.wait_ge(nds_ready, 1)
            nc.vector.scalar_tensor_tensor(out=c["bias0"][:], in0=repeat(c["dist"][:], HEADS), scalar=c["nds"][:],
                                           in1=c["bias0"][:], op0=ALU.mult, op1=ALU.add).then_inc(made, 1)
            dve.wait_ge(made, 1)
    return c



def attention_buffers(nc, ctx, tag, ps):
    def sb(name, shape):
        return [ctx.enter_context(nc.sbuf_tensor(f"{tag}_{name}{s}", shape, F32)) for s in range(SLOTS)]

    def sem(name, lead=0):
        return ctx.sem(f"{tag}_{name}", lead)

    b = dict(ps=ps, **{name: sem(name) for name in (
        "k_done", "k_rotated", "qv_done", "k_ready", "v_ready", "scores_done", "scores_biased", "max_ready", "probs_ready",
        "probs_transposed", "probs_t_ready", "mixed", "mix_back", "rsum_ready",
        "mix_scaled", "mix_transposed", "mixT_ready", "attn_done")})
    b["mix_copied"] = [sem("mix_copied_even"), sem("mix_copied_odd")]
    b["qm"] = sb("q_by_place", [P, G, P])
    b["kg"] = sb("k_by_group", [P, G, P])
    b["va"] = sb("values", [P, HEADS, VC])
    b["sc"] = sb("scores", [P, G, P])
    b["nmax"] = sb("neg_max", [P, G])
    b["pr"] = sb("probs", [P, G, P])
    b["pt"] = sb("probs_t", [P, G * P])
    b["ot"] = sb("mix_t", [P, G * P])
    b["rs"] = sb("rsum", [P, HEADS])
    b["mix"] = sb("mix", [P, P])
    b["mixT"] = sb("mixT", [P, P])
    return b


UNITS = G * SLOTS


def pe_keys(nc, pe, b, w, src, ready):
    for s in range(SLOTS):
        ready(s)
        nc.tensor.matmul(b["ps"]["x"][s][:, 0:P], lhsT=w["wk"][:], rhs=src[s], start=True, stop=True)\
            .then_inc(b["k_done"], 1)


def pe_queries(nc, pe, b, w, q_src, kv_src, ready):
    for s in range(SLOTS):
        ready(s)
        bank_x, bank_y = b["ps"]["x"][s], b["ps"]["y"][s]
        if w["rope"]:
            for k, mat in enumerate((w["wq"], w["wqp"], w["wk"], w["wkp"])):
                nc.tensor.matmul(bank_y[:, k * P:(k + 1) * P], lhsT=mat[:], rhs=q_src[s], start=True, stop=True)
            v = bank_x[:, 0:P]
        else:
            nc.tensor.matmul(bank_y[:, 0:P], lhsT=w["wq"][:], rhs=q_src[s], start=True, stop=True)
            v = bank_y[:, P:2 * P]
        nc.tensor.matmul(v, lhsT=kv_src[s], rhs=w["wv"][:], start=True, stop=True).then_inc(b["qv_done"], 1)


def act_keys(nc, act, b, w, m):
    for s in range(SLOTS):
        act.wait_ge(b["k_rotated" if w["rope"] else "k_done"], m * SLOTS + (s + 1))
        src = b["pr"][s][:, 2, :] if w["rope"] else b["ps"]["x"][s][:, 0:P]
        for g in range(G):
            last = nc.scalar.activation(b["kg"][s][:, g, :], src, ACT.Identity, bias=w["bk_by_group"][:, g:g + 1],
                                        scale=w["mask_k"][:, g:g + 1])
        last.then_inc(b["k_ready"], 1)


def dve_queries(nc, dve, b, w, m, chain, slots=range(SLOTS)):
    for s in slots:
        dve.wait_ge(b["qv_done"], m * SLOTS + (s + 1))
        bank_x, bank_y = b["ps"]["x"][s], b["ps"]["y"][s]
        if w["rope"]:
            temps, steps = (b["pr"][s], b["sc"][s]), [None, None]
            for tmp, k in zip(temps, (1, 0)):
                nc.vector.tensor_tensor(tmp[:, 0, :], bank_y[:, 2 * k * P:(2 * k + 1) * P], w["cos"][:], ALU.mult)
                steps[k] = chain.mark(nc.vector.tensor_tensor(tmp[:, 1, :], bank_y[:, (2 * k + 1) * P:(2 * k + 2) * P],
                                                              w["sin"][:], ALU.mult))
            chain.wait(steps[1])
            nc.vector.tensor_tensor(temps[0][:, 2, :], temps[0][:, 0, :], temps[0][:, 1, :], ALU.add)\
                .then_inc(b["k_rotated"], 1)
            chain.wait(steps[0])
            step = chain.mark(nc.vector.tensor_tensor(temps[1][:, 2, :], temps[1][:, 0, :], temps[1][:, 1, :], ALU.add))
            nc.vector.tensor_copy(b["va"][s][:, :, 0:DH], bank_x[:, 0:P].rearrange("p (h d) -> p h d", d=DH))
            chain.wait(step)
            nc.vector.tensor_tensor(b["qm"][s][:], repeat(temps[1][:, 2, :], G), bcast(w["mask_q"][:], P), ALU.mult)\
                .then_inc(b["v_ready"], 1)
        else:
            nc.vector.scalar_tensor_tensor(out=b["qm"][s][:], in0=repeat(bank_y[:, 0:P], G), scalar=w["bq"][:],
                                           in1=bcast(w["mask_q"][:], P), op0=ALU.add, op1=ALU.mult)
            nc.vector.tensor_tensor(b["va"][s][:, :, 0:DH], bank_y[:, P:2 * P].rearrange("p (h d) -> p h d", d=DH),
                                    w["bv"][:].rearrange("p (h d) -> p h d", d=DH), ALU.add).then_inc(b["v_ready"], 1)


def pe_attention(nc, pe, b, w, m, first=None):
    bank_x, bank_y = b["ps"]["x"], b["ps"]["y"]

    def mix(j, s):
        pe.wait_ge(b["probs_t_ready"], m * UNITS + (SLOTS * j + s + 1))
        for g in range(G):
            last = nc.tensor.matmul(bank_y[s][32 * g:32 * g + VC, j * P:(j + 1) * P],
                                    lhsT=b["va"][s][:, G * g + j, :], rhs=b["pt"][s][:, g * P:(g + 1) * P],
                                    start=True, stop=True)
        last.then_inc(b["mixed"], 1)

    def scores(j, s):
        if j == 0:
            pe.wait_ge(b["k_ready"], m * SLOTS + (s + 1))
            pe.wait_ge(b["v_ready"], m * SLOTS + (s + 1))
            if first:
                first(s)
        nc.tensor.matmul(bank_x[s][:], lhsT=b["qm"][s][:, j, :], rhs=b["kg"][s][:].rearrange("p g u -> p (g u)"),
                         start=True, stop=True).then_inc(b["scores_done"], 1)

    def turn(j, s):
        pe.wait_ge(b["probs_ready"], m * UNITS + (SLOTS * j + s + 1))
        for g in range(G):
            last = nc.tensor.transpose(bank_x[s][:, g * P:(g + 1) * P], b["pr"][s][:, g, :], w["ident"][:])
        last.then_inc(b["probs_transposed"], 1)

    for k in range(UNITS + 2):
        if k < UNITS:
            if k >= SLOTS:
                mix(k // SLOTS - 1, k % SLOTS)
            scores(k // SLOTS, k % SLOTS)
        if k >= 2:
            turn((k - 2) // SLOTS, (k - 2) % SLOTS)
    for s in range(SLOTS):
        mix(G - 1, s)
    for s in range(SLOTS):
        pe.wait_ge(b["mix_copied"][s % 2], m * (SLOTS // 2) + (s // 2 + 1))
        for j in range(G):
            last = nc.tensor.transpose(bank_x[s][:, j * P:(j + 1) * P], b["ot"][s][:, j * P:(j + 1) * P], w["ident"][:])
        last.then_inc(b["mix_back"], 1)
    for s in range(SLOTS):
        pe.wait_ge(b["mix_scaled"], m * SLOTS + (s + 1))
        nc.tensor.transpose(bank_y[s][:, 0:P], b["mix"][s][:], w["ident"][:]).then_inc(b["mix_transposed"], 1)
    for s in range(SLOTS):
        pe.wait_ge(b["mixT_ready"], m * SLOTS + (s + 1))
        nc.tensor.matmul(bank_y[s][:, P:2 * P], lhsT=b["mixT"][s][:], rhs=w["wo"][:],
                         start=True, stop=True).then_inc(b["attn_done"], 1)


def act_attention(nc, act, b, m):
    for k in range(UNITS + 1):
        if k < UNITS:
            s = k % SLOTS
            act.wait_ge(b["max_ready"], m * UNITS + (k + 1))
            for g in range(G):
                last = nc.scalar.activation(b["pr"][s][:, g, :], b["sc"][s][:, g, :], ACT.Exp,
                                            bias=b["nmax"][s][:, g:g + 1], scale=1.0)
            last.then_inc(b["probs_ready"], 1)
        if k >= 1:
            s = (k - 1) % SLOTS
            act.wait_ge(b["probs_transposed"], m * UNITS + k)
            if k - 1 >= SLOTS:
                act.wait_ge(b["mixed"], m * UNITS + (k - SLOTS))
            nc.scalar.activation(b["pt"][s][:], b["ps"]["x"][s][:], ACT.Copy).then_inc(b["probs_t_ready"], 1)
    for s in range(0, SLOTS, 2):
        act.wait_ge(b["mixed"], m * UNITS + (UNITS - SLOTS + s + 1))
        nc.scalar.activation(b["ot"][s][:], b["ps"]["y"][s][:], ACT.Copy).then_inc(b["mix_copied"][0], 1)
    for s in range(SLOTS):
        act.wait_ge(b["mix_transposed"], m * SLOTS + (s + 1))
        nc.scalar.activation(b["mixT"][s][:], b["ps"]["y"][s][:, 0:P], ACT.Copy).then_inc(b["mixT_ready"], 1)


def dve_attention(nc, dve, b, w, m, chain):
    for k in range(UNITS):
        j, s = k // SLOTS, k % SLOTS
        dve.wait_ge(b["scores_done"], m * UNITS + (k + 1))
        bias = w["bias"][:, G * j:G * j + G, :] if w["bias_by_head"] else repeat(w["bias"][:], G)
        nc.vector.tensor_tensor(b["sc"][s][:], b["ps"]["x"][s][:].rearrange("p (g u) -> p g u", g=G), bias,
                                ALU.add).then_inc(b["scores_biased"], 1)
        dve.wait_ge(b["scores_biased"], m * UNITS + (k + 1))
        nc.vector.tensor_reduce(b["nmax"][s][:], b["sc"][s][:], AX.X, ALU.max, negate=True)\
            .then_inc(b["max_ready"], 1)
    for s in range(1, SLOTS, 2):
        dve.wait_ge(b["mixed"], m * UNITS + (UNITS - SLOTS + s + 1))
        nc.vector.tensor_copy(b["ot"][s][:], b["ps"]["y"][s][:]).then_inc(b["mix_copied"][1], 1)
    for s in range(SLOTS):
        dve.wait_ge(b["mix_back"], m * SLOTS + (s + 1))
        mixed = b["ps"]["x"][s][:].rearrange("p (h c) -> p h c", c=VC)
        nc.vector.reciprocal(b["rs"][s][:], mixed[:, :, DH]).then_inc(b["rsum_ready"], 1)
    for s in range(SLOTS):
        mixed = b["ps"]["x"][s][:].rearrange("p (j g c) -> p j g c", c=VC, j=G)
        dve.wait_ge(b["rsum_ready"], m * SLOTS + (s + 1))
        nc.vector.tensor_tensor(b["mix"][s][:].rearrange("p (g j d) -> p j g d", g=G, j=G), mixed[:, :, :, 0:DH],
                                b["rs"][s][:].rearrange("p (j g) -> p j g", g=G).unsqueeze(3).to_broadcast([P, G, G, DH]),
                                ALU.mult).then_inc(b["mix_scaled"], 1)



def norm_buffers(nc, ctx, tag, c):
    def sb(name, shape):
        return ctx.enter_context(nc.sbuf_tensor(f"{tag}_{name}", shape, F32))
    return dict(c=c, stats=[sb(f"stats{s}", [P, 6]) for s in range(SLOTS)], mv=sb("mean_var", [P, SLOTS, 2]),
                ve=sb("var_eps", [P, SLOTS]), rstd=sb("rstd", [P, SLOTS]),
                var_ready=ctx.sem(f"{tag}_var_ready"), rstd_ready=ctx.sem(f"{tag}_rstd_ready"))


def dve_norm(nc, dve, n, chain, index, src, src_step, dst, affine=None, free=None, done=None, meanwhile=None):
    def finish(s, ins):
        if done is None:
            return chain.mark(ins)
        ins.then_inc(done[0], 1)
        return done[0], done[2] + done[1] * SLOTS + (s + 1)

    steps = list(src_step)
    for s in range(SLOTS):
        chain.wait(steps[s])
        steps[s] = chain.mark(nc.vector.bn_stats(n["stats"][s][:], src[s]))
    for s in range(SLOTS):
        chain.wait(steps[s])
        stand_alone(dve, n["c"])
        steps[s] = chain.mark(nc.vector.bn_aggr(n["mv"][:, s, :], n["stats"][s][:]))
    chain.wait(steps[-1])
    nc.vector.tensor_scalar_add(n["ve"][:], n["mv"][:, :, 1], EPS).then_inc(n["var_ready"], 1)
    if affine:
        gain, offset = affine
        for s in range(SLOTS):
            steps[s] = chain.mark(nc.vector.scalar_tensor_tensor(
                out=src[s], in0=src[s], scalar=n["mv"][:, s, 0:1], in1=gain[:], op0=ALU.subtract, op1=ALU.mult))
    if meanwhile:
        meanwhile()
    dve.wait_ge(n["rstd_ready"], index + 1)
    for s in range(SLOTS):
        if free:
            free(s)
        if affine:
            chain.wait(steps[s])
            ins = nc.vector.scalar_tensor_tensor(out=dst[s], in0=src[s], scalar=n["rstd"][:, s:s + 1], in1=offset[s],
                                                 op0=ALU.mult, op1=ALU.add)
        else:
            ins = nc.vector.tensor_scalar(dst[s], src[s], n["mv"][:, s, 0:1], n["rstd"][:, s:s + 1],
                                          ALU.subtract, ALU.mult)
        steps[s] = finish(s, ins)
    return steps


def pool_norm(nc, pool, n, c, index):
    pool.wait_ge(n["var_ready"], index + 1)
    nc.gpsimd.tensor_tensor(n["rstd"][:], n["ve"][:], c["minus_half"][:], ALU.pow).then_inc(n["rstd_ready"], 1)


def banks(nc, ctx, tag):
    def by_slot(name):
        return [ctx.enter_context(nc.psum_tensor(f"{tag}_bank_{name}{s}", [P, 512], F32)) for s in range(SLOTS)]

    return dict(x=by_slot("x"), y=by_slot("y"))



LOGITS, COUNTS = 0, 1


def route_buffers(nc, ctx, tag, picks):
    def sb(name, shape, dt=F32):
        return ctx.enter_context(nc.sbuf_tensor(f"{tag}_{name}", shape, dt))

    def sem(name, lead=0):
        return ctx.sem(f"{tag}_{name}", lead)

    return dict(picks=picks, logits=sb("logits", [P, SLOTS, EXPERTS]), top=sb("top", [P, SLOTS, 8]),
                at=sb("at", [P, SLOTS, 8], U32), at_f=sb("at_f", [P, SLOTS, 8]),
                hot=[sb(f"hot{q}", [P, SLOTS, EXPERTS]) for q in range(picks)],
                any=sb("any", [P, SLOTS, EXPERTS], BF16), place=sb("place", [P, SLOTS, EXPERTS]),
                put=[sb(f"put{q}", [P, SLOTS, EXPERTS]) for q in range(picks)],
                row_u=sb("row_u", [P, SLOTS, picks], U32), gap=sb("gap", [P, SLOTS, EXPERTS]),
                ex=sb("ex", [P, SLOTS, EXPERTS]), den=sb("den", [P, SLOTS]),
                logits_done=sem("logits_done"), gap_ready=sem("gap_ready"), ex_ready=sem("ex_ready"),
                hot_ready=sem("hot_ready"), counted=sem("counted"), rows_ready=sem("rows_ready", LEAD),
                scattered=[sem(f"scattered{s}") for s in range(SLOTS)], rows_free=sem("rows_free", LEAD))


def pe_logits(nc, pe, r, bank, xT, gate, ready):
    for s in range(SLOTS):
        ready(s)
        last = nc.tensor.matmul(bank[LOGITS][:, s * EXPERTS:(s + 1) * EXPERTS], lhsT=xT[s][:], rhs=gate[:],
                                start=True, stop=True)
    last.then_inc(r["logits_done"], 1)


def pe_count(nc, pe, r, c, bank, turn):
    pe.wait_ge(r["hot_ready"], turn + 1)
    for s in range(SLOTS + 1):
        out = bank[COUNTS][:, s * EXPERTS:(s + 1) * EXPERTS]
        for before in range(s):
            last = nc.tensor.matmul(out, lhsT=c["ones"][:], rhs=r["any"][:, before, :], start=before == 0,
                                    stop=s == SLOTS and before == s - 1)
        if s < SLOTS:
            nc.tensor.matmul(out, lhsT=c["tri"][:], rhs=r["any"][:, s, :], start=s == 0, stop=True)
    last.then_inc(r["counted"], 1)


def dve_route(nc, dve, r, c, chain, turn, bank, gate_bias, kept):
    picks, taken = r["picks"], kept["taken"]
    wide = [P, SLOTS, EXPERTS]

    def of_turn(big, q):
        return big[:, bass.ds(turn * SLOTS, SLOTS), q:q + 1].rearrange("p n o -> p (n o)")

    dve.wait_ge(r["logits_done"], turn + 1)
    logits = bank[LOGITS][:, 0:SLOTS * EXPERTS].rearrange("p (s e) -> p s e", e=EXPERTS)
    if gate_bias is None:
        step = chain.mark(nc.vector.tensor_copy(r["logits"][:], logits))
    else:
        step = chain.mark(nc.vector.tensor_tensor(r["logits"][:], logits, repeat(gate_bias[:], SLOTS), ALU.add))
    chain.wait(step)
    stand_alone(dve, c)
    steps = [chain.mark(nc.vector.max(r["top"][:, s, :], r["logits"][:, s, :])) for s in range(SLOTS)]
    for s in range(SLOTS):
        chain.wait(steps[s])
        stand_alone(dve, c)
        step = chain.mark(nc.vector.max_index(r["at"][:, s, :], r["top"][:, s, :], r["logits"][:, s, :]))
    nc.vector.tensor_tensor(r["gap"][:], (r["logits"] if picks == 1 else r["top"])[:],
                            r["top"][:, :, 0:1].to_broadcast(wide), ALU.subtract).then_inc(r["gap_ready"], 1)
    chain.wait(step)
    chain.wait(chain.mark(nc.vector.tensor_copy(r["at_f"][:], r["at"][:])))
    for q in range(picks):
        step = chain.mark(nc.vector.tensor_tensor(r["hot"][q][:], repeat(c["iota8"][:], SLOTS),
                                                  r["at_f"][:, :, q:q + 1].to_broadcast(wide), ALU.is_equal))
    chain.wait(step)
    if picks == 2:
        nc.vector.tensor_tensor(r["any"][:], r["hot"][0][:], r["hot"][1][:], ALU.add).then_inc(r["hot_ready"], 1)
    else:
        nc.vector.tensor_copy(r["any"][:], r["hot"][0][:]).then_inc(r["hot_ready"], 1)
    dve.wait_ge(r["ex_ready"], turn + 1)
    if picks == 1:
        step = chain.mark(nc.vector.reduce_sum(r["den"][:], r["ex"][:], AX.X))
    else:
        step = chain.mark(nc.vector.tensor_scalar_add(r["den"][:], r["ex"][:, :, 1], 1.0))
    chain.wait(step)
    chain.wait(chain.mark(nc.vector.reciprocal(r["den"][:], r["den"][:])))
    stand_alone(dve, c)
    nc.vector.tensor_copy(of_turn(kept["weights"], 0), r["den"][:])
    if picks == 2:
        nc.vector.tensor_tensor(of_turn(kept["weights"], 1), r["den"][:], r["ex"][:, :, 1], ALU.mult)
    dve.wait_ge(r["counted"], turn + 1)
    counts = bank[COUNTS][:, 0:(SLOTS + 1) * EXPERTS].rearrange("p (s e) -> p s e", e=EXPERTS)
    step = chain.mark(nc.vector.tensor_tensor(r["place"][:], counts[:, 0:SLOTS, :], repeat(taken[:], SLOTS), ALU.add))
    chain.wait(step)
    after = chain.mark(nc.vector.tensor_tensor(taken[:], counts[:, SLOTS, :], taken[:], ALU.add))
    steps = [chain.mark(nc.vector.tensor_tensor(r["put"][q][:], r["hot"][q][:], r["place"][:], ALU.mult))
             for q in range(picks)]
    for q in range(picks):
        chain.wait(steps[q])
        step = chain.mark(nc.vector.reduce_sum(of_turn(kept["rows"], q), r["put"][q][:], AX.X))
    chain.wait(step)
    dve.wait_ge(r["rows_free"], LEAD + turn * SLOTS)
    stand_alone(dve, c)
    nc.vector.tensor_copy(r["row_u"][:], kept["rows"][:, bass.ds(turn * SLOTS, SLOTS), :]).then_inc(r["rows_ready"], 1)
    chain.wait(after)


def act_route(nc, act, r, turn):
    act.wait_ge(r["gap_ready"], turn + 1)
    nc.scalar.activation(r["ex"][:], r["gap"][:], ACT.Exp).then_inc(r["ex_ready"], 1)


def pool_scatter(nc, pool, r, c, turn, src, dst):
    pool.wait_ge(r["rows_ready"], LEAD + turn + 1)
    stand_alone(pool, c)
    for s in range(SLOTS):
        for q in range(r["picks"]):
            nc.gpsimd.indirect_dma_start(out=dst, out_offset=bass.IndirectOffsetOnAxis(ap=r["row_u"][:, s, q:q + 1], axis=0),
                                         in_=src[s][:], in_offset=None).then_inc(r["scattered"][s], 16)
    for s in range(SLOTS):
        pool.wait_ge(r["scattered"][s], (turn + 1) * (16 * r["picks"]))
        pool.sem_inc(r["rows_free"], 1)



LINKS1 = 72


def phase_encode(nc, c, d, scr, keep, experts0):
    with Phase(nc) as ctx:
        def sb(name, shape, dt=F32):
            return [ctx.enter_context(nc.sbuf_tensor(f"e_{name}{s}", shape, dt)) for s in range(SLOTS)]

        def sem(name, lead=0):
            return ctx.sem("e_" + name, lead)

        ps = banks(nc, ctx, "e")
        b = attention_buffers(nc, ctx, "e", ps)
        nrm = norm_buffers(nc, ctx, "e", c)
        r = route_buffers(nc, ctx, "e", 2)
        wa = dict(wq=c["a_wq"], wk=c["a_wk"], wv=c["a_wv"], wo=c["a_wo"], bq=c["a_bq"], bk=c["a_bk"], bv=c["a_bv"], bias=c["bias0"], bk_by_group=c["a_bk_by_group"],
                   bias_by_head=True, rope=False, ident=c["ident"], mask_q=c["mask_q"], mask_k=c["mask_k"])
        wx = dict(wq=c["x_wq"], wk=c["x_wk"], wv=c["x_wv"], wo=c["x_wo"], bq=c["x_bq"], bk=c["x_bk"], bv=c["x_bv"], bias=c["window"], bk_by_group=c["x_bk_by_group"],
                   bias_by_head=False, rope=False, ident=c["ident"], mask_q=c["mask_q"], mask_k=c["mask_k"])
        xin, cin = sb("x_in", [P, P]), sb("ctx_in", [P, P])
        x_bo, x_ln2b, x1_b2, x2_bo = sb("x_bo", [P, P]), sb("x_ln2b", [P, P]), sb("x1_b2", [P, P]), sb("x2_bo", [P, P])
        xc = sb("xT_ctxT", [P, 2 * P])
        xT, cT = [t[:, 0:P] for t in xc], [t[:, P:2 * P] for t in xc]
        sub, x1, x1T = sb("sub", [P, P]), sb("x1", [P, P]), sb("x1T", [P, P])
        hid, x2, x2T = sb("hidden", [P, FF1]), sb("x2", [P, P]), sb("x2T", [P, P])
        x3, x3T = sb("x3", [P, P]), sb("x3T", [P, P])

        x_loaded = [sem(f"x_loaded{s}") for s in range(SLOTS)]
        ctx_saved, x3_saved = ([sem(f"{n}{s}", LEAD) for s in range(SLOTS)] for n in ("ctx_saved", "x3_saved"))
        x_transposed, xT_ready, x_summed = sem("x_transposed"), sem("xT_ready"), sem("x_summed")
        x1_ready, x1_transposed, x1T_ready = sem("x1_ready"), sem("x1_transposed"), sem("x1T_ready")
        hidden_done, dense_done = sem("hidden_done"), sem("dense_done")
        hidden_ready = [sem("hidden_ready_even"), sem("hidden_ready_odd")]
        cross_joined = sem("cross_joined", LEAD)
        x2_ready, x2_transposed, x2T_ready = sem("x2_ready", LEAD), sem("x2_transposed"), sem("x2T_ready")
        x3_ready, x3_transposed, x3T_ready = sem("x3_ready"), sem("x3_transposed"), sem("x3T_ready")
        x1_b2_ready, x2_bo_ready = sem("x1_b2_ready"), sem("x2_bo_ready")
        dve_step, buffers_set = sem("dve_step"), sem("buffers_set")
        block = ctx.enter_context(nc.Block())

        @block.sync
        def _(sp):
            give_leads(sp, ctx)
            load_experts(sp, keep, experts0, d, ("m_wgv", "m_wd", "m_bgv", "m_bd"))

            def load(i, s):
                sp.dma_start(xin[s][:], dram_tile(d["x"], i * SLOTS + s)).then_inc(x_loaded[s], 16)
                sp.dma_start(cin[s][:], dram_tile(d["ctx"], i * SLOTS + s)).then_inc(x_loaded[s], 16)

            def turn(i, last):
                for s in range(SLOTS):
                    sp.wait_ge(xT_ready, i * SLOTS + (s + 1))
                    sp.dma_start(dram_tile(scr["ctxT"], i * SLOTS + s), cT[s]).then_inc(ctx_saved[s], 16)
                if not last:
                    for s in range(SLOTS):
                        sp.wait_ge(x_transposed, i * SLOTS + SLOTS)
                        sp.wait_ge(x_summed, i * SLOTS + SLOTS)
                        load(i + 1, s)
                for s in range(SLOTS):
                    sp.wait_ge(x3_ready, i * SLOTS + (s + 1))
                    sp.dma_start(dram_tile(scr["x3"], i * SLOTS + s), x3[s][:]).then_inc(x3_saved[s], 16)

            for s in range(SLOTS):
                load(0, s)
            with sp.Fori(0, TURNS - 1) as i:
                turn(i, False)
            turn(TURNS - 1, True)
            for s in range(SLOTS):
                sp.wait_ge(ctx_saved[s], LEAD + 16 * TURNS)
                sp.wait_ge(x3_saved[s], LEAD + 16 * TURNS)

        @block.tensor
        def _(pe):
            def front(i):
                for s in range(SLOTS):
                    pe.wait_ge(x_loaded[s], i * 32 + 32)
                    nc.tensor.transpose(ps["x"][s][:, 0:P], xin[s][:], c["ident"][:])
                    nc.tensor.transpose(ps["x"][s][:, P:2 * P], cin[s][:], c["ident"][:]).then_inc(x_transposed, 1)
                pe_keys(nc, pe, b, wa, xT, lambda s: pe.wait_ge(xT_ready, i * SLOTS + (s + 1)))
                pe_queries(nc, pe, b, wa, xT, xT, lambda s: pe.wait_ge(cross_joined, LEAD + i * SLOTS))

            def turn(i, last):
                pe_attention(nc, pe, b, wa, i * 2, lambda s: pe.wait_ge(r["rows_ready"], LEAD + i))
                for s in range(SLOTS):
                    pe.wait_ge(x1_ready, i * SLOTS + (s + 1))
                    nc.tensor.transpose(ps["y"][s][:, 0:P], x1[s][:], c["ident"][:]).then_inc(x1_transposed, 1)
                for s in range(SLOTS):
                    pe.wait_ge(x1T_ready, i * SLOTS + (s + 1))
                    for k in range(FF1 // P):
                        step = nc.tensor.matmul(ps["x"][s][:, k * P:(k + 1) * P], lhsT=c["a_w1"][:, k * P:(k + 1) * P],
                                                rhs=x1T[s][:], start=True, stop=True)
                    step.then_inc(hidden_done, 1)
                for s in range(SLOTS):
                    pe.wait_ge(hidden_ready[s % 2], i * (SLOTS // 2) + (s // 2 + 1))
                    for k in range(FF1 // P):
                        step = nc.tensor.matmul(ps["y"][s][:, P:2 * P], lhsT=hid[s][:, k * P:(k + 1) * P],
                                                rhs=c["a_w2"][:, k, :], start=k == 0, stop=k == FF1 // P - 1)
                    step.then_inc(dense_done, 1)
                pe_keys(nc, pe, b, wx, cT, lambda s: None)
                for s in range(SLOTS):
                    pe.wait_ge(x2_ready, LEAD + i * SLOTS + (s + 1))
                    nc.tensor.transpose(ps["y"][s][:, 0:P], x2[s][:], c["ident"][:]).then_inc(x2_transposed, 1)
                pe_queries(nc, pe, b, wx, [t[:] for t in x2T], cT, lambda s: pe.wait_ge(x2T_ready, i * SLOTS + (s + 1)))
                pe_attention(nc, pe, b, wx, i * 2 + 1)
                if not last:
                    front(i + 1)
                for s in range(SLOTS):
                    pe.wait_ge(x3_ready, i * SLOTS + (s + 1))
                    if not last:
                        pe.wait_ge(b["k_ready"], (i * 2 + 2) * SLOTS + (s + 1))
                    nc.tensor.transpose(ps["x"][s][:, 0:P], x3[s][:], c["ident"][:]).then_inc(x3_transposed, 1)
                pe_logits(nc, pe, r, ps["x"], x3T, c["gate0"], lambda s: pe.wait_ge(x3T_ready, i * SLOTS + (s + 1)))
                pe_count(nc, pe, r, c, ps["x"], i)

            pe.wait_ge(buffers_set, 1)
            front(0)
            with pe.Fori(0, TURNS - 1) as i:
                turn(i, False)
            turn(TURNS - 1, True)

        @block.scalar
        def _(act):
            def front(i):
                for s in range(SLOTS):
                    act.wait_ge(x_transposed, i * SLOTS + (s + 1))
                    act.wait_ge(ctx_saved[s], LEAD + i * 16)
                    nc.scalar.activation(xc[s][:], ps["x"][s][:, 0:2 * P], ACT.Copy).then_inc(xT_ready, 1)
                act_keys(nc, act, b, wa, i * 2)

            def turn(i, last):
                act_attention(nc, act, b, i * 2)
                for s in range(SLOTS):
                    act.wait_ge(x1_transposed, i * SLOTS + (s + 1))
                    nc.scalar.activation(x1T[s][:], ps["y"][s][:, 0:P], ACT.Copy).then_inc(x1T_ready, 1)
                for s in range(0, SLOTS, 2):
                    act.wait_ge(hidden_done, i * SLOTS + (s + 1))
                    for k in range(FF1 // P):
                        step = nc.scalar.activation(hid[s][:, k * P:(k + 1) * P], ps["x"][s][:, k * P:(k + 1) * P],
                                                    ACT.Relu, bias=c["a_b1"][:, k:k + 1])
                    step.then_inc(hidden_ready[0], 1)
                act_keys(nc, act, b, wx, i * 2 + 1)
                for s in range(SLOTS):
                    act.wait_ge(x2_transposed, i * SLOTS + (s + 1))
                    nc.scalar.activation(x2T[s][:], ps["y"][s][:, 0:P], ACT.Copy).then_inc(x2T_ready, 1)
                act_attention(nc, act, b, i * 2 + 1)
                if not last:
                    front(i + 1)
                for s in range(SLOTS):
                    act.wait_ge(x3_transposed, i * SLOTS + (s + 1))
                    nc.scalar.activation(x3T[s][:], ps["x"][s][:, 0:P], ACT.Copy).then_inc(x3T_ready, 1)
                act_route(nc, act, r, i)

            front(0)
            with act.Fori(0, TURNS - 1) as i:
                turn(i, False)
            turn(TURNS - 1, True)

        @block.gpsimd
        def _(pool):
            with pool.Fori(0, TURNS) as i:
                for s in range(SLOTS):
                    pool.wait_ge(x_loaded[s], i * 32 + 32)
                    nc.gpsimd.tensor_tensor(x_bo[s][:], xin[s][:], c["a_bo"][:], ALU.add)
                    nc.gpsimd.tensor_tensor(x_ln2b[s][:], xin[s][:], c["ln2_b"][:], ALU.add).then_inc(x_summed, 1)
                pool_norm(nc, pool, nrm, c, i * 4)
                for s in range(SLOTS):
                    pool.wait_ge(x1_ready, i * SLOTS + (s + 1))
                    nc.gpsimd.tensor_tensor(x1_b2[s][:], x1[s][:], c["a_b2"][:], ALU.add).then_inc(x1_b2_ready, 1)
                pool_norm(nc, pool, nrm, c, i * 4 + 1)
                pool_norm(nc, pool, nrm, c, i * 4 + 2)
                for s in range(SLOTS):
                    pool.wait_ge(x2_ready, LEAD + i * SLOTS + (s + 1))
                    nc.gpsimd.tensor_tensor(x2_bo[s][:], x2[s][:], c["x_bo"][:], ALU.add).then_inc(x2_bo_ready, 1)
                pool_norm(nc, pool, nrm, c, i * 4 + 3)
                pool_scatter(nc, pool, r, c, i, x3, scr["sorted0"])

        @block.vector
        def _(dve):
            for s in range(SLOTS):
                nc.vector.memset(b["va"][s][:], 0.0)
            nc.vector.tensor_copy(keep["route0"]["taken"][:], c["row_base"][:]).then_inc(buffers_set, 1)
            dve.wait_ge(buffers_set, 1)
            for s in range(SLOTS):
                last = nc.vector.memset(b["va"][s][:, :, DH:DH + 1], 1.0)
            last.then_inc(buffers_set, 1)
            dve.wait_ge(buffers_set, 2)
            def join(i, products, residual, joined, done, mark):
                steps = []
                for s in range(SLOTS):
                    dve.wait_ge(products, done + (s + 1))
                    dve.wait_ge(joined, i * SLOTS + (s + 1))
                    steps.append(mark(s, nc.vector.tensor_tensor(sub[s][:], ps["y"][s][:, P:2 * P], residual[s][:], ALU.add)))
                return steps

            def turn(i, last):
                chain = Chain(dve, dve_step, i, LINKS1)
                sub_all = [t[:] for t in sub]
                dve_attention(nc, dve, b, wa, i * 2, chain)
                step = join(i, b["attn_done"], x_bo, x_summed, i * (2 * SLOTS), lambda s, ins: chain.mark(ins))
                dve_norm(nc, dve, nrm, chain, i * 4, sub_all, step, [t[:] for t in x1],
                         (c["ln1_g"], [c["ln1_b"][:]] * SLOTS), done=(x1_ready, i, 0))
                for s in range(1, SLOTS, 2):
                    dve.wait_ge(hidden_done, i * SLOTS + (s + 1))
                    for k in range(FF1 // P):
                        step = nc.vector.tensor_scalar(hid[s][:, k * P:(k + 1) * P], ps["x"][s][:, k * P:(k + 1) * P],
                                                       c["a_b1"][:, k:k + 1], 0.0, ALU.add, ALU.max)
                    step.then_inc(hidden_ready[1], 1)
                step = join(i, dense_done, x1_b2, x1_b2_ready, i * SLOTS, lambda s, ins: chain.mark(ins))
                step = dve_norm(nc, dve, nrm, chain, i * 4 + 1, sub_all, step, sub_all, (c["ln2_g"], [t[:] for t in x_ln2b]))
                dve_norm(nc, dve, nrm, chain, i * 4 + 2, sub_all, step, [t[:] for t in x2], done=(x2_ready, i, LEAD))
                dve_queries(nc, dve, b, wx, i * 2 + 1, chain)
                dve_attention(nc, dve, b, wx, i * 2 + 1, chain)

                def joined(s, ins):
                    ins.then_inc(cross_joined, 1)
                    return cross_joined, LEAD + i * SLOTS + (s + 1)
                step = join(i, b["attn_done"], x2_bo, x2_bo_ready, i * (2 * SLOTS) + SLOTS, joined)

                def x3_free(s):
                    dve.wait_ge(x3_saved[s], LEAD + i * 16)
                    dve.wait_ge(r["rows_free"], LEAD + i * SLOTS)
                dve_norm(nc, dve, nrm, chain, i * 4 + 3, sub_all, step, [t[:] for t in x3],
                         free=x3_free, done=(x3_ready, i, 0))
                if not last:
                    dve_queries(nc, dve, b, wa, i * 2 + 2, chain)
                dve_route(nc, dve, r, c, chain, i, ps["x"], None, keep["route0"])
                chain.close()

            dve_queries(nc, dve, b, wa, 0, None)
            with dve.Fori(0, TURNS - 1) as i:
                turn(i, False)
            turn(TURNS - 1, True)



def phase_table(nc, c, kept, tag, sorted_rows):
    with Phase(nc) as ctx:
        def sb(name, shape, dt=F32):
            return ctx.enter_context(nc.sbuf_tensor(f"{tag}_{name}", shape, dt))

        def sem(name, lead=0):
            return ctx.sem(f"{tag}_{name}", lead)

        tiles, picks = kept["tiles"], kept["picks"]
        need_f, need_i, need = sb("need_f", [P, EXPERTS]), sb("need_i", [P, EXPERTS], I32), sb("need", [P, EXPERTS])
        pad_f, pad = sb("pad_f", [P, EXPERTS]), sb("pad", [P, EXPERTS], U32)
        end, last = sb("end", [P, EXPERTS]), sb("last", [P, 1])
        tile, past = sb("tile", [P, tiles]), sb("past", [P, tiles, EXPERTS])
        weighed, expert, first = sb("weighed", [P, tiles, EXPERTS]), sb("expert", [P, tiles]), sb("first", [P, tiles])
        row = sb("row", [P, tiles])
        shift, jump = sb("shift", [P, EXPERTS]), sb("jump", [P, EXPERTS])
        n_rows = BATCH * picks
        over, moved, out_f = sb("over", [P, n_rows, EXPERTS]), sb("moved", [P, n_rows]), sb("out_f", [P, n_rows])
        pad_ready, padded, step_sem = sem("pad_ready"), sem("padded"), sem("step")
        block = ctx.enter_context(nc.Block())

        @block.vector
        def _(dve):
            count = [0]

            def step(ins):
                ins.then_inc(step_sem, 1)
                count[0] += 1
                dve.wait_ge(step_sem, count[0])

            ones = c["one_row"][:, 0:EXPERTS]
            step(nc.vector.tensor_scalar(pad_f[:], kept["taken"][:], c["part_iota"][:], None, ALU.add))
            nc.vector.tensor_copy(pad[:], pad_f[:]).then_inc(pad_ready, 1)
            step(nc.vector.tensor_tensor(need_f[:], kept["taken"][:], c["row_base"][:], ALU.subtract))
            step(nc.vector.tensor_scalar_add(need_f[:], need_f[:], float(P - 1)))
            step(nc.vector.tensor_copy(need_i[:], need_f[:]))
            step(nc.vector.tensor_scalar(need_i[:], need_i[:], 7, None, ALU.arith_shift_right))
            step(nc.vector.tensor_copy(need[:], need_i[:]))
            step(nc.vector.tensor_tensor_scan(end[:], ones, need[:], 0.0, ALU.mult, ALU.add))
            step(nc.vector.tensor_scalar_add(last[:], end[:, EXPERTS - 1:EXPERTS], -1.0))
            step(nc.vector.tensor_scalar(tile[:], c["iota_tiles"][:, 0:tiles], last[:], None, ALU.min))
            step(nc.vector.tensor_tensor(past[:], bcast(tile[:], EXPERTS), repeat(end[:], tiles), ALU.is_ge))
            step(nc.vector.reduce_sum(expert[:], past[:], AX.X))
            step(nc.vector.tensor_tensor(weighed[:], past[:], repeat(need[:], tiles), ALU.mult))
            step(nc.vector.reduce_sum(first[:], weighed[:], AX.X))
            step(nc.vector.tensor_tensor(tile[:], tile[:], first[:], ALU.subtract))
            step(nc.vector.tensor_scalar_mul(row[:], expert[:], float(REGION)))
            step(nc.vector.scalar_tensor_tensor(out=row[:], in0=tile[:], scalar=float(P), in1=row[:],
                                                op0=ALU.mult, op1=ALU.add))
            nc.vector.tensor_copy(kept["tile_expert"][:], expert[:])
            nc.vector.tensor_copy(kept["tile_row"][:], row[:])
            step(nc.vector.tensor_tensor(shift[:], end[:], need[:], ALU.subtract))
            step(nc.vector.scalar_tensor_tensor(out=shift[:], in0=shift[:], scalar=float(P), in1=c["row_base"][:],
                                                op0=ALU.mult, op1=ALU.subtract))
            nc.vector.tensor_copy(jump[:, 0:1], shift[:, 0:1])
            step(nc.vector.tensor_tensor(jump[:, 1:EXPERTS], shift[:, 1:EXPERTS], shift[:, 0:EXPERTS - 1], ALU.subtract))
            rows = kept["rows"][:, 0:BATCH, :].rearrange("p n k -> p (n k)")
            step(nc.vector.tensor_tensor(over[:], bcast(rows, EXPERTS), repeat(c["row_base"][:], n_rows), ALU.is_ge))
            step(nc.vector.tensor_tensor(over[:], over[:], repeat(jump[:], n_rows), ALU.mult))
            step(nc.vector.reduce_sum(moved[:], over[:], AX.X))
            step(nc.vector.tensor_tensor(out_f[:], moved[:], rows, ALU.add))
            nc.vector.memset(kept["weights"][:, BATCH:, :], 0.0)
            nc.vector.memset(kept["out_rows"][:, BATCH:, :], 0)
            step(nc.vector.tensor_copy(kept["out_rows"][:, 0:BATCH, :].rearrange("p n k -> p (n k)"), out_f[:]))

        @block.gpsimd
        def _(pool):
            pool.wait_ge(pad_ready, 1)
            for e in range(EXPERTS):
                nc.gpsimd.indirect_dma_start(out=sorted_rows, out_offset=bass.IndirectOffsetOnAxis(ap=pad[:, e:e + 1], axis=0),
                                             in_=c["zeros"][:], in_offset=None).then_inc(padded, 16)
            pool.wait_ge(padded, 16 * EXPERTS)



def expert_buffers(nc, ctx, tag, down):
    def sb(name, shape):
        return ctx.enter_context(nc.sbuf_tensor(name + tag, shape, F32))
    return dict(up=sb("up", [P, EXPERTS, FF1]), up_b=sb("up_b", [P, EXPERTS, FF1]),
                 down=sb("down", [P, EXPERTS, down, P]), down_b=sb("down_b", [P, EXPERTS, P]))


def load_experts(sp, keep, e, d, names):
    up, down, up_b, down_b = names
    sp.dma_start(e["up"][:], d[up]).then_inc(keep["experts_loaded"], 16)
    sp.dma_start(e["down"][:], d[down]).then_inc(keep["experts_loaded"], 16)
    sp.dma_start(e["up_b"][:], d[up_b].partition_broadcast(P)).then_inc(keep["experts_loaded"], 16)
    sp.dma_start(e["down_b"][:], d[down_b].partition_broadcast(P)).then_inc(keep["experts_loaded"], 16)


def phase_experts(nc, c, keep, kept, e, tag, gated, sorted_rows, out_rows, loaded):
    with Phase(nc) as ctx:
        def sb(name, shape, dt=F32):
            return [ctx.enter_context(nc.sbuf_tensor(f"{tag}_{name}{s}", shape, dt)) for s in range(SLOTS)]

        def sem(name, lead=0):
            return ctx.sem(f"{tag}_{name}", lead)

        wide = [ctx.enter_context(nc.psum_tensor(f"{tag}_wide{s}", [P, FF1], F32)) for s in range(SLOTS)]
        turned_rows, sums = ([ctx.enter_context(nc.psum_tensor(f"{tag}_{name}{s}", [P, 512], F32)) for s in range(2)]
                             for name in ("turned_rows", "sums"))
        hidden = FF0 if gated else FF1
        blocks = hidden // P
        rows, rowsT, pre, h, hT, y = (sb("rows", [P, P]), sb("rowsT", [P, P]), sb("pre", [P, FF1]), sb("h", [P, FF1]),
                                      sb("hT", [P, hidden]), sb("y", [P, P]))
        rows_loaded, y_saved = [sem(f"rows_loaded{s}") for s in range(SLOTS)], [sem(f"y_saved{s}", LEAD) for s in range(SLOTS)]
        rows_transposed, rowsT_ready, up_done, pre_ready = (sem("rows_transposed"), sem("rowsT_ready"), sem("up_done"),
                                                            sem("pre_ready"))
        act_ready, h_ready, h_transposed, hT_ready = sem("act_ready"), sem("h_ready"), sem("h_transposed"), sem("hT_ready")
        down_done, y_ready = sem("down_done"), sem("y_ready", LEAD)
        tiles = kept["tiles"]
        last_turn = tiles // SLOTS - 1
        block = ctx.enter_context(nc.Block())

        def experts_of(eng, i, turns, part):
            values = []
            for k in range(turns):
                registers = [eng.alloc_register(f"{tag}_{part}_expert{k}_{s}") for s in range(SLOTS)]
                eng.load(registers, kept["tile_expert"][0:1, bass.ds(i * SLOTS + k * SLOTS, SLOTS)])
                values += [eng.snap(r, donate=True).with_bounds(min_val=0, max_val=EXPERTS - 1) for r in registers]
            return values

        @block.sync
        def _(sp):
            give_leads(sp, ctx)

            def load(i, k):
                if not (isinstance(i, int) and i * SLOTS + k < SLOTS):
                    sp.wait_ge(rows_transposed, i * SLOTS + (k - SLOTS + 1))
                row = sp.value_load(kept["tile_row"][0:1, bass.ds(i * SLOTS + k, 1)], min_val=0,
                                    max_val=EXPERTS * REGION - P)
                sp.dma_start(rows[k % SLOTS][:], sorted_rows[bass.ds(row, P), :]).then_inc(rows_loaded[k % SLOTS], 16)

            def store(i, k):
                sp.wait_ge(y_ready, LEAD + i * SLOTS + (k + 1))
                sp.dma_start(out_rows[bass.ds((i * SLOTS + k) * P, P), :], y[k % SLOTS][:]).then_inc(y_saved[k % SLOTS], 16)

            for k in range(SLOTS + 3):
                load(0, k)
            with sp.Fori(0, last_turn - 1) as i:
                for k in range(SLOTS):
                    load(i, k + SLOTS + 3)
                    store(i, k)
            load(last_turn - 1, SLOTS + 3)
            for k in range(2 * SLOTS):
                store(last_turn - 1, k)
            for s in range(SLOTS):
                sp.wait_ge(y_saved[s], LEAD + 16 * (last_turn + 1))

        @block.tensor
        def _(pe):
            def turned(i, k):
                pe.wait_ge(rows_loaded[k % SLOTS], (i + k // SLOTS) * 16 + 16)
                nc.tensor.transpose(turned_rows[k % 2][:, 0:P], rows[k % SLOTS][:], c["ident"][:]).then_inc(rows_transposed, 1)

            def up(i, k, experts):
                pe.wait_ge(rowsT_ready, i * SLOTS + (k + 1))
                nc.tensor.matmul(wide[k % SLOTS][:], lhsT=rowsT[k % SLOTS][:], rhs=tile_of(e["up"], experts[k]),
                                 start=True, stop=True).then_inc(up_done, 1)

            def hidden_turned(i, k):
                pe.wait_ge(h_ready, i * SLOTS + (k + 1))
                for n in range(blocks):
                    last = nc.tensor.transpose(wide[k % SLOTS][:, n * P:(n + 1) * P], h[k % SLOTS][:, n * P:(n + 1) * P],
                                               c["ident"][:])
                last.then_inc(h_transposed, 1)

            def down(i, k, experts):
                pe.wait_ge(hT_ready, i * SLOTS + (k + 1))
                pe.wait_ge(y_ready, LEAD + i * SLOTS + max(k - 1, 0))
                for n in range(blocks):
                    last = nc.tensor.matmul(
                        sums[k % 2][:, 0:P], lhsT=hT[k % SLOTS][:, n * P:(n + 1) * P],
                        rhs=e["down"][:, bass.ds(experts[k], 1), n, :].rearrange("p o n -> p (o n)"),
                        start=n == 0, stop=n == blocks - 1)
                last.then_inc(down_done, 1)

            pe.wait_ge(keep["experts_loaded"], loaded)
            experts = experts_of(pe, 0, 1, "first")
            turned(0, 0)
            turned(0, 1)
            up(0, 0, experts)
            turned(0, 2)
            up(0, 1, experts)
            turned(0, 3)
            hidden_turned(0, 0)
            with pe.Fori(0, last_turn) as i:
                experts = experts_of(pe, i, 2, "middle")
                for k in range(2, SLOTS + 2):
                    up(i, k, experts)
                    turned(i, k + 2)
                    hidden_turned(i, k - 1)
                    down(i, k - 2, experts)
            experts = experts_of(pe, last_turn, 1, "last")
            up(last_turn, 2, experts)
            hidden_turned(last_turn, 1)
            down(last_turn, 0, experts)
            up(last_turn, 3, experts)
            hidden_turned(last_turn, 2)
            down(last_turn, 1, experts)
            hidden_turned(last_turn, 3)
            down(last_turn, 2, experts)
            down(last_turn, 3, experts)

        @block.vector
        def _(dve):
            def rows_kept(i, k):
                dve.wait_ge(rows_transposed, i * SLOTS + (k + 1))
                nc.vector.tensor_copy(rowsT[k % SLOTS][:], turned_rows[k % 2][:, 0:P]).then_inc(rowsT_ready, 1)

            def biased(i, k, experts):
                dve.wait_ge(up_done, i * SLOTS + (k + 1))
                nc.vector.tensor_tensor(pre[k % SLOTS][:], wide[k % SLOTS][:], tile_of(e["up_b"], experts[k]), ALU.add)\
                    .then_inc(pre_ready, 1)

            def gated_by(i, k):
                if gated:
                    dve.wait_ge(act_ready, i * SLOTS + (k + 1))
                    nc.vector.tensor_tensor(h[k % SLOTS][:, 0:FF0], h[k % SLOTS][:, 0:FF0], pre[k % SLOTS][:, FF0:2 * FF0],
                                            ALU.mult).then_inc(h_ready, 1)

            def hidden_kept(i, k):
                dve.wait_ge(h_transposed, i * SLOTS + (k + 1))
                nc.vector.tensor_copy(hT[k % SLOTS][:], wide[k % SLOTS][:, 0:hidden]).then_inc(hT_ready, 1)

            def output(i, k, experts):
                dve.wait_ge(down_done, i * SLOTS + (k + 1))
                dve.wait_ge(y_saved[k % SLOTS], LEAD + (i + k // SLOTS) * 16)
                nc.vector.tensor_tensor(y[k % SLOTS][:], sums[k % 2][:, 0:P], tile_of(e["down_b"], experts[k]), ALU.add)\
                    .then_inc(y_ready, 1)

            experts = experts_of(dve, 0, 1, "first")
            rows_kept(0, 0)
            rows_kept(0, 1)
            biased(0, 0, experts)
            rows_kept(0, 2)
            gated_by(0, 0)
            biased(0, 1, experts)
            rows_kept(0, 3)
            hidden_kept(0, 0)
            with dve.Fori(0, last_turn) as i:
                experts = experts_of(dve, i, 2, "middle")
                for k in range(2, SLOTS + 2):
                    gated_by(i, k - 1)
                    biased(i, k, experts)
                    rows_kept(i, k + 2)
                    hidden_kept(i, k - 1)
                    output(i, k - 2, experts)
            experts = experts_of(dve, last_turn, 1, "last")
            gated_by(last_turn, 1)
            biased(last_turn, 2, experts)
            hidden_kept(last_turn, 1)
            output(last_turn, 0, experts)
            gated_by(last_turn, 2)
            biased(last_turn, 3, experts)
            hidden_kept(last_turn, 2)
            output(last_turn, 1, experts)
            gated_by(last_turn, 3)
            hidden_kept(last_turn, 3)
            output(last_turn, 2, experts)
            output(last_turn, 3, experts)

        @block.scalar
        def _(act):
            with act.Fori(0, last_turn + 1) as i:
                for s in range(SLOTS):
                    act.wait_ge(pre_ready, i * SLOTS + (s + 1))
                    if gated:
                        nc.scalar.activation(h[s][:, 0:FF0], pre[s][:, 0:FF0], ACT.Silu).then_inc(act_ready, 1)
                    else:
                        nc.scalar.activation(h[s][:], pre[s][:], ACT.Gelu_apprx_tanh).then_inc(h_ready, 1)



def gather_buffers(nc, ctx, tag, picks):
    def sb(name, shape, dt=F32):
        return [ctx.enter_context(nc.sbuf_tensor(f"{tag}_{name}{s}", shape, dt)) for s in range(SLOTS)]
    return dict(picks=picks, rows=sb("g_rows", [P, picks], U32), weights=sb("g_weights", [P, picks]),
                 y=[sb(f"g_y{q}", [P, P]) for q in range(picks)],
                 rows_ready=ctx.sem(f"{tag}_g_rows_ready"),
                 gathered=[ctx.sem(f"{tag}_g_gathered{s}") for s in range(SLOTS)])


def pool_gather(nc, pool, g, c, kept, turn, src):
    for s in range(SLOTS):
        nc.gpsimd.tensor_copy(g["weights"][s][:], tile_of(kept["weights"], turn * SLOTS + s))
        nc.gpsimd.tensor_copy(g["rows"][s][:], tile_of(kept["out_rows"], turn * SLOTS + s)).then_inc(g["rows_ready"], 1)
    pool.wait_ge(g["rows_ready"], turn * SLOTS + SLOTS)
    stand_alone(pool, c)
    for s in range(SLOTS):
        for q in range(g["picks"]):
            nc.gpsimd.indirect_dma_start(out=g["y"][q][s][:], out_offset=None, in_=src,
                                         in_offset=bass.IndirectOffsetOnAxis(ap=g["rows"][s][:, q:q + 1], axis=0))\
                .then_inc(g["gathered"][s], 16)



LINKS3 = 40


def phase_decode(nc, c, d, keep, scr, xT_all, experts1):
    with Phase(nc) as ctx:
        def sb(name, shape, dt=F32):
            return [ctx.enter_context(nc.sbuf_tensor(f"d_{name}{s}", shape, dt)) for s in range(SLOTS)]

        def sem(name, lead=0):
            return ctx.sem("d_" + name, lead)

        ps = banks(nc, ctx, "d")
        b = attention_buffers(nc, ctx, "d", ps)
        nrm = norm_buffers(nc, ctx, "d", c)
        g = gather_buffers(nc, ctx, "d", 2)
        w = dict(wq=c["l_wq"], wqp=c["l_wqp"], wk=c["l_wk"], wkp=c["l_wkp"], wv=c["l_wv"], wo=c["l_wo"], bias=c["causal"], bk_by_group=c["zeros"],
                  bias_by_head=False, rope=True, ident=c["ident"], mask_q=c["mask_q"], mask_k=c["mask_k"],
                  cos=c["cos"], sin=c["sin"])
        x3, sub, x4, x4T, x5 = sb("x3", [P, P]), sb("sub", [P, P]), sb("x4", [P, P]), sb("x4T", [P, P]), sb("x5", [P, P])
        x3_loaded = [sem(f"x3_loaded{s}") for s in range(SLOTS)]
        joined, x4_ready, x4_transposed, x4T_ready = sem("joined", LEAD), sem("x4_ready"), sem("x4_transposed"), sem("x4T_ready")
        x5_ready, x5_transposed, x5T_ready = sem("x5_ready", LEAD), sem("x5_transposed"), sem("x5T_ready")
        dve_step, buffers_set = sem("dve_step"), sem("buffers_set")
        block = ctx.enter_context(nc.Block())

        @block.sync
        def _(sp):
            give_leads(sp, ctx)
            load_experts(sp, keep, experts1, d, ("s_w1", "s_w2", "s_b1", "s_b2"))
            with sp.Fori(0, TURNS) as i:
                for s in range(SLOTS):
                    sp.wait_ge(joined, LEAD + i * SLOTS)
                    sp.dma_start(x3[s][:], dram_tile(scr["x3"], i * SLOTS + s)).then_inc(x3_loaded[s], 16)

        @block.gpsimd
        def _(pool):
            pool_gather(nc, pool, g, c, keep["route0"], 0, scr["expert_out0"])
            with pool.Fori(0, TURNS) as i:
                pool.wait_ge(joined, LEAD + i * SLOTS + SLOTS)
                stand_alone(pool, c)
                pool_norm(nc, pool, nrm, c, i * 2)
                pool_gather(nc, pool, g, c, keep["route0"], i + 1, scr["expert_out0"])
                pool_norm(nc, pool, nrm, c, i * 2 + 1)
            for s in range(SLOTS):
                pool.wait_ge(g["gathered"][s], 32 * (TURNS + 1))

        @block.tensor
        def _(pe):
            pe.wait_ge(buffers_set, 2)
            with pe.Fori(0, TURNS) as i:
                for s in range(SLOTS):
                    pe.wait_ge(x4_ready, i * SLOTS + (s + 1))
                    nc.tensor.transpose(ps["y"][s][:, 0:P], x4[s][:], c["ident"][:]).then_inc(x4_transposed, 1)

                def self_ready(s):
                    pe.wait_ge(x4T_ready, i * SLOTS + (s + 1))
                pe_queries(nc, pe, b, w, [t[:] for t in x4T], [t[:] for t in x4T], self_ready)
                pe_attention(nc, pe, b, w, i)
                for s in range(SLOTS):
                    pe.wait_ge(x5_ready, LEAD + i * SLOTS + (s + 1))
                    nc.tensor.transpose(ps["x"][s][:, 0:P], x5[s][:], c["ident"][:]).then_inc(x5_transposed, 1)

        @block.scalar
        def _(act):
            with act.Fori(0, TURNS) as i:
                for s in range(SLOTS):
                    act.wait_ge(x4_transposed, i * SLOTS + (s + 1))
                    nc.scalar.activation(x4T[s][:], ps["y"][s][:, 0:P], ACT.Copy).then_inc(x4T_ready, 1)
                act_keys(nc, act, b, w, i)
                act_attention(nc, act, b, i)
                for s in range(SLOTS):
                    act.wait_ge(x5_transposed, i * SLOTS + (s + 1))
                    nc.scalar.activation(tile_of(xT_all, i * SLOTS + s), ps["x"][s][:, 0:P], ACT.Copy).then_inc(x5T_ready, 1)
            act.wait_ge(x5T_ready, 2 * TURNS)

        @block.vector
        def _(dve):
            for s in range(SLOTS):
                last = nc.vector.memset(b["va"][s][:], 0.0)
            last.then_inc(buffers_set, 1)
            dve.wait_ge(buffers_set, 1)
            for s in range(SLOTS):
                last = nc.vector.memset(b["va"][s][:, :, DH:DH + 1], 1.0)
            last.then_inc(buffers_set, 1)
            with dve.Fori(0, TURNS) as i:
                chain = Chain(dve, dve_step, i, LINKS3)
                step = [None] * SLOTS
                for s in range(SLOTS):
                    dve.wait_ge(x3_loaded[s], i * 16 + 16)
                    dve.wait_ge(x5_ready, LEAD + i * SLOTS)
                    dve.wait_ge(g["gathered"][s], i * 32 + 32)
                    step[s] = chain.mark(nc.vector.scalar_tensor_tensor(
                        out=sub[s][:], in0=g["y"][0][s][:], scalar=g["weights"][s][:, 0:1], in1=x3[s][:], op0=ALU.mult, op1=ALU.add))
                for s in range(SLOTS):
                    chain.wait(step[s])
                    nc.vector.scalar_tensor_tensor(
                        out=sub[s][:], in0=g["y"][1][s][:], scalar=g["weights"][s][:, 1:2], in1=sub[s][:],
                        op0=ALU.mult, op1=ALU.add).then_inc(joined, 1)
                    step[s] = (joined, LEAD + i * SLOTS + (s + 1))
                x4_step = dve_norm(nc, dve, nrm, chain, i * 2, [t[:] for t in sub], step, [t[:] for t in x4],
                                   done=(x4_ready, i, 0))
                dve_queries(nc, dve, b, w, i, chain)
                dve_attention(nc, dve, b, w, i, chain)
                dve.wait_ge(b["attn_done"], i * SLOTS + SLOTS)
                for s in range(SLOTS):
                    chain.wait(x4_step[s])
                    step[s] = chain.mark(nc.vector.tensor_tensor(sub[s][:], ps["y"][s][:, P:2 * P], x4[s][:], ALU.add))
                for s in range(SLOTS):
                    chain.wait(step[s])
                    step[s] = chain.mark(nc.vector.tensor_tensor(sub[s][:], sub[s][:], c["l_bo"][:], ALU.add))
                dve_norm(nc, dve, nrm, chain, i * 2 + 1, [t[:] for t in sub], step, [t[:] for t in x5],
                         done=(x5_ready, i, LEAD))
                chain.close()



CHUNK = 4
CHUNKS = BATCH // CHUNK


def phase_recurrent(nc, c, d, scr, xT_all, states):
    with Phase(nc) as ctx:
        def sb(name, shape, dt=F32):
            return ctx.enter_context(nc.sbuf_tensor("n_" + name, shape, dt))

        def sem(name, lead=0):
            return ctx.sem("n_" + name, lead)

        gates, drive = sb("gates", [P, P, BATCH]), sb("drive", [P, P, BATCH])
        wi, wg, wa, wb = (sb(n, [P, P]) for n in ("wi", "wg", "wa", "wb"))
        bi, bg, decay = (sb(n, [P, 1]) for n in ("bi", "bg", "decay"))
        cin = [sb(f"ctx{k}", [P, CHUNK, P]) for k in range(2)]
        kv, mem, kept, inp, gate, part, blend = ([sb(f"{n}{k}", [P, CHUNK * P]) for k in range(2)]
                                                 for n in ("kv", "mem", "kept", "inp", "gate", "part", "blend"))
        gated = [sb(f"gated{k}", [P, BATCH]) for k in range(2)]
        pi, pg, pc = ([ctx.enter_context(nc.psum_tensor(f"n_{n}{k}", [P, 512], F32)) for k in range(2)]
                      for n in ("pi", "pg", "pc"))
        pz = [ctx.enter_context(nc.psum_tensor(f"n_pz{k}", [P, 512], F32)) for k in range(2)]
        w_loaded, ctx_loaded = sem("w_loaded"), [sem(f"ctx_loaded{s}") for s in range(SLOTS)]
        squared, scanned, kept_ready, inp_done, inp_ready = (sem(n) for n in ("squared", "scanned", "kept_ready",
                                                                              "inp_done", "inp_ready"))
        gate_done, gate_ready, part_ready, blend_ready, drive_done, drive_ready = (
            sem(n) for n in ("gate_done", "gate_ready", "part_ready", "blend_ready", "drive_done", "drive_ready"))
        gated_ready, summed, state_ready, gates_kept = (sem("gated_ready"), sem("summed"), sem("state_ready", LEAD),
                                                        sem("gates_kept"))
        block = ctx.enter_context(nc.Block())
        WEIGHTS = ((wi, "n_wi"), (wg, "n_wg"), (wa, "n_a"), (wb, "n_b"))
        COLUMNS = ((bi, "n_bi"), (bg, "n_bg"), (decay, "n_decay"))

        def of_chunk(big, k):
            return big[:, :, k * CHUNK:(k + 1) * CHUNK].rearrange("p t b -> p b t")

        @block.sync
        def _(sp):
            give_leads(sp, ctx)
            for tile, name in WEIGHTS:
                sp.dma_start(tile[:], d[name]).then_inc(w_loaded, 16)
            for tile, name in COLUMNS:
                sp.dma_start(tile[:], d[name].rearrange("(p o) -> p o", o=1)).then_inc(w_loaded, 16)
            for k in range(CHUNKS):
                if k >= 2:
                    sp.wait_ge(squared, k - 1)
                sp.dma_start(cin[k % 2][:], scr["ctxT"][k * CHUNK:(k + 1) * CHUNK].rearrange("b p t -> p b t"))\
                    .then_inc(ctx_loaded[k % 2], 16)

        @block.vector
        def _(dve):
            nc.vector.memset(gated[0][:], 0.0).then_inc(gated_ready, 1)
            dve.wait_ge(w_loaded, 16 * 7)

            def memory(k):
                dve.wait_ge(ctx_loaded[k % 2], 16 * (k // 2 + 1))
                flat = cin[k % 2][:].rearrange("p b t -> p (b t)")
                nc.vector.tensor_tensor(kv[k % 2][:], flat, flat, ALU.mult).then_inc(squared, 1)
                dve.wait_ge(squared, k + 1)
                for q in range(CHUNK):
                    last = nc.vector.tensor_tensor_scan(mem[k % 2][:, q * P:(q + 1) * P],
                                                        decay[:].to_broadcast([P, P]),
                                                        kv[k % 2][:, q * P:(q + 1) * P], 0.0, ALU.mult, ALU.add)
                last.then_inc(scanned, 1)
                dve.wait_ge(scanned, k + 1)
                if k >= 2:
                    dve.wait_ge(inp_done, k - 1)
                nc.vector.tensor_tensor(kept[k % 2][:], mem[k % 2][:],
                                        xT_all[:, k * CHUNK:(k + 1) * CHUNK, :].rearrange("p b t -> p (b t)"),
                                        ALU.mult).then_inc(kept_ready, 1)

            def blended(k):
                dve.wait_ge(gate_ready, k + 1)
                if k >= 2:
                    dve.wait_ge(drive_done, k - 1)
                nc.vector.tensor_copy(of_chunk(gates, k), gate[k % 2][:].rearrange("p (b t) -> p b t", b=CHUNK))
                nc.vector.tensor_tensor(part[k % 2][:], gate[k % 2][:], inp[k % 2][:], ALU.mult).then_inc(part_ready, 1)
                dve.wait_ge(part_ready, k + 1)
                nc.vector.tensor_tensor(blend[k % 2][:], inp[k % 2][:], part[k % 2][:], ALU.subtract)\
                    .then_inc(blend_ready, 1)

            def driven(k):
                dve.wait_ge(drive_done, k + 1)
                nc.vector.tensor_copy(of_chunk(drive, k), pc[k % 2][:].rearrange("p (b t) -> p b t", b=CHUNK))\
                    .then_inc(drive_ready, 1)

            memory(0)
            for k in range(CHUNKS):
                if k + 1 < CHUNKS:
                    memory(k + 1)
                blended(k)
                if k:
                    driven(k - 1)
            driven(CHUNKS - 1)
            with dve.Fori(0, P // 2 - 1) as i:
                for k in (1, 0):
                    t = i * 2 + (2 - k)
                    dve.wait_ge(state_ready, LEAD + t)
                    nc.vector.tensor_tensor(gated[k][:], tile_of(gates, t), tile_of(states, t - 1), ALU.mult)\
                        .then_inc(gated_ready, 1)
            dve.wait_ge(state_ready, LEAD + P - 1)
            nc.vector.tensor_tensor(gated[1][:], gates[:, P - 1, :], states[:, P - 2, :], ALU.mult).then_inc(gated_ready, 1)

        @block.tensor
        def _(pe):
            pe.wait_ge(w_loaded, 16 * 7)

            def inputs(k):
                pe.wait_ge(kept_ready, k + 1)
                if k >= 2:
                    pe.wait_ge(inp_ready, k - 1)
                nc.tensor.matmul(pi[k % 2][:], lhsT=wi[:], rhs=kept[k % 2][:], start=True, stop=True).then_inc(inp_done, 1)

            def gating(k):
                pe.wait_ge(inp_ready, k + 1)
                if k >= 2:
                    pe.wait_ge(gate_ready, k - 1)
                nc.tensor.matmul(pg[k % 2][:], lhsT=wg[:], rhs=inp[k % 2][:], start=True, stop=True).then_inc(gate_done, 1)

            def driving(k):
                pe.wait_ge(blend_ready, k + 1)
                if k >= 2:
                    pe.wait_ge(drive_ready, k - 1)
                nc.tensor.matmul(pc[k % 2][:], lhsT=wa[:], rhs=blend[k % 2][:], start=True, stop=False)
                nc.tensor.matmul(pc[k % 2][:], lhsT=wb[:], rhs=inp[k % 2][:], start=False, stop=True).then_inc(drive_done, 1)

            inputs(0)
            for k in range(CHUNKS):
                gating(k)
                if k + 1 < CHUNKS:
                    inputs(k + 1)
                driving(k)
            pe.wait_ge(drive_ready, CHUNKS)
            with pe.Fori(0, P // 2) as i:
                for k in range(2):
                    t = i * 2 + k
                    if k == 0:
                        pe.wait_ge(state_ready, LEAD + i * 2)
                    nc.tensor.matmul(pz[k][:, 0:BATCH], lhsT=c["ident"][:], rhs=tile_of(drive, t), start=True, stop=False)
                    pe.wait_ge(gated_ready, t + 1)
                    nc.tensor.matmul(pz[k][:, 0:BATCH], lhsT=wa[:], rhs=gated[k][:], start=False, stop=True)\
                        .then_inc(summed, 1)

        @block.scalar
        def _(act):
            act.wait_ge(w_loaded, 16 * 7)

            def inputs(k):
                act.wait_ge(inp_done, k + 1)
                if k >= 2:
                    act.wait_ge(drive_done, k - 1)
                    act.wait_ge(blend_ready, k - 1)
                nc.scalar.activation(inp[k % 2][:], pi[k % 2][:], ACT.Identity, bias=bi[:]).then_inc(inp_ready, 1)

            def gating(k):
                act.wait_ge(gate_done, k + 1)
                if k >= 2:
                    act.wait_ge(blend_ready, k - 1)
                nc.scalar.activation(gate[k % 2][:], pg[k % 2][:], ACT.Sigmoid, bias=bg[:]).then_inc(gate_ready, 1)

            inputs(0)
            for k in range(CHUNKS):
                gating(k)
                if k + 1 < CHUNKS:
                    inputs(k + 1)
            with act.Fori(0, P // 2) as i:
                for k in range(2):
                    t = i * 2 + k
                    act.wait_ge(summed, t + 1)
                    nc.scalar.activation(tile_of(states, t), pz[k][:, 0:BATCH], ACT.Tanh).then_inc(state_ready, 1)
            act.wait_ge(state_ready, LEAD + P)



LINKS4 = 25


def phase_project(nc, c, d, scr, keep, xT_all, states):
    with Phase(nc) as ctx:
        def sb(name, shape, dt=F32):
            return [ctx.enter_context(nc.sbuf_tensor(f"p_{name}{s}", shape, dt)) for s in range(SLOTS)]

        def sem(name, lead=0):
            return ctx.sem("p_" + name, lead)

        ps = banks(nc, ctx, "p")
        nrm = norm_buffers(nc, ctx, "p", c)
        r = route_buffers(nc, ctx, "p", 1)
        wo, bo = ctx.enter_context(nc.sbuf_tensor("p_wo", [P, P], F32)), ctx.enter_context(nc.sbuf_tensor("p_bo", [P, 1], F32))
        subT, x6, x6T = sb("subT", [P, P]), sb("x6", [P, P]), sb("x6T", [P, P])
        w_loaded, x6_saved = sem("w_loaded"), [sem(f"x6_saved{s}", LEAD) for s in range(SLOTS)]
        out_done, subT_ready, sub_done, x6_ready, x6_transposed = (
            sem(n) for n in ("out_done", "subT_ready", "sub_done", "x6_ready", "x6_transposed"))
        x6T_ready = sem("x6T_ready", LEAD)
        dve_step, taken_set = sem("dve_step"), sem("taken_set")
        block = ctx.enter_context(nc.Block())

        @block.sync
        def _(sp):
            give_leads(sp, ctx)
            sp.dma_start(wo[:], d["n_wo"]).then_inc(w_loaded, 16)
            sp.dma_start(bo[:], d["n_bo"].rearrange("(p o) -> p o", o=1)).then_inc(w_loaded, 16)
            with sp.Fori(0, TURNS) as i:
                for s in range(SLOTS):
                    sp.wait_ge(x6_ready, i * SLOTS + (s + 1))
                    sp.dma_start(dram_tile(scr["x6"], i * SLOTS + s), x6[s][:]).then_inc(x6_saved[s], 16)
            for s in range(SLOTS):
                sp.wait_ge(x6_saved[s], LEAD + 16 * TURNS)

        @block.tensor
        def _(pe):
            pe.wait_ge(w_loaded, 32)
            with pe.Fori(0, TURNS) as i:
                for s in range(SLOTS):
                    pe.wait_ge(x6T_ready, LEAD + i * SLOTS)
                    nc.tensor.matmul(ps["y"][s][:, 0:P], lhsT=wo[:],
                                     rhs=states[:, :, bass.ds(i * SLOTS + s, 1)].rearrange("p t o -> p (t o)"),
                                     start=True, stop=True).then_inc(out_done, 1)
                for s in range(SLOTS):
                    pe.wait_ge(subT_ready, i * SLOTS + (s + 1))
                    nc.tensor.transpose(ps["x"][s][:, 0:P], subT[s][:], c["ident"][:]).then_inc(sub_done, 1)
                for s in range(SLOTS):
                    pe.wait_ge(x6_ready, i * SLOTS + (s + 1))
                    nc.tensor.transpose(ps["y"][s][:, P:2 * P], x6[s][:], c["ident"][:]).then_inc(x6_transposed, 1)
                pe_logits(nc, pe, r, ps["x"], x6T, c["gate1"],
                          lambda s: pe.wait_ge(x6T_ready, LEAD + i * SLOTS + (s + 1)))
                pe_count(nc, pe, r, c, ps["x"], i)

        @block.scalar
        def _(act):
            with act.Fori(0, TURNS) as i:
                for s in range(SLOTS):
                    act.wait_ge(x6_transposed, i * SLOTS + (s + 1))
                    nc.scalar.activation(x6T[s][:], ps["y"][s][:, P:2 * P], ACT.Copy).then_inc(x6T_ready, 1)
                act_route(nc, act, r, i)

        @block.gpsimd
        def _(pool):
            with pool.Fori(0, TURNS) as i:
                pool_norm(nc, pool, nrm, c, i)
                pool_scatter(nc, pool, r, c, i, x6, scr["sorted1"])

        @block.vector
        def _(dve):
            dve.wait_ge(w_loaded, 32)
            nc.vector.tensor_copy(keep["route1"]["taken"][:], c["row_base"][:]).then_inc(taken_set, 1)
            dve.wait_ge(taken_set, 1)
            with dve.Fori(0, TURNS) as i:
                chain = Chain(dve, dve_step, i, LINKS4)
                for s in range(SLOTS):
                    dve.wait_ge(out_done, i * SLOTS + (s + 1))
                    nc.vector.scalar_tensor_tensor(out=subT[s][:], in0=ps["y"][s][:, 0:P], scalar=bo[:],
                                                   in1=tile_of(xT_all, i * SLOTS + s), op0=ALU.add, op1=ALU.add)\
                        .then_inc(subT_ready, 1)

                def x6_free(s):
                    dve.wait_ge(x6_saved[s], LEAD + i * 16)
                    dve.wait_ge(r["rows_free"], LEAD + i * SLOTS)
                dve_norm(nc, dve, nrm, chain, i, [t[:, 0:P] for t in ps["x"]], [(sub_done, i * SLOTS + (s + 1)) for s in range(SLOTS)],
                         [t[:] for t in x6], free=x6_free, done=(x6_ready, i, 0))
                dve_route(nc, dve, r, c, chain, i, ps["x"], c["gate1_b"], keep["route1"])
                chain.close()



LINKS6 = 8


def phase_finish(nc, c, keep, scr, out):
    with Phase(nc) as ctx:
        def sb(name, shape, dt=F32):
            return [ctx.enter_context(nc.sbuf_tensor(f"f_{name}{s}", shape, dt)) for s in range(SLOTS)]

        def sem(name, lead=0):
            return ctx.sem("f_" + name, lead)

        nrm = norm_buffers(nc, ctx, "f", c)
        g = gather_buffers(nc, ctx, "f", 1)
        x6, sub, x7 = sb("x6", [P, P]), sb("sub", [P, P]), sb("x7", [P, P])
        x6_loaded, x7_saved = [sem(f"x6_loaded{s}") for s in range(SLOTS)], [sem(f"x7_saved{s}", LEAD) for s in range(SLOTS)]
        joined, x7_ready, dve_step = sem("joined", LEAD), sem("x7_ready", LEAD), sem("dve_step")
        block = ctx.enter_context(nc.Block())

        @block.sync
        def _(sp):
            give_leads(sp, ctx)
            with sp.Fori(0, TURNS) as i:
                for s in range(SLOTS):
                    sp.wait_ge(joined, LEAD + i * SLOTS)
                    sp.dma_start(x6[s][:], dram_tile(scr["x6"], i * SLOTS + s)).then_inc(x6_loaded[s], 16)

        @block.scalar
        def _(act):
            with act.Fori(0, TURNS) as i:
                for s in range(SLOTS):
                    act.wait_ge(x7_ready, LEAD + i * SLOTS + (s + 1))
                    act.dma_start(dram_tile(out, i * SLOTS + s), x7[s][:]).then_inc(x7_saved[s], 16)
            for s in range(SLOTS):
                act.wait_ge(x7_saved[s], LEAD + 16 * TURNS)

        @block.gpsimd
        def _(pool):
            pool_gather(nc, pool, g, c, keep["route1"], 0, scr["expert_out1"])
            with pool.Fori(0, TURNS) as i:
                pool.wait_ge(joined, LEAD + i * SLOTS + SLOTS)
                stand_alone(pool, c)
                pool_gather(nc, pool, g, c, keep["route1"], i + 1, scr["expert_out1"])
                pool_norm(nc, pool, nrm, c, i)
            for s in range(SLOTS):
                pool.wait_ge(g["gathered"][s], 16 * (TURNS + 1))

        @block.vector
        def _(dve):
            with dve.Fori(0, TURNS) as i:
                chain = Chain(dve, dve_step, i, LINKS6)
                for s in range(SLOTS):
                    dve.wait_ge(x6_loaded[s], i * 16 + 16)
                    dve.wait_ge(x7_ready, LEAD + i * SLOTS)
                    dve.wait_ge(g["gathered"][s], i * 16 + 16)
                    nc.vector.scalar_tensor_tensor(out=sub[s][:], in0=g["y"][0][s][:], scalar=g["weights"][s][:, 0:1],
                                                   in1=x6[s][:], op0=ALU.mult, op1=ALU.add).then_inc(joined, 1)

                def x7_free(s):
                    dve.wait_ge(x7_saved[s], LEAD + i * 16)
                dve_norm(nc, dve, nrm, chain, i, [t[:] for t in sub], [(joined, LEAD + i * SLOTS + (s + 1)) for s in range(SLOTS)],
                         [t[:] for t in x7], free=x7_free, done=(x7_ready, i, LEAD))
                chain.close()


def lay_out(inputs):
    f = {k: np.asarray(v) for k, v in inputs.items()}
    con = np.ascontiguousarray
    qkv = f["L1_attn_w_qkv"]
    swap = np.arange(P).reshape(HEADS, 2, DH // 2)[:, ::-1].reshape(P)
    heads = np.array([G * g + j for j in range(G) for g in range(G)])
    t = np.arange(P)
    inv = (np.float32(1.0) / np.float32(10000.0) ** (np.arange(0, DH, 2, dtype=np.float32) / np.float32(DH))).astype(np.float32)
    angle = (t.astype(np.float32)[None, :] * np.tile(np.concatenate([inv, inv]), HEADS)[:, None]).astype(np.float32)
    sign = np.where(np.arange(P) % DH < DH // 2, -1.0, 1.0)[:, None]
    feature = np.arange(P)
    out = dict(
        x=f["x"], ctx=f["ctx_1024"],
        ident=np.eye(P, dtype=np.float32),
        mask_q=np.float32(SCALE) * ((feature % 32 // DH)[:, None] == np.arange(G)[None, :]).astype(np.float32),
        mask_k=((feature // 32)[:, None] == np.arange(G)[None, :]).astype(np.float32),
        iota8=np.arange(EXPERTS, dtype=np.float32),
        window=np.where(np.abs(t[:, None] - t[None, :]) <= WINDOW, 0.0, MASKED).astype(np.float32),
        causal=np.where(t[None, :] <= t[:, None], 0.0, MASKED).astype(np.float32),
        head_mask=np.where(t[None, :] < heads[:, None], MASKED, 0.0).astype(np.float32),
        cos=np.cos(angle).astype(np.float32), sin=(np.sin(angle) * sign).astype(np.float32),
        tri=(t[:, None] < t[None, :]).astype(np.float32),
        dist=np.abs(t[:, None] - t[None, :]).astype(np.float32),
        row_base=(REGION * np.arange(EXPERTS)).astype(np.float32),
        iota_tiles=np.arange(TILES0, dtype=np.float32),
        part_iota=t.astype(np.float32)[:, None].copy(),
        ds=f["L0_attn_dist_scale"].reshape(1),
        a_wq=f["L0_attn_Wq"], a_wk=f["L0_attn_Wk"], a_wv=f["L0_attn_Wv"], a_wo=f["L0_attn_Wo"],
        a_bq=f["L0_attn_bq"], a_bk=f["L0_attn_bk"], a_bv=f["L0_attn_bv"], a_bo=f["L0_attn_bo"],
        a_w1=f["L0_attn_W1"], a_b1=f["L0_attn_b1"].reshape(FF1 // P, P).T, a_w2=f["L0_attn_W2"], a_b2=f["L0_attn_b2"],
        ln1_g=f["L0_attn_ln1_g"], ln1_b=f["L0_attn_ln1_b"], ln2_g=f["L0_attn_ln2_g"], ln2_b=f["L0_attn_ln2_b"],
        x_wq=con(f["L0_xattn_Wq"].T), x_wk=con(f["L0_xattn_Wk"].T), x_wv=con(f["L0_xattn_Wv"].T),
        x_wo=con(f["L0_xattn_Wo"].T), x_bq=f["L0_xattn_bq"], x_bk=f["L0_xattn_bk"], x_bv=f["L0_xattn_bv"],
        x_bo=f["L0_xattn_bo"], gate0=con(f["L0_ffn_Wg"].T),
        m_wgv=con(np.concatenate([f["L0_ffn_W1"], f["L0_ffn_W2"]], axis=1).transpose(2, 0, 1)),
        m_bgv=con(np.concatenate([f["L0_ffn_b1"], f["L0_ffn_b2"]], axis=1)),
        m_wd=f["L0_ffn_W3"].transpose(2, 0, 1).reshape(FF0 // P, P, EXPERTS, P).transpose(1, 2, 0, 3), m_bd=f["L0_ffn_b3"],
        l_wq=con(qkv[:, 0:P]), l_wk=con(qkv[:, P:2 * P]), l_wv=con(qkv[:, 2 * P:]),
        l_wqp=con(qkv[:, 0:P][:, swap]), l_wkp=con(qkv[:, P:2 * P][:, swap]),
        l_wo=f["L1_attn_w_proj"], l_bo=f["L1_attn_b_proj"],
        n_wi=con(f["L1_xattn_Wi"].T), n_wg=con(f["L1_xattn_Wg"].T), n_a=con(f["L1_xattn_A"].T),
        n_b=con(f["L1_xattn_Bm"].T), n_wo=con(f["L1_xattn_Wo"].T),
        n_bi=f["L1_xattn_bi"], n_bg=f["L1_xattn_bg"], n_bo=f["L1_xattn_bo"],
        n_decay=con(np.repeat(f["L1_xattn_decay"].reshape(HEADS), DH)),
        gate1=f["L1_ffn_switch_w"], gate1_b=f["L1_ffn_switch_b"],
        s_w1=con(f["L1_ffn_w1"].transpose(1, 0, 2)), s_b1=f["L1_ffn_b1"],
        s_w2=f["L1_ffn_w2"].reshape(EXPERTS, FF1 // P, P, P).transpose(2, 0, 1, 3), s_b2=f["L1_ffn_b2"],
    )
    return {k: con(v) for k, v in out.items()}


def keep_buffers(nc, ctx):
    def sb(name, shape, dt=F32):
        return ctx.enter_context(nc.sbuf_tensor("keep_" + name, shape, dt))
    def routing(tag, picks, tiles):
        return dict(picks=picks, tiles=tiles, weights=sb("weights" + tag, [P, BATCH + SLOTS, picks]),
                     rows=sb("rows" + tag, [P, BATCH + SLOTS, picks]), taken=sb("taken" + tag, [P, EXPERTS]),
                     out_rows=sb("out_rows" + tag, [P, BATCH + SLOTS, picks], U32),
                     tile_expert=sb("tile_expert" + tag, [P, tiles], I32),
                     tile_row=sb("tile_row" + tag, [P, tiles], I32))

    return dict(route0=routing("0", 2, TILES0), route1=routing("1", 1, TILES1),
                 experts_loaded=nc.alloc_semaphore("experts_loaded"))



def program(nc, d, out):
    with ExitStack() as ctx:
        keep, scr = keep_buffers(nc, ctx), scratch(nc)
        c = load_constants(nc, ctx, d)
        with ExitStack() as first:
            experts0 = expert_buffers(nc, first, "0", FF0 // P)
            phase_encode(nc, c, d, scr, keep, experts0)
            phase_table(nc, c, keep["route0"], "t0", scr["sorted0"])
            phase_experts(nc, c, keep, keep["route0"], experts0, "m0", True, scr["sorted0"], scr["expert_out0"], 16 * 4)
        experts1 = expert_buffers(nc, ctx, "1", FF1 // P)
        with ExitStack() as second:
            xT_all = second.enter_context(nc.sbuf_tensor("xT_all", [P, BATCH, P], F32))
            phase_decode(nc, c, d, keep, scr, xT_all, experts1)
            states = second.enter_context(nc.sbuf_tensor("states", [P, P, BATCH], F32))
            phase_recurrent(nc, c, d, scr, xT_all, states)
            phase_project(nc, c, d, scr, keep, xT_all, states)
        phase_table(nc, c, keep["route1"], "t1", scr["sorted1"])
        phase_experts(nc, c, keep, keep["route1"], experts1, "m1", False, scr["sorted1"], scr["expert_out1"], 16 * 8)
        phase_finish(nc, c, keep, scr, out)


def scratch(nc):
    def dram(name, shape):
        return nc.dram_tensor("scratch_" + name, shape, F32, kind="Internal").ap()
    return dict(ctxT=dram("ctxT", (BATCH, P, P)), x3=dram("x3", (BATCH, P, P)),
                x6=dram("x6", (BATCH, P, P)),
                sorted0=dram("sorted0", (EXPERTS * REGION, P)), sorted1=dram("sorted1", (EXPERTS * REGION, P)),
                expert_out0=dram("expert_out0", (TILES0 * P, P)), expert_out1=dram("expert_out1", (TILES1 * P, P)))




def kernel(**inputs):
    from concourse import bacc
    from concourse.bass_utils import run_bass_kernel_spmd

    nc = bacc.Bacc("TRN2", target_bir_lowering=False, num_devices=1)
    arrays = lay_out(inputs)
    dram = {name: nc.dram_tensor("in_" + name, a.shape, mybir.dt.from_np(a.dtype), kind="ExternalInput").ap()
            for name, a in arrays.items()}
    out = nc.dram_tensor("out_x", (BATCH, P, P), F32, kind="ExternalOutput").ap()
    program(nc, dram, out)
    result = run_bass_kernel_spmd(nc, [{"in_" + name: a for name, a in arrays.items()}], core_ids=[0])
    return result.results[0]["out_x"]
```

```python
from contextlib import ExitStack

import numpy as np
import concourse.bass as bass
from concourse import mybir

F32 = mybir.dt.float32
BF16 = mybir.dt.bfloat16
I32 = mybir.dt.int32
U32 = mybir.dt.uint32
ACT = mybir.ActivationFunctionType
ALU = mybir.AluOpType
AX = mybir.AxisListType

P = 128
BATCH = 32
SLOTS = 4
TURNS = BATCH // SLOTS
HEADS = 16
DH = P // HEADS
G = 4
VC = 32
SCALE = float(np.float32(1.0) / np.sqrt(np.float32(DH)))
EPS = 1e-5
MASKED = -1e30
WINDOW = 64
EXPERTS = 8
FF0 = 256
FF1 = 512
TOKENS = BATCH * P
REGION = TOKENS + P
TILES0 = 2 * TOKENS // P + EXPERTS
TILES1 = TOKENS // P + EXPERTS


class Chain:

    def __init__(self, eng, sem, turn, per_turn):
        self.eng, self.sem, self.turn, self.per_turn, self.count = eng, sem, turn, per_turn, 0

    def mark(self, ins):
        ins.then_inc(self.sem, 1)
        self.count += 1
        return self.sem, self.turn * self.per_turn + self.count

    def wait(self, step):
        self.eng.wait_ge(*step)

    def close(self):
        assert self.count == self.per_turn, f"per_turn should be {self.count}"


LEAD = 8


def give_leads(eng, ctx):
    for sem in ctx.led:
        eng.sem_inc(sem, LEAD)


class Phase(ExitStack):

    def __init__(self, nc):
        super().__init__()
        self.nc, self.sems, self.led = nc, [], []
        self.callback(self.clear)

    def sem(self, name, lead=0):
        self.sems.append(self.nc.alloc_semaphore(name))
        if lead:
            self.led.append(self.sems[-1])
        return self.sems[-1]

    def clear(self):
        self.nc.clear_and_free_semaphores(self.sems)
        self.nc.all_engine_barrier()


def stand_alone(eng, c):
    eng.sem_inc(c["stood"], 1)


def bcast(ap, n):
    return ap.unsqueeze(2).to_broadcast([ap.shape[0], ap.shape[1], n])


def repeat(ap, n):
    return ap.unsqueeze(1).to_broadcast([ap.shape[0], n, ap.shape[1]])


def tile_of(big, n):
    return big[:, bass.ds(n, 1), :].rearrange("p o a -> p (o a)")


def dram_tile(d, n):
    return d[bass.ds(n, 1)].rearrange("o p a -> (o p) a")



MATRICES = tuple((n, P) for n in (
    "ident", "a_wq", "a_wk", "a_wv", "a_wo", "x_wq", "x_wk", "x_wv", "x_wo", "l_wq", "l_wk", "l_wqp", "l_wkp",
    "l_wv", "l_wo", "window", "causal", "cos", "sin", "tri_f", "dist")) + (
    ("a_w1", FF1), ("a_w2", FF1), ("mask_q", G), ("mask_k", G), ("part_iota", 1), ("a_bq", 1), ("a_bk", 1), ("x_bq", 1),
    ("x_bk", 1), ("a_b1", FF1 // P), ("gate0", EXPERTS), ("gate1", EXPERTS))
ROWS = tuple((n, P) for n in ("a_bv", "a_bo", "a_b2", "ln1_g", "ln1_b", "ln2_g", "ln2_b", "x_bv", "x_bo", "l_bo")) + (
    ("iota8", EXPERTS), ("row_base", EXPERTS), ("gate1_b", EXPERTS), ("iota_tiles", TILES0), ("ds_col", 1))
PARTS = 4


def load_constants(nc, ctx, d):
    c = dict()
    loads = []

    def sb(name, shape, dt=F32):
        return ctx.enter_context(nc.sbuf_tensor("c_" + name, shape, dt))

    def packed(name, members):
        tile, at = sb(name, [P, sum(n for _, n in members)]), 0
        for member, n in members:
            c[member] = tile[:, at:at + n]
            at += n
        return tile, at

    matrices, n = packed("matrices", MATRICES)
    for k in range(PARTS):
        part = slice(k * n // PARTS, (k + 1) * n // PARTS)
        loads.append((matrices[:, part], d["matrices"][:, part]))
    rows, n = packed("rows", ROWS)
    loads.append((rows[:], d["rows"].partition_broadcast(P)))
    c["a_w2"] = c["a_w2"].rearrange("p (k n) -> p k n", n=P)
    c["bias0"] = sb("bias0", [P, HEADS, P])
    loads.append((c["bias0"][:], d["head_mask"].partition_broadcast(P)))
    c["nds"] = sb("nds", [P, 1])
    c["zeros"] = sb("zeros", [P, P])
    c["one_row"] = sb("one_row", [P, EXPERTS])
    c["tri"] = sb("tri", [P, P], BF16)
    c["ones"] = sb("ones", [P, P], BF16)
    c["minus_half"] = sb("minus_half", [P, SLOTS])
    c["a_bk_by_group"], c["x_bk_by_group"] = sb("a_bk_by_group", [P, G]), sb("x_bk_by_group", [P, G])
    c["stood"] = nc.alloc_semaphore("stood")

    with Phase(nc) as inner:
        loaded = inner.sem("constants_loaded")
        nds_ready = inner.sem("nds_ready")
        made = inner.sem("constants_made")
        block = inner.enter_context(nc.Block())

        @block.sync
        def _(sp):
            for tile, src in loads[0::2]:
                sp.dma_start(tile, src).then_inc(loaded, 16)

        @block.scalar
        def _(act):
            for tile, src in loads[1::2]:
                act.dma_start(tile, src).then_inc(loaded, 16)

        @block.vector
        def _(dve):
            nc.vector.memset(c["zeros"][:], 0.0)
            nc.vector.memset(c["one_row"][:], 1.0)
            nc.vector.memset(c["ones"][:], 1.0)
            nc.vector.memset(c["minus_half"][:], -0.5)
            dve.wait_ge(loaded, 16 * len(loads))
            nc.vector.tensor_copy(c["tri"][:], c["tri_f"][:])
            nc.vector.tensor_scalar(c["a_bk_by_group"][:], c["mask_k"][:], c["a_bk"][:], None, ALU.mult)
            nc.vector.tensor_scalar(c["x_bk_by_group"][:], c["mask_k"][:], c["x_bk"][:], None, ALU.mult)
            nc.vector.tensor_scalar_mul(c["nds"][:], c["ds_col"][:], -SCALE).then_inc(nds_ready, 1)
            dve.wait_ge(nds_ready, 1)
            nc.vector.scalar_tensor_tensor(out=c["bias0"][:], in0=repeat(c["dist"][:], HEADS), scalar=c["nds"][:],
                                           in1=c["bias0"][:], op0=ALU.mult, op1=ALU.add).then_inc(made, 1)
            dve.wait_ge(made, 1)
    return c



def attention_buffers(nc, ctx, tag, ps, rope=False):
    def sb(name, shape):
        return [ctx.enter_context(nc.sbuf_tensor(f"{tag}_{name}{s}", shape, F32)) for s in range(SLOTS)]

    def sem(name, lead=0):
        return ctx.sem(f"{tag}_{name}", lead)

    b = dict(ps=ps, **{name: sem(name) for name in (
        "k_done", "k_rotated", "qv_done", "k_ready", "v_ready", "scores_done", "scores_biased", "max_ready", "probs_ready",
        "probs_transposed", "probs_t_ready", "mixed", "mix_back", "rsum_ready",
        "mix_scaled", "mix_transposed", "mixT_ready", "attn_done")})
    b["mix_copied"] = [sem("mix_copied_even"), sem("mix_copied_odd")]
    b["qm"] = sb("q_by_place", [P, G, P])
    b["kg"] = sb("k_by_group", [P, G, P])
    b["va"] = sb("values", [P, HEADS, VC])
    if rope:
        b["turned"] = sb("q_k_turned", [P, 2, P])
    b["sc"] = sb("scores", [P, G, P])
    b["nmax"] = sb("neg_max", [P, G])
    b["pr"] = sb("probs", [P, G, P])
    b["pt"] = sb("probs_t", [P, G * P])
    b["ot"] = sb("mix_t", [P, G * P])
    b["rs"] = sb("rsum", [P, HEADS])
    b["mix"] = sb("mix", [P, P])
    b["mixT"] = sb("mixT", [P, P])
    return b


UNITS = G * SLOTS


def pe_keys(nc, pe, b, w, src, ready):
    for s in range(SLOTS):
        ready(s)
        nc.tensor.matmul(b["ps"]["x"][s][:, 0:P], lhsT=w["wk"][:], rhs=src[s], start=True, stop=True)\
            .then_inc(b["k_done"], 1)


def pe_queries(nc, pe, b, w, q_src, kv_src, ready):
    for s in range(SLOTS):
        ready(s)
        bank_x, bank_y = b["ps"]["x"][s], b["ps"]["y"][s]
        if w["rope"]:
            for k, mat in enumerate((w["wq"], w["wk"], w["wqp"], w["wkp"])):
                nc.tensor.matmul(bank_y[:, k * P:(k + 1) * P], lhsT=mat[:], rhs=q_src[s], start=True, stop=True)
            v = bank_x[:, 0:P]
        else:
            nc.tensor.matmul(bank_y[:, 0:P], lhsT=w["wq"][:], rhs=q_src[s], start=True, stop=True)
            v = bank_y[:, P:2 * P]
        nc.tensor.matmul(v, lhsT=kv_src[s], rhs=w["wv"][:], start=True, stop=True).then_inc(b["qv_done"], 1)


def act_keys(nc, act, b, w, m):
    for s in range(SLOTS):
        act.wait_ge(b["k_rotated" if w["rope"] else "k_done"], m * SLOTS + (s + 1))
        src = b["turned"][s][:, 1, :] if w["rope"] else b["ps"]["x"][s][:, 0:P]
        for g in range(G):
            last = nc.scalar.activation(b["kg"][s][:, g, :], src, ACT.Identity, bias=w["bk_by_group"][:, g:g + 1],
                                        scale=w["mask_k"][:, g:g + 1])
        last.then_inc(b["k_ready"], 1)


def dve_queries(nc, dve, b, w, m, chain, slots=range(SLOTS)):
    for s in slots:
        dve.wait_ge(b["qv_done"], m * SLOTS + (s + 1))
        bank_x, bank_y = b["ps"]["x"][s], b["ps"]["y"][s]
        if w["rope"]:
            both = bank_y[:].rearrange("p (a u) -> p a u", u=P)
            nc.vector.tensor_tensor(b["pr"][s][:, 0:2, :], both[:, 0:2, :], repeat(w["cos"][:], 2), ALU.mult)
            step = chain.mark(nc.vector.tensor_tensor(b["pr"][s][:, 2:4, :], both[:, 2:4, :], repeat(w["sin"][:], 2), ALU.mult))
            chain.wait(step)
            nc.vector.tensor_tensor(b["turned"][s][:], b["pr"][s][:, 0:2, :], b["pr"][s][:, 2:4, :], ALU.add)\
                .then_inc(b["k_rotated"], 1)
            nc.vector.tensor_copy(b["va"][s][:, :, 0:DH], bank_x[:, 0:P].rearrange("p (h d) -> p h d", d=DH))
            dve.wait_ge(b["k_rotated"], m * SLOTS + (s + 1))
            nc.vector.tensor_tensor(b["qm"][s][:], repeat(b["turned"][s][:, 0, :], G), bcast(w["mask_q"][:], P), ALU.mult)\
                .then_inc(b["v_ready"], 1)
        else:
            nc.vector.scalar_tensor_tensor(out=b["qm"][s][:], in0=repeat(bank_y[:, 0:P], G), scalar=w["bq"][:],
                                           in1=bcast(w["mask_q"][:], P), op0=ALU.add, op1=ALU.mult)
            nc.vector.tensor_tensor(b["va"][s][:, :, 0:DH], bank_y[:, P:2 * P].rearrange("p (h d) -> p h d", d=DH),
                                    w["bv"][:].rearrange("p (h d) -> p h d", d=DH), ALU.add).then_inc(b["v_ready"], 1)


def pe_attention(nc, pe, b, w, m, first=None, first_mix=None, beside=None):
    bank_x, bank_y = b["ps"]["x"], b["ps"]["y"]

    def mix(j, s):
        pe.wait_ge(b["probs_t_ready"], m * UNITS + (SLOTS * j + s + 1))
        if j == 0 and first_mix:
            first_mix(s)
        for g in range(G):
            last = nc.tensor.matmul(bank_y[s][32 * g:32 * g + VC, j * P:(j + 1) * P],
                                    lhsT=b["va"][s][:, G * g + j, :], rhs=b["pt"][s][:, g * P:(g + 1) * P],
                                    start=True, stop=True)
        last.then_inc(b["mixed"], 1)

    def scores(j, s):
        if j == 0:
            pe.wait_ge(b["k_ready"], m * SLOTS + (s + 1))
            pe.wait_ge(b["v_ready"], m * SLOTS + (s + 1))
            if first:
                first(s)
        nc.tensor.matmul(bank_x[s][:], lhsT=b["qm"][s][:, j, :], rhs=b["kg"][s][:].rearrange("p g u -> p (g u)"),
                         start=True, stop=True).then_inc(b["scores_done"], 1)

    def turn(j, s):
        pe.wait_ge(b["probs_ready"], m * UNITS + (SLOTS * j + s + 1))
        for g in range(G):
            last = nc.tensor.transpose(bank_x[s][:, g * P:(g + 1) * P], b["pr"][s][:, g, :], w["ident"][:])
        last.then_inc(b["probs_transposed"], 1)

    for k in range(UNITS + 2):
        if k < UNITS:
            if k >= SLOTS:
                mix(k // SLOTS - 1, k % SLOTS)
            scores(k // SLOTS, k % SLOTS)
            if beside:
                beside(k)
        if k >= 2:
            turn((k - 2) // SLOTS, (k - 2) % SLOTS)
    for s in range(SLOTS):
        mix(G - 1, s)
    for s in range(SLOTS):
        pe.wait_ge(b["mix_copied"][s % 2], m * (SLOTS // 2) + (s // 2 + 1))
        for j in range(G):
            last = nc.tensor.transpose(bank_x[s][:, j * P:(j + 1) * P], b["ot"][s][:, j * P:(j + 1) * P], w["ident"][:])
        last.then_inc(b["mix_back"], 1)
    for s in range(SLOTS):
        pe.wait_ge(b["mix_scaled"], m * SLOTS + (s + 1))
        nc.tensor.transpose(bank_y[s][:, 0:P], b["mix"][s][:], w["ident"][:]).then_inc(b["mix_transposed"], 1)
    for s in range(SLOTS):
        pe.wait_ge(b["mixT_ready"], m * SLOTS + (s + 1))
        nc.tensor.matmul(bank_y[s][:, P:2 * P], lhsT=b["mixT"][s][:], rhs=w["wo"][:],
                         start=True, stop=True).then_inc(b["attn_done"], 1)


def act_attention(nc, act, b, m, beside=None):
    for k in range(UNITS + 1):
        if k < UNITS:
            s = k % SLOTS
            act.wait_ge(b["max_ready"], m * UNITS + (k + 1))
            for g in range(G):
                last = nc.scalar.activation(b["pr"][s][:, g, :], b["sc"][s][:, g, :], ACT.Exp,
                                            bias=b["nmax"][s][:, g:g + 1], scale=1.0)
            last.then_inc(b["probs_ready"], 1)
            if beside:
                beside(k)
        if k >= 1:
            s = (k - 1) % SLOTS
            act.wait_ge(b["probs_transposed"], m * UNITS + k)
            if k - 1 >= SLOTS:
                act.wait_ge(b["mixed"], m * UNITS + (k - SLOTS))
            nc.scalar.activation(b["pt"][s][:], b["ps"]["x"][s][:], ACT.Copy).then_inc(b["probs_t_ready"], 1)
    for s in range(0, SLOTS, 2):
        act.wait_ge(b["mixed"], m * UNITS + (UNITS - SLOTS + s + 1))
        nc.scalar.activation(b["ot"][s][:], b["ps"]["y"][s][:], ACT.Copy).then_inc(b["mix_copied"][0], 1)
    for s in range(SLOTS):
        act.wait_ge(b["mix_transposed"], m * SLOTS + (s + 1))
        nc.scalar.activation(b["mixT"][s][:], b["ps"]["y"][s][:, 0:P], ACT.Copy).then_inc(b["mixT_ready"], 1)


def dve_attention(nc, dve, b, w, m, chain, beside=None):
    for k in range(UNITS):
        j, s = k // SLOTS, k % SLOTS
        dve.wait_ge(b["scores_done"], m * UNITS + (k + 1))
        bias = w["bias"][:, G * j:G * j + G, :] if w["bias_by_head"] else repeat(w["bias"][:], G)
        nc.vector.tensor_tensor(b["sc"][s][:], b["ps"]["x"][s][:].rearrange("p (g u) -> p g u", g=G), bias,
                                ALU.add).then_inc(b["scores_biased"], 1)
        dve.wait_ge(b["scores_biased"], m * UNITS + (k + 1))
        nc.vector.tensor_reduce(b["nmax"][s][:], b["sc"][s][:], AX.X, ALU.max, negate=True)\
            .then_inc(b["max_ready"], 1)
        if beside:
            beside(k)
    for s in range(1, SLOTS, 2):
        dve.wait_ge(b["mixed"], m * UNITS + (UNITS - SLOTS + s + 1))
        nc.vector.tensor_copy(b["ot"][s][:], b["ps"]["y"][s][:]).then_inc(b["mix_copied"][1], 1)
    for s in range(SLOTS):
        dve.wait_ge(b["mix_back"], m * SLOTS + (s + 1))
        mixed = b["ps"]["x"][s][:].rearrange("p (h c) -> p h c", c=VC)
        nc.vector.reciprocal(b["rs"][s][:], mixed[:, :, DH]).then_inc(b["rsum_ready"], 1)
        mixed = b["ps"]["x"][s][:].rearrange("p (j g c) -> p j g c", c=VC, j=G)
        dve.wait_ge(b["rsum_ready"], m * SLOTS + (s + 1))
        nc.vector.tensor_tensor(b["mix"][s][:].rearrange("p (g j d) -> p j g d", g=G, j=G), mixed[:, :, :, 0:DH],
                                b["rs"][s][:].rearrange("p (j g) -> p j g", g=G).unsqueeze(3).to_broadcast([P, G, G, DH]),
                                ALU.mult).then_inc(b["mix_scaled"], 1)



def norm_buffers(nc, ctx, tag, c):
    def sb(name, shape):
        return ctx.enter_context(nc.sbuf_tensor(f"{tag}_{name}", shape, F32))
    return dict(c=c, stats=[sb(f"stats{s}", [P, 6]) for s in range(SLOTS)], mv=sb("mean_var", [P, SLOTS, 2]),
                ve=sb("var_eps", [P, SLOTS]), rstd=sb("rstd", [P, SLOTS]),
                var_ready=ctx.sem(f"{tag}_var_ready"), rstd_ready=ctx.sem(f"{tag}_rstd_ready"))


def dve_norm_begin(nc, dve, n, chain, src, src_step, gain=None):
    steps = list(src_step)
    for s in range(SLOTS):
        chain.wait(steps[s])
        steps[s] = chain.mark(nc.vector.bn_stats(n["stats"][s][:], src[s]))
    for s in range(SLOTS):
        chain.wait(steps[s])
        stand_alone(dve, n["c"])
        steps[s] = chain.mark(nc.vector.bn_aggr(n["mv"][:, s, :], n["stats"][s][:]))
    chain.wait(steps[-1])
    nc.vector.tensor_scalar_add(n["ve"][:], n["mv"][:, :, 1], EPS).then_inc(n["var_ready"], 1)
    if gain is not None:
        for s in range(SLOTS):
            steps[s] = chain.mark(nc.vector.scalar_tensor_tensor(
                out=src[s], in0=src[s], scalar=n["mv"][:, s, 0:1], in1=gain[:], op0=ALU.subtract, op1=ALU.mult))
    return steps


def dve_norm_end(nc, dve, n, chain, index, src, steps, dst, offset=None, free=None, done=None):
    steps = list(steps)
    dve.wait_ge(n["rstd_ready"], index + 1)
    for s in range(SLOTS):
        if free:
            free(s)
        if offset:
            chain.wait(steps[s])
            ins = nc.vector.scalar_tensor_tensor(out=dst[s], in0=src[s], scalar=n["rstd"][:, s:s + 1], in1=offset[s],
                                                 op0=ALU.mult, op1=ALU.add)
        else:
            ins = nc.vector.tensor_scalar(dst[s], src[s], n["mv"][:, s, 0:1], n["rstd"][:, s:s + 1],
                                          ALU.subtract, ALU.mult)
        if done is None:
            steps[s] = chain.mark(ins)
        else:
            ins.then_inc(done[0], 1)
            steps[s] = done[0], done[2] + done[1] * SLOTS + (s + 1)
    return steps


def dve_norm(nc, dve, n, chain, index, src, src_step, dst, affine=None, free=None, done=None):
    gain, offset = affine or (None, None)
    steps = dve_norm_begin(nc, dve, n, chain, src, src_step, gain)
    return dve_norm_end(nc, dve, n, chain, index, src, steps, dst, offset, free, done)


def pool_norm(nc, pool, n, c, index):
    pool.wait_ge(n["var_ready"], index + 1)
    nc.gpsimd.tensor_tensor(n["rstd"][:], n["ve"][:], c["minus_half"][:], ALU.pow).then_inc(n["rstd_ready"], 1)


def banks(nc, ctx, tag):
    def by_slot(name):
        return [ctx.enter_context(nc.psum_tensor(f"{tag}_bank_{name}{s}", [P, 512], F32)) for s in range(SLOTS)]

    return dict(x=by_slot("x"), y=by_slot("y"))



LOGITS, COUNTS = 2, 3


def route_buffers(nc, ctx, tag, picks):
    def sb(name, shape, dt=F32):
        return ctx.enter_context(nc.sbuf_tensor(f"{tag}_{name}", shape, dt))

    def sem(name, lead=0):
        return ctx.sem(f"{tag}_{name}", lead)

    return dict(picks=picks, logits=sb("logits", [P, SLOTS, EXPERTS]), top=sb("top", [P, SLOTS, 8]),
                at=sb("at", [P, SLOTS, 8], U32), at_f=sb("at_f", [P, SLOTS, 8]),
                hot=[sb(f"hot{q}", [P, SLOTS, EXPERTS]) for q in range(picks)],
                any=sb("any", [P, SLOTS, EXPERTS], BF16), place=sb("place", [P, SLOTS, EXPERTS]),
                put=[sb(f"put{q}", [P, SLOTS, EXPERTS]) for q in range(picks)],
                row_u=sb("row_u", [P, SLOTS, picks], U32), gap=sb("gap", [P, SLOTS, EXPERTS]),
                ex=sb("ex", [P, SLOTS, EXPERTS]), den=sb("den", [P, SLOTS]),
                logits_done=sem("logits_done"), gap_ready=sem("gap_ready"), ex_ready=sem("ex_ready"),
                hot_ready=sem("hot_ready"), counted=sem("counted"), rows_ready=sem("rows_ready", LEAD),
                scattered=[sem(f"scattered{s}") for s in range(SLOTS)], rows_free=sem("rows_free", LEAD))


def pe_logits(nc, pe, r, bank, xT, gate):
    for s in range(SLOTS):
        last = nc.tensor.matmul(bank[LOGITS][:, s * EXPERTS:(s + 1) * EXPERTS], lhsT=xT[s], rhs=gate[:],
                                start=True, stop=True)
    last.then_inc(r["logits_done"], 1)


def pe_count(nc, pe, r, c, bank, turn):
    pe.wait_ge(r["hot_ready"], turn + 1)
    for s in range(SLOTS + 1):
        out = bank[COUNTS][:, s * EXPERTS:(s + 1) * EXPERTS]
        for before in range(s):
            last = nc.tensor.matmul(out, lhsT=c["ones"][:], rhs=r["any"][:, before, :], start=before == 0,
                                    stop=s == SLOTS and before == s - 1)
        if s < SLOTS:
            nc.tensor.matmul(out, lhsT=c["tri"][:], rhs=r["any"][:, s, :], start=s == 0, stop=True)
    last.then_inc(r["counted"], 1)


def dve_route(nc, dve, r, c, chain, turn, bank, gate_bias, kept):
    picks, taken = r["picks"], kept["taken"]
    wide = [P, SLOTS, EXPERTS]

    def of_turn(big, q):
        return big[:, bass.ds(turn * SLOTS, SLOTS), q:q + 1].rearrange("p n o -> p (n o)")

    dve.wait_ge(r["logits_done"], turn + 1)
    logits = bank[LOGITS][:, 0:SLOTS * EXPERTS].rearrange("p (s e) -> p s e", e=EXPERTS)
    if gate_bias is None:
        step = chain.mark(nc.vector.tensor_copy(r["logits"][:], logits))
    else:
        step = chain.mark(nc.vector.tensor_tensor(r["logits"][:], logits, repeat(gate_bias[:], SLOTS), ALU.add))
    chain.wait(step)
    stand_alone(dve, c)
    steps = [chain.mark(nc.vector.max(r["top"][:, s, :], r["logits"][:, s, :])) for s in range(SLOTS)]
    for s in range(SLOTS):
        chain.wait(steps[s])
        stand_alone(dve, c)
        step = chain.mark(nc.vector.max_index(r["at"][:, s, :], r["top"][:, s, :], r["logits"][:, s, :]))
    nc.vector.tensor_tensor(r["gap"][:], (r["logits"] if picks == 1 else r["top"])[:],
                            r["top"][:, :, 0:1].to_broadcast(wide), ALU.subtract).then_inc(r["gap_ready"], 1)
    chain.wait(step)
    chain.wait(chain.mark(nc.vector.tensor_copy(r["at_f"][:], r["at"][:])))
    for q in range(picks):
        step = chain.mark(nc.vector.tensor_tensor(r["hot"][q][:], repeat(c["iota8"][:], SLOTS),
                                                  r["at_f"][:, :, q:q + 1].to_broadcast(wide), ALU.is_equal))
    chain.wait(step)
    if picks == 2:
        nc.vector.tensor_tensor(r["any"][:], r["hot"][0][:], r["hot"][1][:], ALU.add).then_inc(r["hot_ready"], 1)
    else:
        nc.vector.tensor_copy(r["any"][:], r["hot"][0][:]).then_inc(r["hot_ready"], 1)
    dve.wait_ge(r["ex_ready"], turn + 1)
    if picks == 1:
        step = chain.mark(nc.vector.reduce_sum(r["den"][:], r["ex"][:], AX.X))
    else:
        step = chain.mark(nc.vector.tensor_scalar_add(r["den"][:], r["ex"][:, :, 1], 1.0))
    chain.wait(step)
    chain.wait(chain.mark(nc.vector.reciprocal(r["den"][:], r["den"][:])))
    stand_alone(dve, c)
    nc.vector.tensor_copy(of_turn(kept["weights"], 0), r["den"][:])
    if picks == 2:
        nc.vector.tensor_tensor(of_turn(kept["weights"], 1), r["den"][:], r["ex"][:, :, 1], ALU.mult)
    dve.wait_ge(r["counted"], turn + 1)
    counts = bank[COUNTS][:, 0:(SLOTS + 1) * EXPERTS].rearrange("p (s e) -> p s e", e=EXPERTS)
    step = chain.mark(nc.vector.tensor_tensor(r["place"][:], counts[:, 0:SLOTS, :], repeat(taken[:], SLOTS), ALU.add))
    chain.wait(step)
    after = chain.mark(nc.vector.tensor_tensor(taken[:], counts[:, SLOTS, :], taken[:], ALU.add))
    steps = [chain.mark(nc.vector.tensor_tensor(r["put"][q][:], r["hot"][q][:], r["place"][:], ALU.mult))
             for q in range(picks)]
    for q in range(picks):
        chain.wait(steps[q])
        step = chain.mark(nc.vector.reduce_sum(of_turn(kept["rows"], q), r["put"][q][:], AX.X))
    chain.wait(step)
    dve.wait_ge(r["rows_free"], LEAD + turn * SLOTS)
    stand_alone(dve, c)
    nc.vector.tensor_copy(r["row_u"][:], kept["rows"][:, bass.ds(turn * SLOTS, SLOTS), :]).then_inc(r["rows_ready"], 1)
    chain.wait(after)


def act_route(nc, act, r, turn):
    act.wait_ge(r["gap_ready"], turn + 1)
    nc.scalar.activation(r["ex"][:], r["gap"][:], ACT.Exp).then_inc(r["ex_ready"], 1)


def pool_scatter(nc, pool, r, c, turn, src, dst):
    pool.wait_ge(r["rows_ready"], LEAD + turn + 1)
    stand_alone(pool, c)
    for s in range(SLOTS):
        for q in range(r["picks"]):
            nc.gpsimd.indirect_dma_start(out=dst, out_offset=bass.IndirectOffsetOnAxis(ap=r["row_u"][:, s, q:q + 1], axis=0),
                                         in_=src[s][:], in_offset=None).then_inc(r["scattered"][s], 16)


def pool_scattered(pool, r, turn):
    for s in range(SLOTS):
        pool.wait_ge(r["scattered"][s], (turn + 1) * (16 * r["picks"]))
        pool.sem_inc(r["rows_free"], 1)



LINKS1 = 72


def phase_encode(nc, c, d, scr, keep, experts0):
    with Phase(nc) as ctx:
        def sb(name, shape, dt=F32):
            return [ctx.enter_context(nc.sbuf_tensor(f"e_{name}{s}", shape, dt)) for s in range(SLOTS)]

        def sem(name, lead=0):
            return ctx.sem("e_" + name, lead)

        ps = banks(nc, ctx, "e")
        b = attention_buffers(nc, ctx, "e", ps)
        nrm = norm_buffers(nc, ctx, "e", c)
        r = route_buffers(nc, ctx, "e", 2)
        wa = dict(wq=c["a_wq"], wk=c["a_wk"], wv=c["a_wv"], wo=c["a_wo"], bq=c["a_bq"], bk=c["a_bk"], bv=c["a_bv"], bias=c["bias0"], bk_by_group=c["a_bk_by_group"],
                   bias_by_head=True, rope=False, ident=c["ident"], mask_q=c["mask_q"], mask_k=c["mask_k"])
        wx = dict(wq=c["x_wq"], wk=c["x_wk"], wv=c["x_wv"], wo=c["x_wo"], bq=c["x_bq"], bk=c["x_bk"], bv=c["x_bv"], bias=c["window"], bk_by_group=c["x_bk_by_group"],
                   bias_by_head=False, rope=False, ident=c["ident"], mask_q=c["mask_q"], mask_k=c["mask_k"])
        xin, cin = sb("x_in", [P, P]), sb("ctx_in", [P, P])
        x_bo, x_ln2b, x1_b2, x2_bo = sb("x_bo", [P, P]), sb("x_ln2b", [P, P]), sb("x1_b2", [P, P]), sb("x2_bo", [P, P])
        xc = sb("xT_ctxT", [P, 2 * P])
        xT, cT = [t[:, 0:P] for t in xc], [t[:, P:2 * P] for t in xc]
        sub, x1, x1T = sb("sub", [P, P]), sb("x1", [P, P]), sb("x1T", [P, P])
        hid, x2, x2T = sb("hidden", [P, FF1]), sb("x2", [P, P]), sb("x2T", [P, P])
        x3, x3T = sb("x3", [P, P]), sb("x3T", [P, P])

        x_loaded = [sem(f"x_loaded{s}") for s in range(SLOTS)]
        ctx_saved, x3_saved = ([sem(f"{n}{s}", LEAD) for s in range(SLOTS)] for n in ("ctx_saved", "x3_saved"))
        x_transposed, xT_ready, x_summed = sem("x_transposed"), sem("xT_ready"), sem("x_summed")
        x1_ready, x1_transposed, x1T_ready = sem("x1_ready"), sem("x1_transposed"), sem("x1T_ready")
        hidden_done, dense_done = sem("hidden_done"), sem("dense_done")
        hidden_ready = [sem("hidden_ready_even"), sem("hidden_ready_odd")]
        cross_joined = sem("cross_joined", LEAD)
        x2_ready, x2_transposed, x2T_ready = sem("x2_ready", LEAD), sem("x2_transposed"), sem("x2T_ready")
        x3_ready, x3_transposed, x3T_ready = sem("x3_ready"), sem("x3_transposed"), sem("x3T_ready")
        x1_b2_ready, x2_bo_ready = sem("x1_b2_ready"), sem("x2_bo_ready")
        dve_step, buffers_set = sem("dve_step"), sem("buffers_set")
        block = ctx.enter_context(nc.Block())

        @block.sync
        def _(sp):
            give_leads(sp, ctx)
            def load(i, s):
                sp.dma_start(xin[s][:], dram_tile(d["x"], i * SLOTS + s)).then_inc(x_loaded[s], 16)
                sp.dma_start(cin[s][:], dram_tile(d["ctx"], i * SLOTS + s)).then_inc(x_loaded[s], 16)

            def turn(i, last):
                for s in range(SLOTS):
                    sp.wait_ge(xT_ready, i * SLOTS + (s + 1))
                    sp.dma_start(dram_tile(scr["ctxT"], i * SLOTS + s), cT[s]).then_inc(ctx_saved[s], 16)
                if not last:
                    for s in range(SLOTS):
                        sp.wait_ge(x_transposed, i * SLOTS + SLOTS)
                        sp.wait_ge(x_summed, i * SLOTS + SLOTS)
                        load(i + 1, s)
                for s in range(SLOTS):
                    sp.wait_ge(x3_ready, i * SLOTS + (s + 1))
                    sp.dma_start(dram_tile(scr["x3"], i * SLOTS + s), x3[s][:]).then_inc(x3_saved[s], 16)

            for s in range(SLOTS):
                load(0, s)
            sp.wait_ge(x_transposed, SLOTS)
            load_experts(sp, keep, experts0, d, ("m_wgv", "m_wd", "m_bgv", "m_bd"))
            with sp.Fori(0, TURNS - 1) as i:
                turn(i, False)
            turn(TURNS - 1, True)
            for s in range(SLOTS):
                sp.wait_ge(ctx_saved[s], LEAD + 16 * TURNS)
                sp.wait_ge(x3_saved[s], LEAD + 16 * TURNS)

        @block.tensor
        def _(pe):
            def front(i):
                for s in range(SLOTS):
                    pe.wait_ge(x_loaded[s], i * 32 + 32)
                    nc.tensor.transpose(ps["x"][s][:, 0:P], xin[s][:], c["ident"][:])
                    nc.tensor.transpose(ps["x"][s][:, P:2 * P], cin[s][:], c["ident"][:]).then_inc(x_transposed, 1)
                pe_keys(nc, pe, b, wa, xT, lambda s: pe.wait_ge(xT_ready, i * SLOTS + (s + 1)))
                pe_queries(nc, pe, b, wa, xT, xT, lambda s: pe.wait_ge(cross_joined, LEAD + i * SLOTS))

            def turn(i, last):
                def banks_free(s):
                    if s in (LOGITS, COUNTS):
                        pe.wait_ge(r["rows_ready"], LEAD + i)
                pe_attention(nc, pe, b, wa, i * 2, banks_free)
                for s in range(SLOTS):
                    pe.wait_ge(x1_ready, i * SLOTS + (s + 1))
                    nc.tensor.transpose(ps["y"][s][:, 0:P], x1[s][:], c["ident"][:]).then_inc(x1_transposed, 1)
                for s in range(SLOTS):
                    pe.wait_ge(x1T_ready, i * SLOTS + (s + 1))
                    for k in range(FF1 // P):
                        step = nc.tensor.matmul(ps["x"][s][:, k * P:(k + 1) * P], lhsT=c["a_w1"][:, k * P:(k + 1) * P],
                                                rhs=x1T[s][:], start=True, stop=True)
                    step.then_inc(hidden_done, 1)
                for s in range(SLOTS):
                    pe.wait_ge(hidden_ready[s % 2], i * (SLOTS // 2) + (s // 2 + 1))
                    for k in range(FF1 // P):
                        step = nc.tensor.matmul(ps["y"][s][:, P:2 * P], lhsT=hid[s][:, k * P:(k + 1) * P],
                                                rhs=c["a_w2"][:, k, :], start=k == 0, stop=k == FF1 // P - 1)
                    step.then_inc(dense_done, 1)
                pe_keys(nc, pe, b, wx, cT, lambda s: None)
                for s in range(SLOTS):
                    pe.wait_ge(x2_ready, LEAD + i * SLOTS + (s + 1))
                    nc.tensor.transpose(ps["y"][s][:, 0:P], x2[s][:], c["ident"][:]).then_inc(x2_transposed, 1)
                pe_queries(nc, pe, b, wx, [t[:] for t in x2T], cT, lambda s: pe.wait_ge(x2T_ready, i * SLOTS + (s + 1)))
                pe_attention(nc, pe, b, wx, i * 2 + 1)
                if not last:
                    front(i + 1)
                for s in range(SLOTS):
                    pe.wait_ge(x3_ready, i * SLOTS + (s + 1))
                    if not last:
                        pe.wait_ge(b["k_ready"], (i * 2 + 2) * SLOTS + (s + 1))
                    nc.tensor.transpose(ps["x"][s][:, 0:P], x3[s][:], c["ident"][:]).then_inc(x3_transposed, 1)
                pe.wait_ge(x3T_ready, i * SLOTS + SLOTS)
                pe_logits(nc, pe, r, ps["x"], [t[:] for t in x3T], c["gate0"])
                pe_count(nc, pe, r, c, ps["x"], i)

            pe.wait_ge(buffers_set, 1)
            front(0)
            with pe.Fori(0, TURNS - 1) as i:
                turn(i, False)
            turn(TURNS - 1, True)

        @block.scalar
        def _(act):
            def front(i):
                for s in range(SLOTS):
                    act.wait_ge(x_transposed, i * SLOTS + (s + 1))
                    act.wait_ge(ctx_saved[s], LEAD + i * 16)
                    nc.scalar.activation(xc[s][:], ps["x"][s][:, 0:2 * P], ACT.Copy).then_inc(xT_ready, 1)
                act_keys(nc, act, b, wa, i * 2)

            def turn(i, last):
                act_attention(nc, act, b, i * 2)
                for s in range(SLOTS):
                    act.wait_ge(x1_transposed, i * SLOTS + (s + 1))
                    nc.scalar.activation(x1T[s][:], ps["y"][s][:, 0:P], ACT.Copy).then_inc(x1T_ready, 1)
                for s in range(0, SLOTS, 2):
                    act.wait_ge(hidden_done, i * SLOTS + (s + 1))
                    for k in range(FF1 // P):
                        step = nc.scalar.activation(hid[s][:, k * P:(k + 1) * P], ps["x"][s][:, k * P:(k + 1) * P],
                                                    ACT.Relu, bias=c["a_b1"][:, k:k + 1])
                    step.then_inc(hidden_ready[0], 1)
                act_keys(nc, act, b, wx, i * 2 + 1)
                for s in range(SLOTS):
                    act.wait_ge(x2_transposed, i * SLOTS + (s + 1))
                    nc.scalar.activation(x2T[s][:], ps["y"][s][:, 0:P], ACT.Copy).then_inc(x2T_ready, 1)
                act_attention(nc, act, b, i * 2 + 1)
                if not last:
                    front(i + 1)
                for s in range(SLOTS):
                    act.wait_ge(x3_transposed, i * SLOTS + (s + 1))
                    nc.scalar.activation(x3T[s][:], ps["x"][s][:, 0:P], ACT.Copy).then_inc(x3T_ready, 1)
                act_route(nc, act, r, i)

            front(0)
            with act.Fori(0, TURNS - 1) as i:
                turn(i, False)
            turn(TURNS - 1, True)

        @block.gpsimd
        def _(pool):
            with pool.Fori(0, TURNS) as i:
                for s in range(SLOTS):
                    pool.wait_ge(x_loaded[s], i * 32 + 32)
                    nc.gpsimd.tensor_tensor(x_bo[s][:], xin[s][:], c["a_bo"][:], ALU.add)
                    nc.gpsimd.tensor_tensor(x_ln2b[s][:], xin[s][:], c["ln2_b"][:], ALU.add).then_inc(x_summed, 1)
                pool_norm(nc, pool, nrm, c, i * 4)
                for s in range(SLOTS):
                    pool.wait_ge(x1_ready, i * SLOTS + (s + 1))
                    nc.gpsimd.tensor_tensor(x1_b2[s][:], x1[s][:], c["a_b2"][:], ALU.add).then_inc(x1_b2_ready, 1)
                pool_norm(nc, pool, nrm, c, i * 4 + 1)
                pool_norm(nc, pool, nrm, c, i * 4 + 2)
                for s in range(SLOTS):
                    pool.wait_ge(x2_ready, LEAD + i * SLOTS + (s + 1))
                    nc.gpsimd.tensor_tensor(x2_bo[s][:], x2[s][:], c["x_bo"][:], ALU.add).then_inc(x2_bo_ready, 1)
                pool_norm(nc, pool, nrm, c, i * 4 + 3)
                pool_scatter(nc, pool, r, c, i, x3, scr["sorted0"])
                pool_scattered(pool, r, i)

        @block.vector
        def _(dve):
            for s in range(SLOTS):
                nc.vector.memset(b["va"][s][:], 0.0)
            nc.vector.tensor_copy(keep["route0"]["taken"][:], c["row_base"][:]).then_inc(buffers_set, 1)
            dve.wait_ge(buffers_set, 1)
            for s in range(SLOTS):
                last = nc.vector.memset(b["va"][s][:, :, DH:DH + 1], 1.0)
            last.then_inc(buffers_set, 1)
            dve.wait_ge(buffers_set, 2)
            def join(i, products, residual, joined, done, mark):
                steps = []
                for s in range(SLOTS):
                    dve.wait_ge(products, done + (s + 1))
                    dve.wait_ge(joined, i * SLOTS + (s + 1))
                    steps.append(mark(s, nc.vector.tensor_tensor(sub[s][:], ps["y"][s][:, P:2 * P], residual[s][:], ALU.add)))
                return steps

            def turn(i, last):
                chain = Chain(dve, dve_step, i, LINKS1)
                sub_all = [t[:] for t in sub]
                dve_attention(nc, dve, b, wa, i * 2, chain)
                step = join(i, b["attn_done"], x_bo, x_summed, i * (2 * SLOTS), lambda s, ins: chain.mark(ins))
                dve_norm(nc, dve, nrm, chain, i * 4, sub_all, step, [t[:] for t in x1],
                         (c["ln1_g"], [c["ln1_b"][:]] * SLOTS), done=(x1_ready, i, 0))
                for s in range(1, SLOTS, 2):
                    dve.wait_ge(hidden_done, i * SLOTS + (s + 1))
                    for k in range(FF1 // P):
                        step = nc.vector.tensor_scalar(hid[s][:, k * P:(k + 1) * P], ps["x"][s][:, k * P:(k + 1) * P],
                                                       c["a_b1"][:, k:k + 1], 0.0, ALU.add, ALU.max)
                    step.then_inc(hidden_ready[1], 1)
                step = join(i, dense_done, x1_b2, x1_b2_ready, i * SLOTS, lambda s, ins: chain.mark(ins))
                step = dve_norm(nc, dve, nrm, chain, i * 4 + 1, sub_all, step, sub_all, (c["ln2_g"], [t[:] for t in x_ln2b]))
                dve_norm(nc, dve, nrm, chain, i * 4 + 2, sub_all, step, [t[:] for t in x2], done=(x2_ready, i, LEAD))
                dve_queries(nc, dve, b, wx, i * 2 + 1, chain)
                dve_attention(nc, dve, b, wx, i * 2 + 1, chain)

                def joined(s, ins):
                    ins.then_inc(cross_joined, 1)
                    return cross_joined, LEAD + i * SLOTS + (s + 1)
                step = join(i, b["attn_done"], x2_bo, x2_bo_ready, i * (2 * SLOTS) + SLOTS, joined)

                def x3_free(s):
                    dve.wait_ge(x3_saved[s], LEAD + i * 16)
                    dve.wait_ge(r["rows_free"], LEAD + i * SLOTS)
                step = dve_norm_begin(nc, dve, nrm, chain, sub_all, step)
                if not last:
                    dve_queries(nc, dve, b, wa, i * 2 + 2, chain, slots=range(0, 1))
                dve_norm_end(nc, dve, nrm, chain, i * 4 + 3, sub_all, step, [t[:] for t in x3],
                             free=x3_free, done=(x3_ready, i, 0))
                if not last:
                    dve_queries(nc, dve, b, wa, i * 2 + 2, chain, slots=range(1, SLOTS))
                dve_route(nc, dve, r, c, chain, i, ps["x"], None, keep["route0"])
                chain.close()

            dve_queries(nc, dve, b, wa, 0, None)
            with dve.Fori(0, TURNS - 1) as i:
                turn(i, False)
            turn(TURNS - 1, True)



def phase_table(nc, c, kept, tag, sorted_rows):
    with Phase(nc) as ctx:
        def sb(name, shape, dt=F32):
            return ctx.enter_context(nc.sbuf_tensor(f"{tag}_{name}", shape, dt))

        def sem(name, lead=0):
            return ctx.sem(f"{tag}_{name}", lead)

        tiles, picks = kept["tiles"], kept["picks"]
        need_f, need_i, need = sb("need_f", [P, EXPERTS]), sb("need_i", [P, EXPERTS], I32), sb("need", [P, EXPERTS])
        pad_f, pad = sb("pad_f", [P, EXPERTS]), sb("pad", [P, EXPERTS], U32)
        end, last = sb("end", [P, EXPERTS]), sb("last", [P, 1])
        tile, past = sb("tile", [P, tiles]), sb("past", [P, tiles, EXPERTS])
        weighed, expert, first = sb("weighed", [P, tiles, EXPERTS]), sb("expert", [P, tiles]), sb("first", [P, tiles])
        row = sb("row", [P, tiles])
        shift, jump = sb("shift", [P, EXPERTS]), sb("jump", [P, EXPERTS])
        n_rows = BATCH * picks
        over, moved, out_f = sb("over", [P, n_rows, EXPERTS]), sb("moved", [P, n_rows]), sb("out_f", [P, n_rows])
        pad_ready, padded, step_sem = sem("pad_ready"), sem("padded"), sem("step")
        block = ctx.enter_context(nc.Block())

        @block.vector
        def _(dve):
            count = [0]

            def step(ins):
                ins.then_inc(step_sem, 1)
                count[0] += 1
                dve.wait_ge(step_sem, count[0])

            ones = c["one_row"][:, 0:EXPERTS]
            step(nc.vector.tensor_scalar(pad_f[:], kept["taken"][:], c["part_iota"][:], None, ALU.add))
            nc.vector.tensor_copy(pad[:], pad_f[:]).then_inc(pad_ready, 1)
            step(nc.vector.tensor_tensor(need_f[:], kept["taken"][:], c["row_base"][:], ALU.subtract))
            step(nc.vector.tensor_scalar_add(need_f[:], need_f[:], float(P - 1)))
            step(nc.vector.tensor_copy(need_i[:], need_f[:]))
            step(nc.vector.tensor_scalar(need_i[:], need_i[:], 7, None, ALU.arith_shift_right))
            step(nc.vector.tensor_copy(need[:], need_i[:]))
            step(nc.vector.tensor_tensor_scan(end[:], ones, need[:], 0.0, ALU.mult, ALU.add))
            step(nc.vector.tensor_scalar_add(last[:], end[:, EXPERTS - 1:EXPERTS], -1.0))
            step(nc.vector.tensor_scalar(tile[:], c["iota_tiles"][:, 0:tiles], last[:], None, ALU.min))
            step(nc.vector.tensor_tensor(past[:], bcast(tile[:], EXPERTS), repeat(end[:], tiles), ALU.is_ge))
            step(nc.vector.reduce_sum(expert[:], past[:], AX.X))
            step(nc.vector.tensor_tensor(weighed[:], past[:], repeat(need[:], tiles), ALU.mult))
            step(nc.vector.reduce_sum(first[:], weighed[:], AX.X))
            step(nc.vector.tensor_tensor(tile[:], tile[:], first[:], ALU.subtract))
            step(nc.vector.tensor_scalar_mul(row[:], expert[:], float(REGION)))
            step(nc.vector.scalar_tensor_tensor(out=row[:], in0=tile[:], scalar=float(P), in1=row[:],
                                                op0=ALU.mult, op1=ALU.add))
            nc.vector.tensor_copy(kept["tile_expert"][:], expert[:])
            nc.vector.tensor_copy(kept["tile_row"][:], row[:])
            step(nc.vector.tensor_tensor(shift[:], end[:], need[:], ALU.subtract))
            step(nc.vector.scalar_tensor_tensor(out=shift[:], in0=shift[:], scalar=float(P), in1=c["row_base"][:],
                                                op0=ALU.mult, op1=ALU.subtract))
            nc.vector.tensor_copy(jump[:, 0:1], shift[:, 0:1])
            step(nc.vector.tensor_tensor(jump[:, 1:EXPERTS], shift[:, 1:EXPERTS], shift[:, 0:EXPERTS - 1], ALU.subtract))
            rows = kept["rows"][:, 0:BATCH, :].rearrange("p n k -> p (n k)")
            step(nc.vector.tensor_tensor(over[:], bcast(rows, EXPERTS), repeat(c["row_base"][:], n_rows), ALU.is_ge))
            step(nc.vector.tensor_tensor(over[:], over[:], repeat(jump[:], n_rows), ALU.mult))
            step(nc.vector.reduce_sum(moved[:], over[:], AX.X))
            step(nc.vector.tensor_tensor(out_f[:], moved[:], rows, ALU.add))
            nc.vector.memset(kept["weights"][:, BATCH:, :], 0.0)
            nc.vector.memset(kept["out_rows"][:, BATCH:, :], 0)
            step(nc.vector.tensor_copy(kept["out_rows"][:, 0:BATCH, :].rearrange("p n k -> p (n k)"), out_f[:]))

        @block.gpsimd
        def _(pool):
            pool.wait_ge(pad_ready, 1)
            for e in range(EXPERTS):
                nc.gpsimd.indirect_dma_start(out=sorted_rows, out_offset=bass.IndirectOffsetOnAxis(ap=pad[:, e:e + 1], axis=0),
                                             in_=c["zeros"][:], in_offset=None).then_inc(padded, 16)
            pool.wait_ge(padded, 16 * EXPERTS)



def expert_buffers(nc, ctx, tag, down):
    def sb(name, shape):
        return ctx.enter_context(nc.sbuf_tensor(name + tag, shape, F32))
    return dict(up=sb("up", [P, EXPERTS, FF1]), up_b=sb("up_b", [P, EXPERTS, FF1]),
                 down=sb("down", [P, EXPERTS, down, P]), down_b=sb("down_b", [P, EXPERTS, P]))


def load_experts(sp, keep, e, d, names):
    up, down, up_b, down_b = names
    sp.dma_start(e["up"][:], d[up]).then_inc(keep["experts_loaded"], 16)
    sp.dma_start(e["down"][:], d[down]).then_inc(keep["experts_loaded"], 16)
    sp.dma_start(e["up_b"][:], d[up_b].partition_broadcast(P)).then_inc(keep["experts_loaded"], 16)
    sp.dma_start(e["down_b"][:], d[down_b].partition_broadcast(P)).then_inc(keep["experts_loaded"], 16)


def phase_experts(nc, c, keep, kept, e, tag, gated, sorted_rows, out_rows, loaded):
    with Phase(nc) as ctx:
        def sb(name, shape, dt=F32):
            return [ctx.enter_context(nc.sbuf_tensor(f"{tag}_{name}{s}", shape, dt)) for s in range(SLOTS)]

        def sem(name, lead=0):
            return ctx.sem(f"{tag}_{name}", lead)

        wide = [ctx.enter_context(nc.psum_tensor(f"{tag}_wide{s}", [P, FF1], F32)) for s in range(SLOTS)]
        turned_rows, sums = ([ctx.enter_context(nc.psum_tensor(f"{tag}_{name}{s}", [P, 512], F32)) for s in range(2)]
                             for name in ("turned_rows", "sums"))
        hidden = FF0 if gated else FF1
        blocks = hidden // P
        rows, rowsT, pre, h, hT, y = (sb("rows", [P, P]), sb("rowsT", [P, P]), sb("pre", [P, FF1]), sb("h", [P, FF1]),
                                      sb("hT", [P, hidden]), sb("y", [P, P]))
        rows_loaded, y_saved = [sem(f"rows_loaded{s}") for s in range(SLOTS)], [sem(f"y_saved{s}", LEAD) for s in range(SLOTS)]
        rows_transposed, rowsT_ready, up_done, pre_ready = (sem("rows_transposed"), sem("rowsT_ready"), sem("up_done"),
                                                            sem("pre_ready"))
        act_ready, h_ready, h_transposed, hT_ready = sem("act_ready"), sem("h_ready"), sem("h_transposed"), sem("hT_ready")
        down_done, y_ready = sem("down_done"), sem("y_ready", LEAD)
        tiles = kept["tiles"]
        last_turn = tiles // SLOTS - 1
        block = ctx.enter_context(nc.Block())

        def experts_of(eng, i, part):
            registers = [eng.alloc_register(f"{tag}_{part}_expert{s}") for s in range(SLOTS)]
            eng.load(registers, kept["tile_expert"][0:1, bass.ds(i * SLOTS, SLOTS)])
            return [eng.snap(r, donate=True).with_bounds(min_val=0, max_val=EXPERTS - 1) for r in registers]

        @block.sync
        def _(sp):
            give_leads(sp, ctx)

            def load(i, k):
                if not (isinstance(i, int) and i * SLOTS + k < SLOTS):
                    sp.wait_ge(rows_transposed, i * SLOTS + (k - SLOTS + 1))
                row = sp.value_load(kept["tile_row"][0:1, bass.ds(i * SLOTS + k, 1)], min_val=0,
                                    max_val=EXPERTS * REGION - P)
                sp.dma_start(rows[k % SLOTS][:], sorted_rows[bass.ds(row, P), :]).then_inc(rows_loaded[k % SLOTS], 16)

            def store(i, k):
                sp.wait_ge(y_ready, LEAD + i * SLOTS + (k + 1))
                sp.dma_start(out_rows[bass.ds((i * SLOTS + k) * P, P), :], y[k % SLOTS][:]).then_inc(y_saved[k % SLOTS], 16)

            for k in range(SLOTS + 3):
                load(0, k)
            with sp.Fori(0, last_turn - 1) as i:
                for k in range(SLOTS):
                    load(i, k + SLOTS + 3)
                    store(i, k)
            load(last_turn - 1, SLOTS + 3)
            for k in range(2 * SLOTS):
                store(last_turn - 1, k)
            for s in range(SLOTS):
                sp.wait_ge(y_saved[s], LEAD + 16 * (last_turn + 1))

        @block.tensor
        def _(pe):
            def turned(i, k):
                pe.wait_ge(rows_loaded[k % SLOTS], (i + k // SLOTS) * 16 + 16)
                nc.tensor.transpose(turned_rows[k % 2][:, 0:P], rows[k % SLOTS][:], c["ident"][:]).then_inc(rows_transposed, 1)

            def up(i, k, experts):
                pe.wait_ge(rowsT_ready, i * SLOTS + (k + 1))
                nc.tensor.matmul(wide[k % SLOTS][:], lhsT=rowsT[k % SLOTS][:], rhs=tile_of(e["up"], experts[k]),
                                 start=True, stop=True).then_inc(up_done, 1)

            def hidden_turned(i, k):
                pe.wait_ge(h_ready, i * SLOTS + (k + 1))
                for n in range(blocks):
                    last = nc.tensor.transpose(wide[k % SLOTS][:, n * P:(n + 1) * P], h[k % SLOTS][:, n * P:(n + 1) * P],
                                               c["ident"][:])
                last.then_inc(h_transposed, 1)

            def down(i, k, experts):
                pe.wait_ge(hT_ready, i * SLOTS + (k + 1))
                pe.wait_ge(y_ready, LEAD + i * SLOTS + max(k - 1, 0))
                for n in range(blocks):
                    last = nc.tensor.matmul(
                        sums[k % 2][:, 0:P], lhsT=hT[k % SLOTS][:, n * P:(n + 1) * P],
                        rhs=e["down"][:, bass.ds(experts[k], 1), n, :].rearrange("p o n -> p (o n)"),
                        start=n == 0, stop=n == blocks - 1)
                last.then_inc(down_done, 1)

            pe.wait_ge(keep["experts_loaded"], loaded)
            experts = experts_of(pe, 0, "first")
            turned(0, 0)
            turned(0, 1)
            up(0, 0, experts)
            turned(0, 2)
            up(0, 1, experts)
            turned(0, 3)
            hidden_turned(0, 0)
            with pe.Fori(0, last_turn) as i:
                experts = experts_of(pe, i, "middle")
                for k in range(2, SLOTS + 2):
                    up(i, k, experts)
                    if k == SLOTS - 1:
                        experts += experts_of(pe, i + 1, "next")
                    turned(i, k + 2)
                    hidden_turned(i, k - 1)
                    down(i, k - 2, experts)
            experts = experts_of(pe, last_turn, "last")
            up(last_turn, 2, experts)
            hidden_turned(last_turn, 1)
            down(last_turn, 0, experts)
            up(last_turn, 3, experts)
            hidden_turned(last_turn, 2)
            down(last_turn, 1, experts)
            hidden_turned(last_turn, 3)
            down(last_turn, 2, experts)
            down(last_turn, 3, experts)

        @block.vector
        def _(dve):
            def rows_kept(i, k):
                dve.wait_ge(rows_transposed, i * SLOTS + (k + 1))
                nc.vector.tensor_copy(rowsT[k % SLOTS][:], turned_rows[k % 2][:, 0:P]).then_inc(rowsT_ready, 1)

            def biased(i, k, experts):
                dve.wait_ge(up_done, i * SLOTS + (k + 1))
                nc.vector.tensor_tensor(pre[k % SLOTS][:], wide[k % SLOTS][:], tile_of(e["up_b"], experts[k]), ALU.add)\
                    .then_inc(pre_ready, 1)

            def gated_by(i, k):
                if gated:
                    dve.wait_ge(act_ready, i * SLOTS + (k + 1))
                    nc.vector.tensor_tensor(h[k % SLOTS][:, 0:FF0], h[k % SLOTS][:, 0:FF0], pre[k % SLOTS][:, FF0:2 * FF0],
                                            ALU.mult).then_inc(h_ready, 1)

            def hidden_kept(i, k):
                dve.wait_ge(h_transposed, i * SLOTS + (k + 1))
                nc.vector.tensor_copy(hT[k % SLOTS][:], wide[k % SLOTS][:, 0:hidden]).then_inc(hT_ready, 1)

            def output(i, k, experts):
                dve.wait_ge(down_done, i * SLOTS + (k + 1))
                dve.wait_ge(y_saved[k % SLOTS], LEAD + (i + k // SLOTS) * 16)
                nc.vector.tensor_tensor(y[k % SLOTS][:], sums[k % 2][:, 0:P], tile_of(e["down_b"], experts[k]), ALU.add)\
                    .then_inc(y_ready, 1)

            experts = experts_of(dve, 0, "first")
            rows_kept(0, 0)
            rows_kept(0, 1)
            biased(0, 0, experts)
            rows_kept(0, 2)
            gated_by(0, 0)
            biased(0, 1, experts)
            rows_kept(0, 3)
            hidden_kept(0, 0)
            with dve.Fori(0, last_turn) as i:
                experts = experts_of(dve, i, "middle")
                for k in range(2, SLOTS + 2):
                    gated_by(i, k - 1)
                    biased(i, k, experts)
                    if k == SLOTS - 1:
                        experts += experts_of(dve, i + 1, "next")
                    rows_kept(i, k + 2)
                    hidden_kept(i, k - 1)
                    output(i, k - 2, experts)
            experts = experts_of(dve, last_turn, "last")
            gated_by(last_turn, 1)
            biased(last_turn, 2, experts)
            hidden_kept(last_turn, 1)
            output(last_turn, 0, experts)
            gated_by(last_turn, 2)
            biased(last_turn, 3, experts)
            hidden_kept(last_turn, 2)
            output(last_turn, 1, experts)
            gated_by(last_turn, 3)
            hidden_kept(last_turn, 3)
            output(last_turn, 2, experts)
            output(last_turn, 3, experts)

        @block.scalar
        def _(act):
            def turn(i):
                for s in range(SLOTS):
                    act.wait_ge(pre_ready, i * SLOTS + (s + 1))
                    if gated:
                        nc.scalar.activation(h[s][:, 0:FF0], pre[s][:, 0:FF0], ACT.Silu).then_inc(act_ready, 1)
                    else:
                        nc.scalar.activation(h[s][:], pre[s][:], ACT.Gelu_apprx_tanh).then_inc(h_ready, 1)

            turn(0)
            with act.Fori(0, last_turn) as i:
                turn(i + 1)



def gather_buffers(nc, ctx, tag, picks, sets=1):
    def sb(name, shape, dt=F32):
        return [ctx.enter_context(nc.sbuf_tensor(f"{tag}_{name}{h}", shape, dt)) for h in range(sets)]
    return dict(picks=picks, rows=sb("g_rows", [P, SLOTS, picks], U32), weights=sb("g_weights", [P, SLOTS, picks]),
                y=[[[ctx.enter_context(nc.sbuf_tensor(f"{tag}_g_y{h}_{q}_{s}", [P, P], F32)) for s in range(SLOTS)]
                    for q in range(picks)] for h in range(sets)],
                rows_ready=ctx.sem(f"{tag}_g_rows_ready"),
                gathered=[[ctx.sem(f"{tag}_g_gathered{h}_{s}") for s in range(SLOTS)] for h in range(sets)])


def pool_gather(nc, pool, g, c, kept, turn, src, h=0):
    nc.gpsimd.tensor_copy(g["weights"][h][:], kept["weights"][:, bass.ds(turn * SLOTS, SLOTS), :])
    nc.gpsimd.tensor_copy(g["rows"][h][:], kept["out_rows"][:, bass.ds(turn * SLOTS, SLOTS), :]).then_inc(g["rows_ready"], 1)
    pool.wait_ge(g["rows_ready"], turn + 1)
    stand_alone(pool, c)
    for s in range(SLOTS):
        for q in range(g["picks"]):
            nc.gpsimd.indirect_dma_start(out=g["y"][h][q][s][:], out_offset=None, in_=src,
                                         in_offset=bass.IndirectOffsetOnAxis(ap=g["rows"][h][:, s, q:q + 1], axis=0))\
                .then_inc(g["gathered"][h][s], 16)



LINKS3 = 24


def phase_decode(nc, c, d, keep, scr, xT_all, experts1):
    with Phase(nc) as ctx:
        def sb(name, shape, dt=F32):
            return [ctx.enter_context(nc.sbuf_tensor(f"d_{name}{s}", shape, dt)) for s in range(SLOTS)]

        def sem(name, lead=0):
            return ctx.sem("d_" + name, lead)

        ps = banks(nc, ctx, "d")
        b = attention_buffers(nc, ctx, "d", ps, rope=True)
        nrm = norm_buffers(nc, ctx, "d", c)
        g = gather_buffers(nc, ctx, "d", 2)
        w = dict(wq=c["l_wq"], wqp=c["l_wqp"], wk=c["l_wk"], wkp=c["l_wkp"], wv=c["l_wv"], wo=c["l_wo"], bias=c["causal"], bk_by_group=c["zeros"],
                  bias_by_head=False, rope=True, ident=c["ident"], mask_q=c["mask_q"], mask_k=c["mask_k"],
                  cos=c["cos"], sin=c["sin"])
        x3, sub4, x4, x4T, x4_bo = sb("x3", [P, P]), sb("sub4", [P, P]), sb("x4", [P, P]), sb("x4T", [P, P]), sb("x4_bo", [P, P])
        sub5, x5 = sb("sub5", [P, P]), sb("x5", [P, P])
        x3_loaded = [sem(f"x3_loaded{s}") for s in range(SLOTS)]
        joined, x4_ready, x4_transposed, x4T_ready = sem("joined"), sem("x4_ready"), sem("x4_transposed"), sem("x4T_ready")
        x4_bo_ready, attn_joined = sem("x4_bo_ready"), sem("attn_joined", LEAD)
        x5_ready, x5_transposed, x5T_ready = sem("x5_ready"), sem("x5_transposed"), sem("x5T_ready")
        dve_step, first_step, buffers_set = sem("dve_step"), sem("first_step"), sem("buffers_set")
        block = ctx.enter_context(nc.Block())

        @block.sync
        def _(sp):
            give_leads(sp, ctx)

            def load(i):
                for s in range(SLOTS):
                    sp.dma_start(x3[s][:], dram_tile(scr["x3"], i * SLOTS + s)).then_inc(x3_loaded[s], 16)

            load(0)
            sp.wait_ge(joined, SLOTS)
            load_experts(sp, keep, experts1, d, ("s_w1", "s_w2", "s_b1", "s_b2"))
            with sp.Fori(0, TURNS - 1) as i:
                sp.wait_ge(joined, i * SLOTS + SLOTS)
                load(i + 1)

        @block.gpsimd
        def _(pool):
            def gather(i):
                pool_gather(nc, pool, g, c, keep["route0"], i, scr["expert_out0"])

            def with_bias(i):
                for s in range(SLOTS):
                    pool.wait_ge(x4_ready, i * SLOTS + (s + 1))
                    pool.wait_ge(attn_joined, LEAD + i * SLOTS)
                    nc.gpsimd.tensor_tensor(x4_bo[s][:], x4[s][:], c["l_bo"][:], ALU.add).then_inc(x4_bo_ready, 1)

            gather(0)
            pool_norm(nc, pool, nrm, c, 0)
            with_bias(0)
            pool.wait_ge(joined, SLOTS)
            stand_alone(pool, c)
            gather(1)
            with pool.Fori(0, TURNS - 1) as i:
                pool_norm(nc, pool, nrm, c, i * 2 + 1)
                pool.wait_ge(joined, i * SLOTS + 2 * SLOTS)
                stand_alone(pool, c)
                gather(i + 2)
                pool_norm(nc, pool, nrm, c, i * 2 + 2)
                with_bias(i + 1)
            pool_norm(nc, pool, nrm, c, 2 * TURNS - 1)
            for s in range(SLOTS):
                pool.wait_ge(g["gathered"][0][s], 32 * (TURNS + 1))

        @block.tensor
        def _(pe):
            def front(i):
                for s in range(SLOTS):
                    pe.wait_ge(x4_ready, i * SLOTS + (s + 1))
                    nc.tensor.transpose(ps["x"][s][:, 0:P], x4[s][:], c["ident"][:]).then_inc(x4_transposed, 1)

                def ready(s):
                    pe.wait_ge(x4T_ready, i * SLOTS + (s + 1))
                    pe.wait_ge(attn_joined, LEAD + i * SLOTS)
                pe_queries(nc, pe, b, w, [t[:] for t in x4T], [t[:] for t in x4T], ready)

            def x5_turned(i, s, after_front):
                pe.wait_ge(x5_ready, i * SLOTS + (s + 1))
                if after_front:
                    pe.wait_ge(b["v_ready"], i * SLOTS + (SLOTS + s + 1))
                nc.tensor.transpose(ps["y"][s][:, 0:P], x5[s][:], c["ident"][:]).then_inc(x5_transposed, 1)

            def turn(i, first, last):
                if first:
                    pe_attention(nc, pe, b, w, i)
                else:
                    pe_attention(nc, pe, b, w, i, first_mix=lambda s: pe.wait_ge(x5T_ready, (i - 1) * SLOTS + (s + 1)),
                                 beside=lambda k: k < SLOTS and x5_turned(i - 1, k, True))
                if not last:
                    front(i + 1)

            pe.wait_ge(buffers_set, 2)
            front(0)
            turn(0, True, False)
            with pe.Fori(0, TURNS - 2) as i:
                turn(i + 1, False, False)
            turn(TURNS - 1, False, True)
            for s in range(SLOTS):
                x5_turned(TURNS - 1, s, False)

        @block.scalar
        def _(act):
            def front(i):
                for s in range(SLOTS):
                    act.wait_ge(x4_transposed, i * SLOTS + (s + 1))
                    nc.scalar.activation(x4T[s][:], ps["x"][s][:, 0:P], ACT.Copy).then_inc(x4T_ready, 1)
                act_keys(nc, act, b, w, i)

            def x5T_kept(i, s):
                act.wait_ge(x5_transposed, i * SLOTS + (s + 1))
                nc.scalar.activation(tile_of(xT_all, i * SLOTS + s), ps["y"][s][:, 0:P], ACT.Copy).then_inc(x5T_ready, 1)

            def turn(i, first, last):
                act_attention(nc, act, b, i, None if first else lambda k: k < SLOTS and x5T_kept(i - 1, k))
                if not last:
                    front(i + 1)

            front(0)
            turn(0, True, False)
            with act.Fori(0, TURNS - 2) as i:
                turn(i + 1, False, False)
            turn(TURNS - 1, False, True)
            for s in range(SLOTS):
                x5T_kept(TURNS - 1, s)
            act.wait_ge(x5T_ready, BATCH)

        @block.vector
        def _(dve):
            for s in range(SLOTS):
                last = nc.vector.memset(b["va"][s][:], 0.0)
            last.then_inc(buffers_set, 1)
            dve.wait_ge(buffers_set, 1)
            for s in range(SLOTS):
                last = nc.vector.memset(b["va"][s][:, :, DH:DH + 1], 1.0)
            last.then_inc(buffers_set, 1)

            sub4_all, sub5_all = [t[:] for t in sub4], [t[:] for t in sub5]

            def first_expert(i, chain, s):
                dve.wait_ge(x3_loaded[s], i * 16 + 16)
                dve.wait_ge(g["gathered"][0][s], i * 32 + 32)
                return chain.mark(nc.vector.scalar_tensor_tensor(
                    out=sub4[s][:], in0=g["y"][0][0][s][:], scalar=g["weights"][0][:, s, 0:1], in1=x3[s][:],
                    op0=ALU.mult, op1=ALU.add))

            def second_expert(i, chain, step, s):
                chain.wait(step)
                nc.vector.scalar_tensor_tensor(
                    out=sub4[s][:], in0=g["y"][0][1][s][:], scalar=g["weights"][0][:, s, 1:2], in1=sub4[s][:],
                    op0=ALU.mult, op1=ALU.add).then_inc(joined, 1)
                return joined, i * SLOTS + (s + 1)

            def x4_made(i, chain, index, steps):
                def x4_free(s):
                    if not isinstance(i, int):
                        dve.wait_ge(x4_bo_ready, i * SLOTS)
                dve_norm_end(nc, dve, nrm, chain, index, sub4_all, steps, [t[:] for t in x4], free=x4_free,
                             done=(x4_ready, i, 0))

            def turn(i, last):
                chain = Chain(dve, dve_step, i, LINKS3)
                steps = [None] * SLOTS

                def next_x4(k):
                    nonlocal steps
                    if 2 <= k < 2 + SLOTS:
                        steps[k - 2] = first_expert(i + 1, chain, k - 2)
                    elif 2 + SLOTS <= k < 2 + 2 * SLOTS:
                        steps[k - 2 - SLOTS] = second_expert(i + 1, chain, steps[k - 2 - SLOTS], k - 2 - SLOTS)
                    elif k == 2 + 2 * SLOTS:
                        steps = dve_norm_begin(nc, dve, nrm, chain, sub4_all, steps)
                    elif k == 4 + 2 * SLOTS:
                        x4_made(i + 1, chain, i * 2 + 1, steps)

                dve_attention(nc, dve, b, w, i, chain, None if last else next_x4)
                joins = []
                for s in range(SLOTS):
                    dve.wait_ge(b["attn_done"], i * SLOTS + (s + 1))
                    dve.wait_ge(x4_bo_ready, i * SLOTS + (s + 1))
                    nc.vector.tensor_tensor(sub5[s][:], ps["y"][s][:, P:2 * P], x4_bo[s][:], ALU.add).then_inc(attn_joined, 1)
                    joins.append((attn_joined, LEAD + i * SLOTS + (s + 1)))
                joins = dve_norm_begin(nc, dve, nrm, chain, sub5_all, joins)
                if not last:
                    dve_queries(nc, dve, b, w, i + 1, chain)
                dve_norm_end(nc, dve, nrm, chain, 2 * TURNS - 1 if last else i * 2 + 2, sub5_all, joins,
                             [t[:] for t in x5], done=(x5_ready, i, 0))
                if not last:
                    chain.close()

            chain = Chain(dve, first_step, 0, 0)
            steps = [first_expert(0, chain, s) for s in range(SLOTS)]
            steps = [second_expert(0, chain, steps[s], s) for s in range(SLOTS)]
            steps = dve_norm_begin(nc, dve, nrm, chain, sub4_all, steps)
            x4_made(0, chain, 0, steps)
            dve_queries(nc, dve, b, w, 0, chain)
            with dve.Fori(0, TURNS - 1) as i:
                turn(i, False)
            turn(TURNS - 1, True)



CHUNK = 4
CHUNKS = BATCH // CHUNK


def phase_recurrent(nc, c, d, scr, xT_all, states):
    with Phase(nc) as ctx:
        def sb(name, shape, dt=F32):
            return ctx.enter_context(nc.sbuf_tensor("n_" + name, shape, dt))

        def sem(name, lead=0):
            return ctx.sem("n_" + name, lead)

        gates, drive = sb("gates", [P, P, BATCH]), sb("drive", [P, P, BATCH])
        wi, wg, wa, wb = (sb(n, [P, P]) for n in ("wi", "wg", "wa", "wb"))
        bi, bg, decay = (sb(n, [P, 1]) for n in ("bi", "bg", "decay"))
        squares = sb("squares", [P, BATCH, P])
        mem, kept, inp, gate, part, blend = ([sb(f"{n}{k}", [P, CHUNK * P]) for k in range(2)]
                                                 for n in ("mem", "kept", "inp", "gate", "part", "blend"))
        gated = [sb(f"gated{k}", [P, BATCH]) for k in range(2)]
        pi, pg, pc = ([ctx.enter_context(nc.psum_tensor(f"n_{n}{k}", [P, 512], F32)) for k in range(2)]
                      for n in ("pi", "pg", "pc"))
        pz = [ctx.enter_context(nc.psum_tensor(f"n_pz{k}", [P, 512], F32)) for k in range(2)]
        w_loaded, ctx_loaded = sem("w_loaded"), [sem(f"ctx_loaded{k}") for k in range(CHUNKS)]
        squared, scanned, kept_ready, inp_done, inp_ready = (sem(n) for n in ("squared", "scanned", "kept_ready",
                                                                              "inp_done", "inp_ready"))
        gate_done, gate_ready, part_ready, blend_ready, drive_done, drive_ready = (
            sem(n) for n in ("gate_done", "gate_ready", "part_ready", "blend_ready", "drive_done", "drive_ready"))
        gated_ready, summed, state_ready, gates_kept = (sem("gated_ready"), sem("summed"), sem("state_ready", LEAD),
                                                        sem("gates_kept"))
        block = ctx.enter_context(nc.Block())
        WEIGHTS = ((wi, "n_wi"), (wg, "n_wg"), (wa, "n_a"), (wb, "n_b"))
        COLUMNS = ((bi, "n_bi"), (bg, "n_bg"), (decay, "n_decay"))

        def of_chunk(big, k):
            return big[:, :, k * CHUNK:(k + 1) * CHUNK].rearrange("p t b -> p b t")

        @block.sync
        def _(sp):
            give_leads(sp, ctx)
            for tile, name in WEIGHTS:
                sp.dma_start(tile[:], d[name]).then_inc(w_loaded, 16)
            for tile, name in COLUMNS:
                sp.dma_start(tile[:], d[name].rearrange("(p o) -> p o", o=1)).then_inc(w_loaded, 16)
            for k in range(CHUNKS):
                sp.dma_start(squares[:, k * CHUNK:(k + 1) * CHUNK, :],
                             scr["ctxT"][k * CHUNK:(k + 1) * CHUNK].rearrange("b p t -> p b t")).then_inc(ctx_loaded[k], 16)

        @block.vector
        def _(dve):
            nc.vector.memset(gated[0][:], 0.0).then_inc(gated_ready, 1)
            dve.wait_ge(w_loaded, 16 * 7)

            def memory(k):
                dve.wait_ge(squared, k + 1)
                for q in range(CHUNK):
                    last = nc.vector.tensor_tensor_scan(mem[k % 2][:, q * P:(q + 1) * P],
                                                        decay[:].to_broadcast([P, P]),
                                                        squares[:, k * CHUNK + q, :], 0.0, ALU.mult, ALU.add)
                last.then_inc(scanned, 1)
                dve.wait_ge(scanned, k + 1)
                if k >= 2:
                    dve.wait_ge(inp_done, k - 1)
                nc.vector.tensor_tensor(kept[k % 2][:], mem[k % 2][:],
                                        xT_all[:, k * CHUNK:(k + 1) * CHUNK, :].rearrange("p b t -> p (b t)"),
                                        ALU.mult).then_inc(kept_ready, 1)

            def blended(k):
                dve.wait_ge(gate_ready, k + 1)
                if k >= 2:
                    dve.wait_ge(drive_done, k - 1)
                nc.vector.tensor_tensor(part[k % 2][:], gate[k % 2][:], inp[k % 2][:], ALU.mult).then_inc(part_ready, 1)
                dve.wait_ge(part_ready, k + 1)
                nc.vector.tensor_tensor(blend[k % 2][:], inp[k % 2][:], part[k % 2][:], ALU.subtract)\
                    .then_inc(blend_ready, 1)

            def driven(k):
                dve.wait_ge(drive_done, k + 1)
                nc.vector.tensor_copy(of_chunk(drive, k), pc[k % 2][:].rearrange("p (b t) -> p b t", b=CHUNK))\
                    .then_inc(drive_ready, 1)

            memory(0)
            memory(1)
            for k in range(CHUNKS):
                if k + 2 < CHUNKS:
                    memory(k + 2)
                blended(k)
                if k:
                    driven(k - 1)
            driven(CHUNKS - 1)
            dve.wait_ge(gates_kept, CHUNKS)
            with dve.Fori(0, P // 2 - 1) as i:
                for k in (1, 0):
                    t = i * 2 + (2 - k)
                    dve.wait_ge(state_ready, LEAD + t)
                    nc.vector.tensor_tensor(gated[k][:], tile_of(gates, t), tile_of(states, t - 1), ALU.mult)\
                        .then_inc(gated_ready, 1)
            dve.wait_ge(state_ready, LEAD + P - 1)
            nc.vector.tensor_tensor(gated[1][:], gates[:, P - 1, :], states[:, P - 2, :], ALU.mult).then_inc(gated_ready, 1)

        @block.gpsimd
        def _(pool):
            def square(k):
                pool.wait_ge(ctx_loaded[k], 16)
                chunk = squares[:, k * CHUNK:(k + 1) * CHUNK, :]
                nc.gpsimd.tensor_tensor(chunk, chunk, chunk, ALU.mult).then_inc(squared, 1)

            for k in range(3):
                square(k)
            for k in range(CHUNKS):
                if k + 3 < CHUNKS:
                    square(k + 3)
                pool.wait_ge(gate_ready, k + 1)
                nc.gpsimd.tensor_copy(of_chunk(gates, k), gate[k % 2][:].rearrange("p (b t) -> p b t", b=CHUNK))\
                    .then_inc(gates_kept, 1)

        @block.tensor
        def _(pe):
            pe.wait_ge(w_loaded, 16 * 7)

            def inputs(k):
                pe.wait_ge(kept_ready, k + 1)
                if k >= 2:
                    pe.wait_ge(inp_ready, k - 1)
                nc.tensor.matmul(pi[k % 2][:], lhsT=wi[:], rhs=kept[k % 2][:], start=True, stop=True).then_inc(inp_done, 1)

            def gating(k):
                pe.wait_ge(inp_ready, k + 1)
                if k >= 2:
                    pe.wait_ge(gate_ready, k - 1)
                nc.tensor.matmul(pg[k % 2][:], lhsT=wg[:], rhs=inp[k % 2][:], start=True, stop=True).then_inc(gate_done, 1)

            def driving(k):
                pe.wait_ge(blend_ready, k + 1)
                if k >= 2:
                    pe.wait_ge(drive_ready, k - 1)
                nc.tensor.matmul(pc[k % 2][:], lhsT=wa[:], rhs=blend[k % 2][:], start=True, stop=False)
                nc.tensor.matmul(pc[k % 2][:], lhsT=wb[:], rhs=inp[k % 2][:], start=False, stop=True).then_inc(drive_done, 1)

            inputs(0)
            inputs(1)
            gating(0)
            for k in range(CHUNKS):
                if k + 1 < CHUNKS:
                    gating(k + 1)
                if k + 2 < CHUNKS:
                    inputs(k + 2)
                driving(k)
            pe.wait_ge(drive_ready, CHUNKS)

            def driven(t, k):
                nc.tensor.matmul(pz[k][:, 0:BATCH], lhsT=c["ident"][:], rhs=tile_of(drive, t), start=True, stop=False)

            def step(t, k):
                pe.wait_ge(gated_ready, t + 1)
                nc.tensor.matmul(pz[k][:, 0:BATCH], lhsT=wa[:], rhs=gated[k][:], start=False, stop=True)\
                    .then_inc(summed, 1)

            driven(0, 0)
            with pe.Fori(0, P // 2 - 1) as i:
                for k in range(2):
                    step(i * 2 + k, k)
                    driven(i * 2 + (k + 1), 1 - k)
            step(P - 2, 0)
            driven(P - 1, 1)
            step(P - 1, 1)

        @block.scalar
        def _(act):
            act.wait_ge(w_loaded, 16 * 7)

            def inputs(k):
                act.wait_ge(inp_done, k + 1)
                if k >= 2:
                    act.wait_ge(drive_done, k - 1)
                    act.wait_ge(blend_ready, k - 1)
                nc.scalar.activation(inp[k % 2][:], pi[k % 2][:], ACT.Identity, bias=bi[:]).then_inc(inp_ready, 1)

            def gating(k):
                act.wait_ge(gate_done, k + 1)
                if k >= 2:
                    act.wait_ge(blend_ready, k - 1)
                    act.wait_ge(gates_kept, k - 1)
                nc.scalar.activation(gate[k % 2][:], pg[k % 2][:], ACT.Sigmoid, bias=bg[:]).then_inc(gate_ready, 1)

            inputs(0)
            for k in range(CHUNKS):
                gating(k)
                if k + 1 < CHUNKS:
                    inputs(k + 1)
            with act.Fori(0, P // 2) as i:
                for k in range(2):
                    t = i * 2 + k
                    act.wait_ge(summed, t + 1)
                    nc.scalar.activation(tile_of(states, t), pz[k][:, 0:BATCH], ACT.Tanh).then_inc(state_ready, 1)
            act.wait_ge(state_ready, LEAD + P)



LINKS4 = 50


def phase_project(nc, c, d, scr, keep, xT_all, states):
    with Phase(nc) as ctx:
        def sb(name, shape, dt=F32):
            return ctx.enter_context(nc.sbuf_tensor(f"p_{name}", shape, dt))

        def sem(name, lead=0):
            return ctx.sem("p_" + name, lead)

        out_bank, sub_bank, x6_bank, logits_bank, counts_bank = (
            ctx.enter_context(nc.psum_tensor(f"p_bank_{name}", [P, 512], F32)) for name in ("out", "sub", "x6", "logits", "counts"))
        route_banks = {LOGITS: logits_bank, COUNTS: counts_bank}
        nrm = norm_buffers(nc, ctx, "p", c)
        r = route_buffers(nc, ctx, "p", 1)
        wo, bo = sb("wo", [P, P]), sb("bo", [P, 1])
        subT, x6T = sb("subT", [P, SLOTS, P]), sb("x6T", [P, SLOTS, P])
        x6 = [[sb(f"x6_{parity}{s}", [P, P]) for s in range(SLOTS)] for parity in ("even", "odd")]
        w_loaded, x6_saved = sem("w_loaded"), [[sem(f"x6_saved{h}_{s}", LEAD) for s in range(SLOTS)] for h in range(2)]
        out_done, subT_ready, sub_done, x6_ready, x6_transposed, x6T_ready = (
            sem(n) for n in ("out_done", "subT_ready", "sub_done", "x6_ready", "x6_transposed", "x6T_ready"))
        dve_step, first_step, taken_set = sem("dve_step"), sem("first_step"), sem("taken_set")
        pairs = TURNS // 2 - 1
        block = ctx.enter_context(nc.Block())

        def slot(bank, s):
            return bank[:, s * P:(s + 1) * P]

        @block.sync
        def _(sp):
            give_leads(sp, ctx)
            sp.dma_start(wo[:], d["n_wo"]).then_inc(w_loaded, 16)
            sp.dma_start(bo[:], d["n_bo"].rearrange("(p o) -> p o", o=1)).then_inc(w_loaded, 16)
            with sp.Fori(0, TURNS // 2) as i:
                for h in range(2):
                    for s in range(SLOTS):
                        sp.wait_ge(x6_ready, i * (2 * SLOTS) + (h * SLOTS + s + 1))
                        sp.dma_start(dram_tile(scr["x6"], i * (2 * SLOTS) + (h * SLOTS + s)), x6[h][s][:])\
                            .then_inc(x6_saved[h][s], 16)
            for h in range(2):
                for s in range(SLOTS):
                    sp.wait_ge(x6_saved[h][s], LEAD + 16 * (TURNS // 2))

        @block.tensor
        def _(pe):
            def outputs(i):
                if not (isinstance(i, int) and i == 0):
                    pe.wait_ge(subT_ready, i)
                for s in range(SLOTS):
                    last = nc.tensor.matmul(slot(out_bank, s), lhsT=wo[:],
                                            rhs=states[:, :, bass.ds(i * SLOTS + s, 1)].rearrange("p t o -> p (t o)"),
                                            start=True, stop=True)
                last.then_inc(out_done, 1)

            def sums_turned(i):
                pe.wait_ge(subT_ready, i + 1)
                for s in range(SLOTS):
                    last = nc.tensor.transpose(slot(sub_bank, s), subT[:, s, :], c["ident"][:])
                last.then_inc(sub_done, 1)

            def turn(i, h, last_turn):
                if not last_turn:
                    outputs(i + 1)
                pe.wait_ge(x6_ready, i * SLOTS + SLOTS)
                for s in range(SLOTS):
                    last = nc.tensor.transpose(slot(x6_bank, s), x6[h][s][:], c["ident"][:])
                last.then_inc(x6_transposed, 1)
                if not last_turn:
                    sums_turned(i + 1)
                pe.wait_ge(x6T_ready, i + 1)
                pe_logits(nc, pe, r, route_banks, [x6T[:, s, :] for s in range(SLOTS)], c["gate1"])
                pe_count(nc, pe, r, c, route_banks, i)

            pe.wait_ge(w_loaded, 32)
            outputs(0)
            sums_turned(0)
            with pe.Fori(0, pairs) as pair:
                for h in range(2):
                    turn(pair * 2 + h, h, False)
            turn(TURNS - 2, 0, False)
            turn(TURNS - 1, 1, True)

        @block.scalar
        def _(act):
            def turn(i):
                act.wait_ge(x6_transposed, i + 1)
                nc.scalar.activation(x6T[:].rearrange("p s t -> p (s t)"), x6_bank[:], ACT.Copy).then_inc(x6T_ready, 1)
                act_route(nc, act, r, i)

            turn(0)
            with act.Fori(0, TURNS - 1) as i:
                turn(i + 1)

        @block.gpsimd
        def _(pool):
            def scatter(i, h):
                pool_scatter(nc, pool, r, c, i, x6[h], scr["sorted1"])

            pool_norm(nc, pool, nrm, c, 0)
            pool_norm(nc, pool, nrm, c, 1)
            scatter(0, 0)
            with pool.Fori(0, pairs) as pair:
                for h in (1, 0):
                    i = pair * 2 + (2 - h)
                    pool_norm(nc, pool, nrm, c, i + 1)
                    pool_scattered(pool, r, i - 1)
                    scatter(i, h)
            pool_scattered(pool, r, TURNS - 2)
            scatter(TURNS - 1, 1)
            pool_scattered(pool, r, TURNS - 1)

        @block.vector
        def _(dve):
            sub_all = [slot(sub_bank, s) for s in range(SLOTS)]

            def sums(i, chain):
                dve.wait_ge(out_done, i + 1)
                nc.vector.scalar_tensor_tensor(out=subT[:], in0=out_bank[:].rearrange("p (s t) -> p s t", t=P), scalar=bo[:],
                                               in1=xT_all[:, bass.ds(i * SLOTS, SLOTS), :], op0=ALU.add, op1=ALU.add)\
                    .then_inc(subT_ready, 1)
                return dve_norm_begin(nc, dve, nrm, chain, sub_all, [(sub_done, i + 1)] * SLOTS)

            def turn(pair, h, chain, last_turn):
                i = pair * 2 + h

                def x6_free(s):
                    dve.wait_ge(x6_saved[h][s], LEAD + pair * 16)
                    dve.wait_ge(r["rows_free"], i * SLOTS + (LEAD - SLOTS))
                dve_norm_end(nc, dve, nrm, chain, i, sub_all, [None] * SLOTS, [t[:] for t in x6[h]],
                             free=x6_free, done=(x6_ready, i, 0))
                if not last_turn:
                    sums(i + 1, chain)
                dve_route(nc, dve, r, c, chain, i, route_banks, c["gate1_b"], keep["route1"])

            dve.wait_ge(w_loaded, 32)
            nc.vector.tensor_copy(keep["route1"]["taken"][:], c["row_base"][:]).then_inc(taken_set, 1)
            dve.wait_ge(taken_set, 1)
            sums(0, Chain(dve, first_step, 0, 0))
            with dve.Fori(0, pairs) as pair:
                chain = Chain(dve, dve_step, pair, LINKS4)
                for h in range(2):
                    turn(pair, h, chain, False)
                chain.close()
            chain = Chain(dve, dve_step, pairs, LINKS4)
            turn(pairs, 0, chain, False)
            turn(pairs, 1, chain, True)



LINKS6 = 16


def phase_finish(nc, c, keep, scr, out):
    with Phase(nc) as ctx:
        def sb(name, shape, dt=F32):
            return [ctx.enter_context(nc.sbuf_tensor(f"f_{name}{s}", shape, dt)) for s in range(SLOTS)]

        def sem(name, lead=0):
            return ctx.sem("f_" + name, lead)

        nrm = norm_buffers(nc, ctx, "f", c)
        g = gather_buffers(nc, ctx, "f", 1, sets=2)
        x6, sub, x7 = ([sb(name + "_even_", [P, P]), sb(name + "_odd_", [P, P])] for name in ("x6", "sub", "x7"))
        x6_loaded = [[sem(f"x6_loaded{h}_{s}") for s in range(SLOTS)] for h in range(2)]
        x7_saved = [[sem(f"x7_saved{h}_{s}", LEAD) for s in range(SLOTS)] for h in range(2)]
        joined, x7_ready, dve_step = sem("joined"), sem("x7_ready", LEAD), sem("dve_step")
        block = ctx.enter_context(nc.Block())

        @block.sync
        def _(sp):
            give_leads(sp, ctx)

            def load(i, h):
                for s in range(SLOTS):
                    sp.dma_start(x6[h][s][:], dram_tile(scr["x6"], i * SLOTS + s)).then_inc(x6_loaded[h][s], 16)

            load(0, 0)
            load(1, 1)
            with sp.Fori(0, TURNS // 2 - 1) as pair:
                for h in range(2):
                    sp.wait_ge(joined, pair * (2 * SLOTS) + (h + 1) * SLOTS)
                    load(pair * 2 + (h + 2), h)

        @block.scalar
        def _(act):
            with act.Fori(0, TURNS // 2) as pair:
                for h in range(2):
                    for s in range(SLOTS):
                        n = pair * (2 * SLOTS) + (h * SLOTS + s)
                        act.wait_ge(x7_ready, LEAD + n + 1)
                        act.dma_start(dram_tile(out, n), x7[h][s][:]).then_inc(x7_saved[h][s], 16)
            for h in range(2):
                for s in range(SLOTS):
                    act.wait_ge(x7_saved[h][s], LEAD + 16 * (TURNS // 2))

        @block.gpsimd
        def _(pool):
            def gather(i, h):
                pool_gather(nc, pool, g, c, keep["route1"], i, scr["expert_out1"], h)

            gather(0, 0)
            gather(1, 1)
            with pool.Fori(0, TURNS // 2 - 1) as pair:
                for h in range(2):
                    i = pair * 2 + h
                    pool_norm(nc, pool, nrm, c, i)
                    pool.wait_ge(joined, i * SLOTS + SLOTS)
                    stand_alone(pool, c)
                    gather(i + 2, h)
            pool_norm(nc, pool, nrm, c, TURNS - 2)
            pool_norm(nc, pool, nrm, c, TURNS - 1)

        @block.vector
        def _(dve):
            with dve.Fori(0, TURNS // 2) as pair:
                chain = Chain(dve, dve_step, pair, LINKS6)
                for h in range(2):
                    i = pair * 2 + h
                    for s in range(SLOTS):
                        dve.wait_ge(x6_loaded[h][s], pair * 16 + 16)
                        dve.wait_ge(x7_ready, LEAD + i * SLOTS)
                        dve.wait_ge(g["gathered"][h][s], pair * 16 + 16)
                        nc.vector.scalar_tensor_tensor(out=sub[h][s][:], in0=g["y"][h][0][s][:],
                                                       scalar=g["weights"][h][:, s, 0:1], in1=x6[h][s][:],
                                                       op0=ALU.mult, op1=ALU.add).then_inc(joined, 1)
                    dve_norm(nc, dve, nrm, chain, i, [t[:] for t in sub[h]],
                             [(joined, i * SLOTS + (s + 1)) for s in range(SLOTS)], [t[:] for t in x7[h]],
                             free=lambda s: dve.wait_ge(x7_saved[h][s], LEAD + pair * 16), done=(x7_ready, i, LEAD))
                chain.close()


def lay_out(inputs):
    f = {k: np.asarray(v) for k, v in inputs.items()}
    con = np.ascontiguousarray
    qkv = f["L1_attn_w_qkv"]
    swap = np.arange(P).reshape(HEADS, 2, DH // 2)[:, ::-1].reshape(P)
    heads = np.array([G * g + j for j in range(G) for g in range(G)])
    t = np.arange(P)
    inv = (np.float32(1.0) / np.float32(10000.0) ** (np.arange(0, DH, 2, dtype=np.float32) / np.float32(DH))).astype(np.float32)
    angle = (t.astype(np.float32)[None, :] * np.tile(np.concatenate([inv, inv]), HEADS)[:, None]).astype(np.float32)
    sign = np.where(np.arange(P) % DH < DH // 2, -1.0, 1.0)[:, None]
    feature = np.arange(P)
    out = dict(
        x=f["x"], ctx=f["ctx_1024"],
        ident=np.eye(P, dtype=np.float32),
        mask_q=np.float32(SCALE) * ((feature % 32 // DH)[:, None] == np.arange(G)[None, :]).astype(np.float32),
        mask_k=((feature // 32)[:, None] == np.arange(G)[None, :]).astype(np.float32),
        iota8=np.arange(EXPERTS, dtype=np.float32),
        window=np.where(np.abs(t[:, None] - t[None, :]) <= WINDOW, 0.0, MASKED).astype(np.float32),
        causal=np.where(t[None, :] <= t[:, None], 0.0, MASKED).astype(np.float32),
        head_mask=np.where(t[None, :] < heads[:, None], MASKED, 0.0).astype(np.float32),
        cos=np.cos(angle).astype(np.float32), sin=(np.sin(angle) * sign).astype(np.float32),
        tri=(t[:, None] < t[None, :]).astype(np.float32),
        dist=np.abs(t[:, None] - t[None, :]).astype(np.float32),
        row_base=(REGION * np.arange(EXPERTS)).astype(np.float32),
        iota_tiles=np.arange(TILES0, dtype=np.float32),
        part_iota=t.astype(np.float32)[:, None].copy(),
        ds=f["L0_attn_dist_scale"].reshape(1),
        a_wq=f["L0_attn_Wq"], a_wk=f["L0_attn_Wk"], a_wv=f["L0_attn_Wv"], a_wo=f["L0_attn_Wo"],
        a_bq=f["L0_attn_bq"], a_bk=f["L0_attn_bk"], a_bv=f["L0_attn_bv"], a_bo=f["L0_attn_bo"],
        a_w1=f["L0_attn_W1"], a_b1=f["L0_attn_b1"].reshape(FF1 // P, P).T, a_w2=f["L0_attn_W2"], a_b2=f["L0_attn_b2"],
        ln1_g=f["L0_attn_ln1_g"], ln1_b=f["L0_attn_ln1_b"], ln2_g=f["L0_attn_ln2_g"], ln2_b=f["L0_attn_ln2_b"],
        x_wq=con(f["L0_xattn_Wq"].T), x_wk=con(f["L0_xattn_Wk"].T), x_wv=con(f["L0_xattn_Wv"].T),
        x_wo=con(f["L0_xattn_Wo"].T), x_bq=f["L0_xattn_bq"], x_bk=f["L0_xattn_bk"], x_bv=f["L0_xattn_bv"],
        x_bo=f["L0_xattn_bo"], gate0=con(f["L0_ffn_Wg"].T),
        m_wgv=con(np.concatenate([f["L0_ffn_W1"], f["L0_ffn_W2"]], axis=1).transpose(2, 0, 1)),
        m_bgv=con(np.concatenate([f["L0_ffn_b1"], f["L0_ffn_b2"]], axis=1)),
        m_wd=f["L0_ffn_W3"].transpose(2, 0, 1).reshape(FF0 // P, P, EXPERTS, P).transpose(1, 2, 0, 3), m_bd=f["L0_ffn_b3"],
        l_wq=con(qkv[:, 0:P]), l_wk=con(qkv[:, P:2 * P]), l_wv=con(qkv[:, 2 * P:]),
        l_wqp=con(qkv[:, 0:P][:, swap]), l_wkp=con(qkv[:, P:2 * P][:, swap]),
        l_wo=f["L1_attn_w_proj"], l_bo=f["L1_attn_b_proj"],
        n_wi=con(f["L1_xattn_Wi"].T), n_wg=con(f["L1_xattn_Wg"].T), n_a=con(f["L1_xattn_A"].T),
        n_b=con(f["L1_xattn_Bm"].T), n_wo=con(f["L1_xattn_Wo"].T),
        n_bi=f["L1_xattn_bi"], n_bg=f["L1_xattn_bg"], n_bo=f["L1_xattn_bo"],
        n_decay=con(np.repeat(f["L1_xattn_decay"].reshape(HEADS), DH)),
        gate1=f["L1_ffn_switch_w"], gate1_b=f["L1_ffn_switch_b"],
        s_w1=con(f["L1_ffn_w1"].transpose(1, 0, 2)), s_b1=f["L1_ffn_b1"],
        s_w2=f["L1_ffn_w2"].reshape(EXPERTS, FF1 // P, P, P).transpose(2, 0, 1, 3), s_b2=f["L1_ffn_b2"],
    )
    column = {"a_b1": out["a_b1"], **{k: out[k].reshape(-1, 1) for k in ("a_bq", "a_bk", "x_bq", "x_bk")}}
    out["a_w2"] = out["a_w2"].reshape(FF1 // P, P, P).transpose(1, 0, 2).reshape(P, FF1)
    out["tri_f"], out["ds_col"] = out["tri"], out["ds"]
    matrices = np.concatenate([column.get(k, out[k]) for k, _ in MATRICES], axis=1)
    rows = np.concatenate([out[k] for k, _ in ROWS])
    for k in [k for k, _ in MATRICES + ROWS] + ["tri", "ds"]:
        del out[k]
    out.update(matrices=matrices, rows=rows)
    return {k: con(v) for k, v in out.items()}


def keep_buffers(nc, ctx):
    def sb(name, shape, dt=F32):
        return ctx.enter_context(nc.sbuf_tensor("keep_" + name, shape, dt))
    def routing(tag, picks, tiles):
        return dict(picks=picks, tiles=tiles, weights=sb("weights" + tag, [P, BATCH + SLOTS, picks]),
                     rows=sb("rows" + tag, [P, BATCH + SLOTS, picks]), taken=sb("taken" + tag, [P, EXPERTS]),
                     out_rows=sb("out_rows" + tag, [P, BATCH + SLOTS, picks], U32),
                     tile_expert=sb("tile_expert" + tag, [P, tiles], I32),
                     tile_row=sb("tile_row" + tag, [P, tiles], I32))

    return dict(route0=routing("0", 2, TILES0), route1=routing("1", 1, TILES1),
                 experts_loaded=nc.alloc_semaphore("experts_loaded"))



def program(nc, d, out):
    with ExitStack() as ctx:
        keep, scr = keep_buffers(nc, ctx), scratch(nc)
        c = load_constants(nc, ctx, d)
        with ExitStack() as first:
            experts0 = expert_buffers(nc, first, "0", FF0 // P)
            phase_encode(nc, c, d, scr, keep, experts0)
            phase_table(nc, c, keep["route0"], "t0", scr["sorted0"])
            phase_experts(nc, c, keep, keep["route0"], experts0, "m0", True, scr["sorted0"], scr["expert_out0"], 16 * 4)
        experts1 = expert_buffers(nc, ctx, "1", FF1 // P)
        with ExitStack() as second:
            xT_all = second.enter_context(nc.sbuf_tensor("xT_all", [P, BATCH, P], F32))
            phase_decode(nc, c, d, keep, scr, xT_all, experts1)
            states = second.enter_context(nc.sbuf_tensor("states", [P, P, BATCH], F32))
            phase_recurrent(nc, c, d, scr, xT_all, states)
            phase_project(nc, c, d, scr, keep, xT_all, states)
        phase_table(nc, c, keep["route1"], "t1", scr["sorted1"])
        phase_experts(nc, c, keep, keep["route1"], experts1, "m1", False, scr["sorted1"], scr["expert_out1"], 16 * 8)
        phase_finish(nc, c, keep, scr, out)


def scratch(nc):
    def dram(name, shape):
        return nc.dram_tensor("scratch_" + name, shape, F32, kind="Internal").ap()
    return dict(ctxT=dram("ctxT", (BATCH, P, P)), x3=dram("x3", (BATCH, P, P)),
                x6=dram("x6", (BATCH, P, P)),
                sorted0=dram("sorted0", (EXPERTS * REGION, P)), sorted1=dram("sorted1", (EXPERTS * REGION, P)),
                expert_out0=dram("expert_out0", (TILES0 * P, P)), expert_out1=dram("expert_out1", (TILES1 * P, P)))




def kernel(**inputs):
    from concourse import bacc
    from concourse.bass_utils import run_bass_kernel_spmd

    nc = bacc.Bacc("TRN2", target_bir_lowering=False, num_devices=1)
    arrays = lay_out(inputs)
    dram = {name: nc.dram_tensor("in_" + name, a.shape, mybir.dt.from_np(a.dtype), kind="ExternalInput").ap()
            for name, a in arrays.items()}
    out = nc.dram_tensor("out_x", (BATCH, P, P), F32, kind="ExternalOutput").ap()
    program(nc, dram, out)
    result = run_bass_kernel_spmd(nc, [{"in_" + name: a for name, a in arrays.items()}], core_ids=[0])
    return result.results[0]["out_x"]
```
